# Optimizing a Trainium2 kernel written in Bass

```python
import numpy as np
import jax
import jax.numpy as jnp

def _softmax(x, axis=-1):
    return jax.nn.softmax(x, axis=axis)

def _gelu(x):
    return jax.nn.gelu(x, approximate=True)

def _silu(x):
    return jax.nn.silu(x)

def _sigmoid(x):
    return jax.nn.sigmoid(x)

def _layernorm(x, axis=-1, eps=1e-05):
    m = jnp.mean(x, axis=axis, keepdims=True)
    v = jnp.var(x, axis=axis, keepdims=True)
    return (x - m) / jnp.sqrt(v + eps)

def _scatter_add(tgt, idx, src, axis=0):
    return tgt.at[idx].add(src)

def _segment_sum(src, seg, n):
    return jax.ops.segment_sum(src, seg, n)
kernel_name = 'mk_perceiver_d1_seqx_r4_8ff76c'

def setup_inputs(seed: int=0):
    np.random.seed(seed)
    _w = jnp.asarray

    def _rec_inputs():
        import jax
        import jax.numpy as jnp
        _rk = jax.random.key(seed)
        x = 7.22e-05 + 1 * jax.random.normal(jax.random.fold_in(_rk, 1), (128, 32, 256), jnp.float32)
        _lenS = 32 - jax.random.randint(jax.random.fold_in(_rk, 7), (128,), 0, max(1, 32 // 4) + 1, jnp.int32)
        _lenS2 = 257 - jax.random.randint(jax.random.fold_in(_rk, 8), (128,), 0, max(1, 257 // 4) + 1, jnp.int32)
        _ctx_768P = jax.random.normal(jax.random.fold_in(_rk, 11), (128, 16, 192), jnp.float32)
        _ctx_768c = jax.random.dirichlet(jax.random.fold_in(_rk, 511), 0.3 * jnp.ones((16,), jnp.float32), (128, 257))
        _ctx_768t = jnp.einsum('bsk,bkd->bsd', _ctx_768c, _ctx_768P)
        _ctx_768t = _ctx_768t * jax.lax.rsqrt(jnp.mean(jnp.square(_ctx_768t)) + 1e-12) * 0.953939
        ctx_768 = -0.000191848 + 0.999787 * (_ctx_768t + 0.3 * jax.random.normal(jax.random.fold_in(_rk, 611), (128, 257, 192), jnp.float32))
        return (x, ctx_768)
    x, ctx_768 = _rec_inputs()

    def _L0_xattn_setup():
        import jax, jax.numpy as jnp
        import numpy as np
        N_HEADS = 16
        key = jax.random.key(seed)
        ks = jax.random.split(key, 8)
        b, l, m = (8, 256, 256)
        d_embed, d_cross = (256, 192)
        s_q = 1.0 / np.sqrt(d_embed)
        s_kv = 1.0 / np.sqrt(d_cross)
        return {'x': jax.random.normal(ks[0], (b, l, d_embed), jnp.float32), 'y': jax.random.normal(ks[1], (b, m, d_cross), jnp.float32), 'Wq': jax.random.normal(ks[2], (d_embed, d_embed), jnp.float32) * s_q, 'bq': jax.random.normal(ks[3], (d_embed,), jnp.float32) * 0.01, 'Wkv': jax.random.normal(ks[4], (2 * d_embed, d_cross), jnp.float32) * s_kv, 'bkv': jax.random.normal(ks[5], (2 * d_embed,), jnp.float32) * 0.01, 'Wo': jax.random.normal(ks[6], (d_embed, d_embed), jnp.float32) * s_q, 'bo': jax.random.normal(ks[7], (d_embed,), jnp.float32) * 0.01}
    _L0_xattn_all = _L0_xattn_setup()
    _L0_xattn_in = {k: v for k, v in _L0_xattn_all.items() if k in ('Wq', 'bq', 'Wkv', 'bkv', 'Wo', 'bo')}
    del _L0_xattn_all

    def _L0_attn_setup():
        import jax, jax.numpy as jnp
        import numpy as np
        import math

        def surrogate_spike(m):
            return jnp.clip(jnp.round(m), -1.0, 1.0)

        def rmsnorm(x, gamma):
            n = jnp.linalg.norm(x, axis=-1, keepdims=True)
            return x / jnp.maximum(n, 1e-12) * x.shape[-1] ** 0.5 * (gamma + 1.0)
        DIM = 256
        HEADS = 8
        HEAD_DIM = DIM // HEADS
        INNER = int(HEAD_DIM * 1.5)
        FF_INNER = int(DIM * 4 * 2 / 3)
        B, L = (8, 512)
        BETA0 = 0.9
        key = jax.random.key(seed)
        ks = jax.random.split(key, 10)
        s = 0.02
        beta_raw0 = math.log(BETA0 / (1.0 - BETA0))
        return {'x': jax.random.normal(ks[0], (B, L, DIM), dtype=jnp.float32), 'in_gamma': jnp.zeros((DIM,), jnp.float32), 'gate_W': jax.random.normal(ks[1], (HEADS, INNER, HEAD_DIM), jnp.float32) * s, 'cand_W': jax.random.normal(ks[2], (HEADS, INNER, HEAD_DIM), jnp.float32) * s, 'out_W': jax.random.normal(ks[3], (HEADS, HEAD_DIM, INNER), jnp.float32) * s, 'gate_beta_raw': jnp.full((HEADS, INNER), beta_raw0, jnp.float32), 'gate_theta': jnp.ones((HEADS, INNER), jnp.float32), 'cand_beta_raw': jnp.full((HEADS, INNER), beta_raw0, jnp.float32), 'cand_theta': jnp.ones((HEADS, INNER), jnp.float32), 'ff_gamma': jnp.zeros((DIM,), jnp.float32), 'ffg_W': jax.random.normal(ks[4], (FF_INNER, DIM), jnp.float32) * s, 'ffu_W': jax.random.normal(ks[5], (FF_INNER, DIM), jnp.float32) * s, 'ffd_W': jax.random.normal(ks[6], (DIM, FF_INNER), jnp.float32) * s}
    _L0_attn_all = _L0_attn_setup()
    _L0_attn_in = {k: v for k, v in _L0_attn_all.items() if k in ('in_gamma', 'gate_W', 'cand_W', 'out_W', 'gate_beta_raw', 'gate_theta', 'cand_beta_raw', 'cand_theta', 'ff_gamma', 'ffg_W', 'ffu_W', 'ffd_W')}
    del _L0_attn_all

    def _L0_ffn_setup():
        import jax, jax.numpy as jnp
        import numpy as np
        B, S, DIM, FFN, E = (4, 512, 256, 1024, 8)
        key = jax.random.key(seed)
        k0, k1, k2, k3 = jax.random.split(key, 4)
        scale = 0.02
        return {'hidden_states': jax.random.normal(k0, (B, S, DIM), jnp.float32), 'router_w': jax.random.normal(k1, (DIM, E), jnp.float32) * scale, 'router_b': jnp.zeros((E,), jnp.float32), 'w1': jax.random.normal(k2, (E, DIM, 2 * FFN), jnp.float32) * scale, 'w2': jax.random.normal(k3, (E, FFN, DIM), jnp.float32) * scale}
    _L0_ffn_all = _L0_ffn_setup()
    _L0_ffn_in = {k: v for k, v in _L0_ffn_all.items() if k in ('router_w', 'router_b', 'w1', 'w2')}
    del _L0_ffn_all
    return {'x': x, 'ctx_768': ctx_768, 'L0_xattn_Wq': _L0_xattn_in['Wq'], 'L0_xattn_bq': _L0_xattn_in['bq'], 'L0_xattn_Wkv': _L0_xattn_in['Wkv'], 'L0_xattn_bkv': _L0_xattn_in['bkv'], 'L0_xattn_Wo': _L0_xattn_in['Wo'], 'L0_xattn_bo': _L0_xattn_in['bo'], 'L0_attn_in_gamma': _L0_attn_in['in_gamma'], 'L0_attn_gate_W': _L0_attn_in['gate_W'], 'L0_attn_cand_W': _L0_attn_in['cand_W'], 'L0_attn_out_W': _L0_attn_in['out_W'], 'L0_attn_gate_beta_raw': _L0_attn_in['gate_beta_raw'], 'L0_attn_gate_theta': _L0_attn_in['gate_theta'], 'L0_attn_cand_beta_raw': _L0_attn_in['cand_beta_raw'], 'L0_attn_cand_theta': _L0_attn_in['cand_theta'], 'L0_attn_ff_gamma': _L0_attn_in['ff_gamma'], 'L0_attn_ffg_W': _L0_attn_in['ffg_W'], 'L0_attn_ffu_W': _L0_attn_in['ffu_W'], 'L0_attn_ffd_W': _L0_attn_in['ffd_W'], 'L0_ffn_router_w': _L0_ffn_in['router_w'], 'L0_ffn_router_b': _L0_ffn_in['router_b'], 'L0_ffn_w1': _L0_ffn_in['w1'], 'L0_ffn_w2': _L0_ffn_in['w2']}

def reference(x, ctx_768, L0_xattn_Wq, L0_xattn_bq, L0_xattn_Wkv, L0_xattn_bkv, L0_xattn_Wo, L0_xattn_bo, L0_attn_in_gamma, L0_attn_gate_W, L0_attn_cand_W, L0_attn_out_W, L0_attn_gate_beta_raw, L0_attn_gate_theta, L0_attn_cand_beta_raw, L0_attn_cand_theta, L0_attn_ff_gamma, L0_attn_ffg_W, L0_attn_ffu_W, L0_attn_ffd_W, L0_ffn_router_w, L0_ffn_router_b, L0_ffn_w1, L0_ffn_w2):
    import jax
    import jax.numpy as jnp

    def _L0_xattn_ref(x, y, Wq, bq, Wkv, bkv, Wo, bo):
        import jax, jax.numpy as jnp
        import numpy as np
        N_HEADS = 16
        b, l, d = x.shape
        m = y.shape[1]
        h = N_HEADS
        dh = d // h
        q = (jnp.einsum('bld,ed->ble', x, Wq) + bq).reshape(b, l, h, dh)
        kv = (jnp.einsum('bmc,ec->bme', y, Wkv) + bkv).reshape(b, m, h, 2 * dh)
        k, v = (kv[..., :dh], kv[..., dh:])
        scale = 1.0 / jnp.sqrt(jnp.asarray(dh, x.dtype))
        att = jax.nn.softmax(jnp.einsum('blhd,bmhd->blmh', q, k) * scale, axis=2)
        out = jnp.einsum('blmh,bmhd->blhd', att, v).reshape(b, l, d)
        return jnp.einsum('bld,ed->ble', out, Wo) + bo

    def _L0_attn_ref(x, in_gamma, gate_W, cand_W, out_W, gate_beta_raw, gate_theta, cand_beta_raw, cand_theta, ff_gamma, ffg_W, ffu_W, ffd_W):
        import jax, jax.numpy as jnp
        import numpy as np
        import math

        def surrogate_spike(m):
            return jnp.clip(jnp.round(m), -1.0, 1.0)

        def rmsnorm(x, gamma):
            n = jnp.linalg.norm(x, axis=-1, keepdims=True)
            return x / jnp.maximum(n, 1e-12) * x.shape[-1] ** 0.5 * (gamma + 1.0)
        DIM = 256
        HEADS = 8
        HEAD_DIM = DIM // HEADS
        INNER = int(HEAD_DIM * 1.5)
        FF_INNER = int(DIM * 4 * 2 / 3)
        B, L = (8, 512)
        BETA0 = 0.9
        Bv, Lv, Dv = x.shape
        res_scale = 1.0 / math.sqrt(1.0)
        xn = rmsnorm(x, in_gamma)
        xh = xn.reshape(Bv, Lv, HEADS, HEAD_DIM)
        xh = jnp.transpose(xh, (1, 0, 2, 3))
        beta_g = jax.nn.sigmoid(gate_beta_raw)
        beta_c = jax.nn.sigmoid(cand_beta_raw)
        h0 = jnp.zeros((Bv, HEADS, INNER), x.dtype)
        gm0 = jnp.zeros_like(h0)
        cm0 = jnp.zeros_like(h0)

        def step(carry, xt):
            h, gm, cm = carry
            gc = jnp.einsum('bhd,hid->bhi', xt, gate_W)
            gm = beta_g * gm + gc
            gs = surrogate_spike(gm)
            gm = gm - gs * gate_theta
            z = (gs + 1.0) * 0.5
            cc = jnp.einsum('bhd,hid->bhi', xt, cand_W)
            cm = beta_c * cm + cc
            cs = surrogate_spike(cm)
            cm = cm - cs * cand_theta
            h = (1.0 - z) * h + z * cs
            out = jnp.einsum('bhi,hdi->bhd', h, out_W)
            return ((h, gm, cm), out)
        _, outs = jax.lax.scan(step, (h0, gm0, cm0), xh)
        gru_out = jnp.transpose(outs, (1, 0, 2, 3)).reshape(Bv, Lv, Dv)
        x = x + res_scale * gru_out
        fn = rmsnorm(x, ff_gamma)
        ff = jnp.einsum('blf,df->bld', jax.nn.silu(jnp.einsum('bld,fd->blf', fn, ffg_W)) * jnp.einsum('bld,fd->blf', fn, ffu_W), ffd_W)
        x = x + res_scale * ff
        return x

    def _L0_ffn_ref(hidden_states, router_w, router_b, w1, w2):
        import jax, jax.numpy as jnp
        import numpy as np
        B, S, DIM, FFN, E = (4, 512, 256, 1024, 8)
        b, s, d = hidden_states.shape
        x = hidden_states.reshape(-1, d)
        logits = x @ router_w + router_b
        route = jax.nn.softmax(logits, axis=1)
        max_prob = jnp.max(route, axis=1, keepdims=True)
        max_ind = jnp.argmax(route, axis=1)
        out = jnp.zeros_like(x)
        num_experts = w1.shape[0]
        for e in range(num_experts):
            h = x @ w1[e]
            a, g = jnp.split(h, 2, axis=1)
            y = jax.nn.silu(a) * g @ w2[e]
            out = jnp.where((max_ind == e)[:, None], y, out)
        out = out * max_prob
        return out.reshape(b, s, d)
    x = x + _L0_xattn_ref(_layernorm(x, axis=-1), ctx_768, L0_xattn_Wq, L0_xattn_bq, L0_xattn_Wkv, L0_xattn_bkv, L0_xattn_Wo, L0_xattn_bo)
    x = x + _L0_attn_ref(_layernorm(x, axis=-1), L0_attn_in_gamma, L0_attn_gate_W, L0_attn_cand_W, L0_attn_out_W, L0_attn_gate_beta_raw, L0_attn_gate_theta, L0_attn_cand_beta_raw, L0_attn_cand_theta, L0_attn_ff_gamma, L0_attn_ffg_W, L0_attn_ffu_W, L0_attn_ffd_W)
    x = x + _L0_ffn_ref(_layernorm(x, axis=-1), L0_ffn_router_w, L0_ffn_router_b, L0_ffn_w1, L0_ffn_w2)
    return x

_drawn_inputs = setup_inputs


def setup_inputs(seed=0):
    import zlib

    import numpy as np

    out = dict(_drawn_inputs(seed))
    spreads = {'L0_attn_in_gamma': (0.0, 0.8),
     'L0_attn_gate_beta_raw': (2.1972246170043945, 0.6),
     'L0_attn_gate_theta': (1.0, 0.6),
     'L0_attn_cand_beta_raw': (2.1972246170043945, 0.6),
     'L0_attn_cand_theta': (1.0, 0.6),
     'L0_attn_ff_gamma': (0.0, 0.8),
     'L0_ffn_router_b': (0.0, 0.8)}
    factors = {'L0_xattn_bq': 8.0,
     'L0_xattn_bkv': 6.431,
     'L0_xattn_bo': 5.936,
     'L0_attn_gate_W': 8.0,
     'L0_attn_cand_W': 6.726,
     'L0_attn_out_W': 6.663,
     'L0_attn_ffg_W': 4.426,
     'L0_attn_ffu_W': 4.383,
     'L0_attn_ffd_W': 4.376,
     'L0_ffn_router_w': 8.0,
     'L0_ffn_w1': 8.0,
     'L0_ffn_w2': 8.0}
    for name, (base, spread) in spreads.items():
        noise = np.random.default_rng([zlib.crc32(name.encode()), seed]).standard_normal(out[name].shape)
        drawn = base * np.exp(spread * noise) if base else spread * noise
        out[name] = jnp.asarray(drawn.astype(out[name].dtype))
    for name, factor in factors.items():
        out[name] = (out[name] * factor).astype(out[name].dtype)
    return out
```

```python
from contextlib import ExitStack

import numpy as np

import concourse.bass as bass
from concourse import mybir

F32 = mybir.dt.float32
I32 = mybir.dt.int32
U32 = mybir.dt.uint32
ALU = mybir.AluOpType
ACT = mybir.ActivationFunctionType
AXX = mybir.AxisListType.X

P = 128
B, L, D = 128, 32, 256
M, C = 257, 192
CK = C // 2
KEYS = M - 1
NH, DH = 16, 16
GB = P // L
NG = B // GB
EPS = 1e-5
NE = 8
FI = D * 4 * 2 // 3
FF = 1024
FT = FF // P
WE = 2 * 2 * FF + FT * D
NS = B * L // P + NE - 1
NF = (FI + P - 1) // P
HB, HI = 32, 48
RMS_MIN = 1e-12
ROUND = 1.5 * 2 ** 23


def at_least(eng, sem, value):
    if isinstance(value, int) and value <= 0:
        return
    eng.wait_ge(sem, value)


def spread(ap, axis, n):
    v = ap.unsqueeze(axis)
    shape = list(v.shape)
    shape[axis] = n
    return v.to_broadcast(shape)


class Plan:

    def __init__(self, nc, base, end):
        self.nc, self.at, self.end = nc, base, end

    def tensor(self, name, shape, dtype=F32):
        size = int(np.prod(shape[1:])) * 4
        self.at = (self.at + 31) // 32 * 32
        t = self.nc.alloc_sbuf_tensor_at(name, list(shape), dtype, offset=self.at)
        self.at += size
        assert self.at <= self.end, (name, self.at, self.end)
        return t


def build(nc, T, out):
    ctx = ExitStack()
    with ctx:
        def sem(name):
            return ctx.enter_context(nc.semaphore(name))

        x1_scr = nc.dram_tensor("x1_scr", (B * L, D), F32, kind="Internal").ap()
        vlast_scr = nc.dram_tensor("vlast_scr", (B, D), F32, kind="Internal").ap()

        base, end = nc.sbuf_base, nc.sbuf_usable_end
        keep = Plan(nc, base, end)
        ident = keep.tensor("ident", [P, P])
        halfneg = keep.tensor("halfneg", [P, 1])

        att = Plan(nc, keep.at, end)
        wk = att.tensor("wk", [CK, 2, D])
        wv = att.tensor("wv", [CK, 2, D])
        wvl = att.tensor("wvl", [CK, 2, D])
        wq = att.tensor("wq", [P, 2, D])
        wo = att.tensor("wo", [64, 4, D])
        bk = att.tensor("bk", [P, 2])
        bq = att.tensor("bq", [P, 2])
        bv = att.tensor("bv", [P, D])
        bvl = att.tensor("bvl", [P, D])
        bo = att.tensor("bo", [P, D])
        headmask = att.tensor("headmask", [P, 4])
        cxl = att.tensor("cxl", [CK, 2, B])
        vlast = att.tensor("vlast", [P, D])
        cx = [att.tensor(f"cx{i}", [CK, GB, 2, M]) for i in range(2)]
        vb = [att.tensor(f"vb{i}", [P, GB, 64]) for i in range(2)]
        x_in = [att.tensor(f"x_in{i}", [P, D]) for i in range(2)]
        x_res = [att.tensor(f"x_res{i}", [P, D]) for i in range(2)]
        xsum = [att.tensor(f"xsum{i}", [P, D]) for i in range(2)]
        x1o = [att.tensor(f"x1o{i}", [P, D]) for i in range(2)]
        xn = [att.tensor(f"xn{i}", [P, D]) for i in range(2)]
        xnT = [att.tensor(f"xnT{i}", [P, 2, P]) for i in range(2)]
        qT = [att.tensor(f"qT{i}", [P, 2, P]) for i in range(2)]
        qbd = [att.tensor(f"qbd{i}", [P, 2, GB, P]) for i in range(2)]
        kT = [att.tensor(f"kT{i}", [P, 2, M]) for i in range(2)]
        v = [att.tensor(f"v{i}", [P, 2, D]) for i in range(2)]
        prob = [att.tensor(f"prob{i}", [P, 4, M]) for i in range(2)]
        probT = att.tensor("probT", [P, 2, 4 * P])
        negmax = [att.tensor(f"negmax{i}", [P, 4]) for i in range(2)]
        rowsum = [att.tensor(f"rowsum{i}", [P, 4]) for i in range(2)]
        rinv = [att.tensor(f"rinv{i}", [P, 4]) for i in range(2)]
        olast = [att.tensor(f"olast{i}", [P, 4, DH]) for i in range(2)]
        oraw = [att.tensor(f"oraw{i}", [P, 4, DH]) for i in range(2)]
        on = [att.tensor(f"on{i}", [P, GB, 64]) for i in range(2)]
        oT = [att.tensor(f"oT{i}", [64, 4, GB, L]) for i in range(2)]
        stats = [att.tensor(f"stats{i}", [P, 6]) for i in range(2)]
        mv = [att.tensor(f"mv{i}", [P, 2]) for i in range(2)]
        vare = [att.tensor(f"vare{i}", [P, 1]) for i in range(2)]
        rstd = [att.tensor(f"rstd{i}", [P, 1]) for i in range(2)]

        bank = [ctx.enter_context(nc.psum_tensor(f"bank{i}", [P, 512], F32)) for i in range(8)]
        kv_bank = bank[0:2]
        s_bank = bank[2:4]
        pT_bank = bank[4:6]
        o_bank = bank[6]
        x_bank = bank[7]

        d_const = sem("d_const")
        d_cx = [sem(f"d_cx{i}") for i in range(2)]
        d_vb = [sem(f"d_vb{i}") for i in range(2)]
        d_xin = [sem(f"d_xin{i}") for i in range(2)]
        d_xres = [sem(f"d_xres{i}") for i in range(2)]
        d_x1 = [sem(f"d_x1{i}") for i in range(2)]
        d_vlast = sem("d_vlast")
        vl_mm, kv_mm, s_mm, pT_mm, o_mm = (sem(n) for n in ("vl_mm", "kv_mm", "s_mm", "pT_mm", "o_mm"))
        xT_mm, q_mm, oT_mm, out_mm = (sem(n) for n in ("xT_mm", "q_mm", "oT_mm", "out_mm"))
        k_ev, p_ex, pT0_ev = (sem(n) for n in ("k_ev", "p_ex", "pT0_ev"))
        xT_ev, q_ev, oT_ev = (sem(n) for n in ("xT_ev", "q_ev", "oT_ev"))
        vl_ev, mx, v_ev, pT1_ev, o_ev, rinv_ok, xsum_ok = (
            sem(n) for n in ("vl_ev", "mx", "v_ev", "pT1_ev", "o_ev", "rinv_ok", "xsum_ok"))
        st_ok, mv_ok, xn_ok = (sem(n) for n in ("st_ok", "mv_ok", "xn_ok"))
        c_ok, qbd_ok, ol_ok, on_ok, x1o_ok, var_ok, rstd_ok = (
            sem(n) for n in ("c_ok", "qbd_ok", "ol_ok", "on_ok", "x1o_ok", "var_ok", "rstd_ok"))

        consts = [(ident, "ident"), (wk, "wk"), (wv, "wv"), (wvl, "wvl"), (wq, "wq"), (wo, "wo"),
                  (bk, "bk"), (bq, "bq"), (headmask, "headmask"), (cxl, "cxl")]
        rows = [(bv, "bv"), (bvl, "bvl"), (bo, "bo")]
        CONST = 16 * (len(consts) + len(rows))

        passed = {}

        def alone(eng, *waits):
            for s_, v in waits:
                at_least(eng, s_, v)
            if eng not in passed:
                passed[eng] = sem(f"passed{len(passed)}")
            eng.sem_inc(passed[eng], 1)

        def slots(eng, slot):
            slot(0, 0, True, False)
            with eng.Fori(0, NG // 2 - 1) as k:
                slot(k * 2 + 1, 1, False, False)
                slot(k * 2 + 2, 0, False, False)
            slot(NG - 1, (NG - 1) % 2, False, True)


        NT = L
        ff = Plan(nc, keep.at, end)
        xall = ff.tensor("xall", [P, NT, D])
        xm = ff.tensor("xm", [P, NT, D])
        logit = ff.tensor("logit", [P, NT, NE])
        moe_at = ff.at
        gw = [ff.tensor(f"gw{i}", [P, 4, P]) for i in range(2)]
        ow = ff.tensor("ow", [P, 3, D])
        braw = ff.tensor("braw", [P, 6])
        thr = ff.tensor("thr", [P, 6])
        beta = ff.tensor("beta", [P, 6])
        nthr = ff.tensor("nthr", [P, 6])
        ebase = ff.tensor("ebase", [P, 6])
        gam = [ff.tensor(f"gam{i}", [P, 2]) for i in range(2)]
        gam1 = [ff.tensor(f"gam1{i}", [P, 2]) for i in range(2)]
        fg = ff.tensor("fg", [P, 2, FI])
        fu = ff.tensor("fu", [P, 2, FI])
        fd = ff.tensor("fd", [P, NF, D])
        rw = ff.tensor("rw", [P, 2, NE])
        rb = ff.tensor("rb", [P, NE])
        xr = ff.tensor("xr", [P, 2, D])
        xrT = ff.tensor("xrT", [P, 2, 2, P])
        gc = [ff.tensor(f"gc{i}", [P, 6, P]) for i in range(2)]
        mem = ff.tensor("mem", [P, 6, P])
        pot = ff.tensor("pot", [P, 6, P])
        rnd = ff.tensor("rnd", [P, 6, P])
        spk = [ff.tensor(f"spk{i}", [P, 6, P]) for i in range(2)]
        zed = ff.tensor("zed", [P, 3, P])
        wed = ff.tensor("wed", [P, 3, P])
        zc = ff.tensor("zc", [P, 3, P])
        wh = ff.tensor("wh", [P, 3, P])
        hT = [ff.tensor(f"hT{i}", [P, 3, P]) for i in range(2)]
        xa = ff.tensor("xa", [P, 2, D])
        fn = ff.tensor("fn", [P, 2, D])
        fnT = [ff.tensor(f"fnT{i}", [P, 2, 2, P]) for i in range(2)]
        sg = [ff.tensor(f"sg{i}", [P, 2 * P]) for i in range(2)]
        fT = ff.tensor("fT", [P, NF, 2, P])
        xmt = ff.tensor("xmt", [P, 2, D])
        xmT = ff.tensor("xmT", [P, 2, 2, P])
        junk = {c: [ff.tensor(f"junk{c}{i}", [P, D]) for i in range(2)] for c in "AB"}
        st = {c: [ff.tensor(f"st{c}{i}", [P, 6]) for i in range(2)] for c in "AB"}
        mv2 = {c: ff.tensor(f"mv2{c}", [P, 2, 2]) for c in "AB"}
        small = {n: ff.tensor(n, [P, 2]) for n in
                 ("veA", "rsA", "veB", "rsB", "ssA", "smA", "spA", "scA", "ssB", "smB", "spB", "scB")}

        wbuf = ff.tensor("wbuf", [P, 2, WE])
        moe = Plan(nc, moe_at, end)
        lt = moe.tensor("lt", [P, P])
        ones = moe.tensor("ones", [P, P])
        descend = moe.tensor("descend", [P, NE])
        slotno = moe.tensor("slotno", [P, NS])
        altern = moe.tensor("altern", [P, NE])
        lmax, lsum, maxp, best, posf = (moe.tensor(n, [P, NT]) for n in ("lmax", "lsum", "maxp", "best", "posf"))
        lsh, lex, oneh, rank, tot, cum, exc = (moe.tensor(n, [P, NT * NE]) for n in (
            "lsh", "lex", "oneh", "rank", "tot", "cum", "exc"))
        cnt, tlf, tiles, ctile, base_e, shift = (moe.tensor(n, [P, NE]) for n in (
            "cnt", "tlf", "tiles", "ctile", "base_e", "shift"))
        pos = moe.tensor("pos", [P, NT], I32)
        cmp7, alt7 = (moe.tensor(n, [P, NS, NE - 1]) for n in ("cmp7", "alt7"))
        expf, parf = (moe.tensor(n, [P, NS]) for n in ("expf", "parf"))
        expi, pari = (moe.tensor(n, [P, NS], I32) for n in ("expi", "pari"))
        endi = moe.tensor("endi", [P, NE], I32)
        xs = [moe.tensor(f"xs{i}", [P, D]) for i in range(2)]
        xsT = [moe.tensor(f"xsT{i}", [P, 2, P]) for i in range(2)]
        sa = [moe.tensor(f"sa{i}", [P, 512]) for i in range(2)]
        hid = [moe.tensor(f"hid{i}", [P, 512]) for i in range(2)]
        hidT = [moe.tensor(f"hidT{i}", [P, 4, P]) for i in range(2)]
        ys = [moe.tensor(f"ys{i}", [P, D]) for i in range(2)]
        yg = [moe.tensor(f"yg{i}", [P, D]) for i in range(4)]
        assert moe.at <= end
        xs_scr = nc.dram_tensor("xs_scr", (NS * P, D), F32, kind="Internal").ap()
        ys_scr = nc.dram_tensor("ys_scr", (NS * P, D), F32, kind="Internal").ap()
        a_bank, g_bank = bank[0:2], bank[2:4]
        hT_bank = bank[4:6]
        xs_bank, y_bank = bank[6], bank[7]

        d_zero, d_mc, d_w = sem("d_zero"), sem("d_mc"), [sem(f"d_w{i}") for i in range(2)]
        z_ok, w_ready, d_sort = sem("z_ok"), sem("w_ready"), sem("d_sort")
        d_xs, d_ys = [sem(f"d_xs{i}") for i in range(2)], [sem(f"d_ys{i}") for i in range(2)]
        d_yg = [sem(f"d_yg{i}") for i in range(4)]
        route_ok, lsh_ok, lex_ok, oneh_ok, rank_mm, pos_ok, tab_ok = (sem(n) for n in (
            "route_ok", "lsh_ok", "lex_ok", "oneh_ok", "rank_mm", "pos_ok", "tab_ok"))
        xsT_mm, xsT_ev, ag_mm, sa_ok, hid_ok, hT_mm, hT0_ev, hT1_ev, y_mm, y_ok, fin_ok = (sem(n) for n in (
            "xsT_mm", "xsT_ev", "ag_mm", "sa_ok", "hid_ok", "hT_mm", "hT0_ev", "hT1_ev", "y_mm", "y_ok", "fin_ok"))
        d_out = sem("d_out")
        moec = [(lt, "lt")]
        moer = [(descend, "descend"), (slotno, "slotno"), (altern, "altern")]
        MOEC = 16 * (len(moec) + len(moer))

        def tiles_of_experts(eng, step):
            step(0, 0, True, False)
            with eng.Fori(0, (NS - 3) // 2) as k:
                step(k * 2 + 1, 1, False, False)
                step(k * 2 + 2, 0, False, False)
            step(NS - 2, (NS - 2) % 2, False, False)
            step(NS - 1, (NS - 1) % 2, False, True)

        gc_bank = bank[0:2]
        t_bank = bank[2]
        r_bank = bank[3]
        gu_bank = bank[4:7]
        fd_bank = bank[7]

        d_ff, d_x = sem("d_ff"), sem("d_x")
        c2, be_ok = sem("c2"), sem("be_ok")
        stA_ok, mvA_ok, veA_ok, rsA_ok, xl_ok, ssA_ok, smA_ok, spA_ok, scA_ok, xr_ok = (sem(n) for n in (
            "stA_ok", "mvA_ok", "veA_ok", "rsA_ok", "xl_ok", "ssA_ok", "smA_ok", "spA_ok", "scA_ok", "xr_ok"))
        xrT_mm, xrT_ev, gc_mm, gc_ev, pot_ok, rnd_ok, spk_ok, mem_ok = (sem(n) for n in (
            "xrT_mm", "xrT_ev", "gc_mm", "gc_ev", "pot_ok", "rnd_ok", "spk_ok", "mem_ok"))
        zw_ok, zc_ok, h_ok, gru_mm, xa_ok, add_ok = (sem(n) for n in (
            "zw_ok", "zc_ok", "h_ok", "gru_mm", "xa_ok", "add_ok"))
        ssB_ok, smB_ok, spB_ok, scB_ok, fn_ok, fnT_mm, fnT_ev = (sem(n) for n in (
            "ssB_ok", "smB_ok", "spB_ok", "scB_ok", "fn_ok", "fnT_mm", "fnT_ev"))
        gu_mm, silu_ok, prod_ok, fd_mm, x2_ok = (sem(n) for n in ("gu_mm", "silu_ok", "prod_ok", "fd_mm", "x2_ok"))
        stB_ok, mvB_ok, veB_ok, rsB_ok, xm_ok, xmT_mm, xmT_ev, rt_mm, rt_ok = (sem(n) for n in (
            "stB_ok", "mvB_ok", "veB_ok", "rsB_ok", "xm_ok", "xmT_mm", "xmT_ev", "rt_mm", "rt_ok"))
        dv_chain = sem("dv_chain")
        xm_kept = sem("xm_kept")

        ffw = [(gw[0], "gw"), (gw[1], "cw"), (ow, "ow"), (braw, "braw"), (thr, "thr"), (gam[0], "gamA"),
               (gam[1], "gamB"), (fg, "fg"), (fu, "fu"), (fd, "fd"), (rw, "rw")]
        FFW = 16 * (len(ffw) + 1)
        FW = [min(P, FI - P * f) for f in range(NF)]

        NQ = NT // 2

        def turns(eng, turn):
            turn(-3, 1, "m")
            turn(-2, 0, "nm")
            turn(-1, 1, "onm")
            turn(0, 0, "fonm")
            with eng.Fori(0, (NQ - 4) // 2) as k:
                turn(k * 2 + 1, 1, "fonmr")
                turn(k * 2 + 2, 0, "fonmr")
            turn(NQ - 3, 1, "fonr")
            turn(NQ - 2, 0, "for")
            turn(NQ - 1, 1, "fr")
            turn(NQ, 0, "r")

        block = ctx.enter_context(nc.Block())

        @block.sync
        def _(sp):
            def ln_row(g):
                return T["x"][bass.ds(g * P, P), :]

            def load_cx(g, s):
                sp.dma_start(cx[s][:, :, :, :], T["cx"][:, bass.ds(g * GB, GB), :, :]).then_inc(d_cx[s], 16)

            def load_vb(g, s):
                for j in range(4):
                    src = vlast_scr[bass.ds(g * GB, GB), 64 * j:64 * j + 64].partition_broadcast(L)
                    sp.dma_start(vb[s][32 * j:32 * j + 32, :, :], src).then_inc(d_vb[s], 16)

            for t, name in consts:
                full = tuple(slice(None) for _ in t.shape)
                sp.dma_start(t[full], T[name]).then_inc(d_const, 16)
            sp.wait_ge(z_ok, 1)
            sp.dma_start(xs_scr.rearrange("(s p) d -> p s d", p=P), spread(x1o[0][:, :], 1, NS)).then_inc(d_zero, 16)
            for t, name in rows:
                sp.dma_start(t[:, :], T[name].partition_broadcast(P)).then_inc(d_const, 16)
            for g in range(2):
                sp.dma_start(x_in[g][:, :], ln_row(g)).then_inc(d_xin[g], 16)
            load_cx(0, 0)
            sp.wait_ge(vl_ev, 1)
            sp.dma_start(vlast_scr, vlast[:, :]).then_inc(d_vlast, 16)
            sp.wait_ge(d_vlast, 16)
            load_vb(0, 0)

            def slot(g, s, first, last):
                if not last:
                    at_least(sp, kv_mm, 3 * GB * g)
                    load_cx(g + 1, 1 - s)
                    at_least(sp, ol_ok, GB * g)
                    load_vb(g + 1, 1 - s)
                if isinstance(g, int) and g + 2 >= NG:
                    pass
                elif not last:
                    sp.wait_ge(xn_ok, g + 1)
                    sp.dma_start(x_in[s][:, :], ln_row(g + 2)).then_inc(d_xin[s], 16)
                at_least(sp, xsum_ok, g - 1)
                sp.dma_start(x_res[s][:, :], ln_row(g)).then_inc(d_xres[s], 16)
                if not first:
                    store_x1(g - 1, 1 - s)

            def store_x1(g, s):
                sp.wait_ge(x1o_ok, g + 1)
                sp.dma_start(x1_scr[bass.ds(g * P, P), :], x1o[s][:, :]).then_inc(d_x1[s], 16)

            slot(0, 0, True, False)
            with sp.Fori(0, NG // 2 - 2) as k:
                slot(k * 2 + 1, 1, False, False)
                slot(k * 2 + 2, 0, False, False)
            slot(NG - 3, 1, False, False)
            slot(NG - 2, 0, False, False)
            slot(NG - 1, 1, False, True)
            store_x1(NG - 1, 1)
            sp.wait_ge(d_x1[0], 16 * NG // 2)
            sp.wait_ge(d_x1[1], 16 * NG // 2)

            sp.wait_ge(out_mm, NG)
            sp.wait_ge(x1o_ok, NG)
            for t, name in ffw:
                full = tuple(slice(None) for _ in t.shape)
                sp.dma_start(t[full], T[name]).then_inc(d_ff, 16)
            sp.dma_start(rb[:, :], T["rb"].partition_broadcast(P)).then_inc(d_ff, 16)
            sp.dma_start(xall[:, :, :], x1_scr.rearrange("(b t) d -> b t d", b=B)).then_inc(d_x, 16)
            def load_w(e):
                sp.dma_start(wbuf[:, e % 2, :], T["we"][e, :, :]).then_inc(d_w[e % 2], 16)

            def signal_w(e):
                sp.wait_ge(d_w[e % 2], 16 * (e // 2 + 1))
                sp.sem_inc(w_ready, 1)

            load_w(0)
            load_w(1)
            signal_w(0)
            signal_w(1)
            sp.wait_ge(xm_kept, NQ)
            sp.wait_ge(rt_ok, NQ)
            for t, name in moec:
                sp.dma_start(t[:, :], T[name]).then_inc(d_mc, 16)
            for t, name in moer:
                sp.dma_start(t[:, :], T[name].partition_broadcast(P)).then_inc(d_mc, 16)
            sp.wait_ge(tab_ok, 3)
            for e in range(NE - 2):
                last = sp.value_load(endi[0:1, e:e + 1], min_val=0, max_val=NS)
                sp.wait_ge(y_mm, last + 1)
                load_w(e + 2)
                signal_w(e + 2)
            for c in range(4):
                sp.wait_ge(fin_ok, 8 * (c + 1))
                sp.dma_start(out.rearrange("(b t) d -> b t d", b=B)[:, 8 * c:8 * c + 8, :],
                             xall[:, 8 * c:8 * c + 8, :]).then_inc(d_out, 16)
            sp.wait_ge(d_out, 64)
            sp.wait_ge(d_zero, 16)

        @block.tensor
        def _(pe):
            def k_half(b, g1, s, bs, u, half):
                if u == 0 and half == 0:
                    pe.wait_ge(d_cx[s], g1)
                if half == 0:
                    at_least(pe, k_ev, 2 * b)
                else:
                    at_least(pe, v_ev, b)
                dst = kv_bank[(b_par(bs) + half) % 2]
                for k in range(2):
                    last = pe.matmul(dst[:, 0:M], wk[:, k, half * P:half * P + P], cx[s][:, u, k, :],
                                     start=(k == 0), stop=(k == 1))
                last.then_inc(kv_mm, 1)

            def b_par(bs):
                return (3 * bs) % 2

            def v_unit(b, s, bs, u):
                at_least(pe, k_ev, 2 * b + 1)
                dst = kv_bank[b_par(bs)]
                for t in range(2):
                    for k in range(2):
                        last = pe.matmul(dst[:, t * D:t * D + D], cx[s][:, u, k, t * P:t * P + P], wv[:, k, :],
                                         start=(k == 0), stop=(k == 1))
                last.then_inc(kv_mm, 1)

            def scores(b, g, s, bs, u, gr):
                if u == 0 and gr == 0:
                    pe.wait_ge(qbd_ok, GB * (g + 1))
                if gr % 2 == 0:
                    pe.wait_ge(k_ev, 2 * b + gr // 2 + 1)
                at_least(pe, p_ex, 4 * b + gr - 1)
                r = 64 * (gr % 2)
                pe.matmul(s_bank[gr % 2][:, 0:M], qbd[s][r:r + 64, gr // 2, u, :], kT[bs][r:r + 64, gr // 2, :],
                          start=True, stop=True).then_inc(s_mm, 1)

            def prob_transpose(b, bs):
                pe.wait_ge(p_ex, 4 * b + 4)
                for t in range(2):
                    at_least(pe, (pT0_ev, pT1_ev)[t], b)
                    for gr in range(4):
                        last = pe.transpose(pT_bank[t][:, gr * P:gr * P + P],
                                            prob[bs][:, gr, t * P:t * P + P], ident[:, :])
                    last.then_inc(pT_mm, 1)

            def attend(b, bs):
                pe.wait_ge(pT0_ev, b + 1)
                pe.wait_ge(pT1_ev, b + 1)
                pe.wait_ge(v_ev, b + 1)
                at_least(pe, o_ev, b)
                for gr in range(4):
                    for t in range(2):
                        last = pe.matmul(o_bank[:, gr * 64:gr * 64 + 64], probT[:, t, gr * P:gr * P + P],
                                         v[bs][:, t, gr * 64:gr * 64 + 64], start=(t == 0), stop=(t == 1))
                last.then_inc(o_mm, 1)

            def x_transpose(g, s):
                pe.wait_ge(xn_ok, g + 1)
                at_least(pe, xsum_ok, g - 2)
                for k in range(2):
                    last = pe.transpose(x_bank[:, k * P:k * P + P], xn[s][:, k * P:k * P + P], ident[:, :])
                last.then_inc(xT_mm, 1)

            def o_transpose(g, s):
                for u in range(GB):
                    last = pe.transpose(x_bank[0:64, u * P:u * P + P], on[s][:, u, :], ident[:, :])
                last.then_inc(oT_mm, 1)

            def q_project(g, s):
                pe.wait_ge(xT_ev, g + 1)
                for half in range(2):
                    for k in range(2):
                        last = pe.matmul(x_bank[:, half * P:half * P + P], wq[:, k, half * P:half * P + P],
                                         xnT[s][:, k, :], start=(k == 0), stop=(k == 1))
                last.then_inc(q_mm, 1)

            def o_project(g, s):
                pe.wait_ge(oT_ev, g + 1)
                for j in range(4):
                    last = pe.matmul(x_bank[:, 0:D], oT[s][:, j, :, :], wo[:, j, :], start=(j == 0), stop=(j == 3))
                last.then_inc(out_mm, 1)

            pe.wait_ge(d_const, CONST)
            for k in range(2):
                last = pe.matmul(x_bank[:, 0:D], cxl[:, k, :], wvl[:, k, :], start=(k == 0), stop=(k == 1))
            last.then_inc(vl_mm, 1)
            pe.wait_ge(vl_ev, 1)
            x_transpose(0, 0)
            k_half(0, 16, 0, 0, 0, 0)
            k_half(0, 16, 0, 0, 0, 1)
            v_unit(0, 0, 0, 0)
            q_project(0, 0)

            def slot(g, s, first, last):
                for u in range(GB):
                    b = g * GB + u
                    nxt = not (last and u == GB - 1)
                    u1, s1, bs, bs1 = (u + 1) % GB, (s if u + 1 < GB else 1 - s), u % 2, (u + 1) % 2
                    arrive = (g + 1 + s) * 8 if isinstance(g, int) else g * 8 + 8 * (1 + s)
                    if nxt:
                        k_half(b + 1, g * 8 + (16 if s == 0 else 24) if s else g * 8 + 16, s1, bs1, u1, 0)
                    if not (first and u == 0):
                        attend(b - 1, bs1)
                    scores(b, g, s, bs, u, 0)
                    scores(b, g, s, bs, u, 1)
                    if nxt:
                        k_half(b + 1, 0, s1, bs1, u1, 1)
                    scores(b, g, s, bs, u, 2)
                    scores(b, g, s, bs, u, 3)
                    if nxt:
                        v_unit(b + 1, s1, bs1, u1)
                    prob_transpose(b, bs)
                    if u == 0 and not last:
                        x_transpose(g + 1, 1 - s)
                    if u == 1 and not first:
                        alone(pe, (xT_ev, 0 if last else g + 2), (on_ok, GB * g))
                        o_transpose(g - 1, 1 - s)
                    if u == 2 and not last:
                        if not first:
                            pe.wait_ge(oT_ev, g)
                        q_project(g + 1, 1 - s)
                    if u == 3 and not first:
                        if not last:
                            pe.wait_ge(q_ev, g + 2)
                        o_project(g - 1, 1 - s)

            slots(pe, slot)
            attend(B - 1, (B - 1) % 2)
            pe.wait_ge(xsum_ok, NG - 1)
            pe.wait_ge(on_ok, B)
            o_transpose(NG - 1, (NG - 1) % 2)
            o_project(NG - 1, (NG - 1) % 2)

            pe.wait_ge(d_ff, FFW)

            def transposes(src, done):
                for k in range(2):
                    for i in range(2):
                        c = (2 * k + i) * P
                        ins = pe.transpose(t_bank[:, c:c + P], src[:, i, k * P:k * P + P], ident[:, :])
                ins.then_inc(done, 1)

            def drives(t, i):
                at_least(pe, gc_ev, t)
                for w in range(2):
                    for c, (m, k) in enumerate(((0, 0), (1, 0), (1, 1), (2, 1))):
                        ins = pe.matmul(gc_bank[w][:, m * P:m * P + P], gw[w][:, c, :], xrT[:, k, i, :],
                                        start=(c in (0, 1, 3)), stop=(c in (0, 2, 3)))
                ins.then_inc(gc_mm, 1)

            def unit_out(Q):
                pe.wait_ge(h_ok, Q * 2 + 2)
                for i in range(2):
                    for m, a, b in ((1, 0, 2), (0, 0, 1), (2, 1, 2)):
                        ins = pe.matmul(r_bank[:, i * D + a * P:i * D + b * P], hT[i][:, m, :], ow[:, m, a * P:b * P],
                                        start=(m == 1), stop=(m == 2))
                ins.then_inc(gru_mm, 1)

            def route(Q):
                pe.wait_ge(xmT_ev, Q + 1)
                for i in range(2):
                    for k in range(2):
                        ins = pe.matmul(r_bank[:, i * NE:i * NE + NE], xmT[:, k, i, :], rw[:, k, :],
                                        start=(k == 0), stop=(k == 1))
                ins.then_inc(rt_mm, 1)

            def gate_up(q, par, f):
                if f == 0:
                    pe.wait_ge(fnT_ev, q + 1)
                at_least(pe, prod_ok, NF * q + f - 2)
                for h, w in enumerate((fg, fu)):
                    for k in range(2):
                        ins = pe.matmul(gu_bank[f % 3][0:FW[f], h * 2 * P:(h + 1) * 2 * P],
                                        w[:, k, f * P:f * P + FW[f]], fnT[par][:, k, :, :],
                                        start=(k == 0), stop=(k == 1))
                ins.then_inc(gu_mm, 1)

            def down(q):
                pe.wait_ge(prod_ok, NF * q + NF - 1)
                at_least(pe, x2_ok, q)
                for i in range(2):
                    for f in range(NF):
                        if i == 0 and f == NF - 1:
                            pe.wait_ge(prod_ok, NF * q + NF)
                        ins = pe.matmul(fd_bank[:, i * D:i * D + D], fT[0:FW[f], f, i, :], fd[0:FW[f], f, :],
                                        start=(f == 0), stop=(f == NF - 1))
                ins.then_inc(fd_mm, 1)

            def turn(q, par, parts):
                f, o, n, r = (c in parts for c in "fonr")
                if n:
                    pe.wait_ge(xr_ok, q * 2 + 6)
                    at_least(pe, xrT_ev, q + 2)
                    at_least(pe, fnT_ev, q + 1)
                    transposes(xr, xrT_mm)
                if f:
                    gate_up(q, par, 0)
                if o:
                    at_least(pe, rt_ok, q - 1)
                    at_least(pe, xa_ok, q + 1)
                    unit_out(q + 1)
                if n:
                    pe.wait_ge(xrT_ev, q + 3)
                    drives(q * 2 + 4, 0)
                if f:
                    gate_up(q, par, 1)
                if r:
                    pe.wait_ge(xm_ok, q * 2)
                    if n:
                        pe.wait_ge(xrT_ev, q + 3)
                    else:
                        pe.wait_ge(fnT_ev, min(q + 1, NQ))
                        pe.wait_ge(xmT_ev, q - 1)
                    transposes(xmt, xmT_mm)
                if f:
                    gate_up(q, par, 2)
                if n:
                    drives(q * 2 + 5, 1)
                if r:
                    if o:
                        pe.wait_ge(xa_ok, q + 2)
                    else:
                        pe.wait_ge(rt_ok, q - 1)
                    route(q - 1)
                if f:
                    gate_up(q, par, 3)
                if o:
                    pe.wait_ge(fn_ok, q * 2 + 4)
                    if r:
                        pe.wait_ge(xmT_ev, q)
                    else:
                        pe.wait_ge(xrT_ev, q + 3)
                    transposes(fn, fnT_mm)
                if f:
                    gate_up(q, par, 4)
                    gate_up(q, par, 5)
                    down(q)

            turns(pe, turn)

            pe.wait_ge(d_mc, MOEC)
            pe.wait_ge(route_ok, 1)
            pe.wait_ge(oneh_ok, 1)
            pe.matmul(bank[4][:, 0:NT * NE], lt[:, :], oneh[:, :], start=True, stop=True)
            pe.matmul(bank[5][:, 0:NT * NE], ones[:, :], oneh[:, :], start=True, stop=True).then_inc(rank_mm, 1)
            pe.wait_ge(tab_ok, 3)

            def xs_transpose(sl, i):
                pe.wait_ge(d_xs[i], (sl - i) * 8 + 16)
                at_least(pe, xsT_ev, sl)
                for k in range(2):
                    ins = pe.transpose(xs_bank[:, k * P:k * P + P], xs[i][:, k * P:k * P + P], ident[:, :])
                ins.then_inc(xsT_mm, 1)

            def hidden(sl, i, half, par):
                at_least(pe, hid_ok, 2 * sl + half - 1)
                for b_, o in ((a_bank, 0), (g_bank, FF)):
                    for k in range(2):
                        c = k * 2 * FF + o + half * 512
                        ins = pe.matmul(b_[half][:, :], xsT[i][:, k, :], wbuf[:, bass.ds(par, 1), c:c + 512],
                                        start=(k == 0), stop=(k == 1))
                ins.then_inc(ag_mm, 1)

            def hid_transpose(sl, half):
                pe.wait_ge(hid_ok, 2 * sl + half + 1)
                at_least(pe, (hT0_ev, hT1_ev)[half], sl)
                for f in range(4):
                    ins = pe.transpose(hT_bank[half][:, f * P:f * P + P], hid[half][:, f * P:f * P + P], ident[:, :])
                ins.then_inc(hT_mm, 1)

            def expert_down(sl, par):
                at_least(pe, y_ok, sl)
                for f in range(FT):
                    if f % 4 == 0:
                        pe.wait_ge((hT0_ev, hT1_ev)[f // 4], sl + 1)
                    c = 4 * FF + f * D
                    ins = pe.matmul(y_bank[:, 0:D], hidT[f // 4][:, f % 4, :], wbuf[:, bass.ds(par, 1), c:c + D],
                                    start=(f == 0), stop=(f == FT - 1))
                ins.then_inc(y_mm, 1)

            def parity(sl):
                return pe.value_load(pari[0:1, bass.ds(sl, 1)], min_val=0, max_val=1)

            pe.sem_inc(y_mm, 1)
            xs_transpose(0, 0)

            def estep(sl, i, first, last):
                e = pe.value_load(expi[0:1, bass.ds(sl, 1)], min_val=0, max_val=NE - 1)
                par = parity(sl)
                pe.wait_ge(w_ready, e + 1)
                pe.wait_ge(xsT_ev, sl + 1)
                hidden(sl, i, 0, par)
                if not first:
                    hid_transpose(sl - 1, 1)
                    expert_down(sl - 1, parity(sl - 1))
                hidden(sl, i, 1, par)
                hid_transpose(sl, 0)
                if not last:
                    xs_transpose(sl + 1, 1 - i)

            tiles_of_experts(pe, estep)
            hid_transpose(NS - 1, 1)
            expert_down(NS - 1, parity(NS - 1))

        @block.scalar
        def _(act):
            def k_copy(b, bs, half):
                act.wait_ge(kv_mm, 3 * b + half + 1)
                src = kv_bank[((3 * bs) % 2 + half) % 2]
                act.activation(kT[bs][:, half, :], src[:, 0:M], ACT.Identity,
                               bias=bk[:, half:half + 1]).then_inc(k_ev, 1)

            def exp(b, bs, gr):
                if gr == 0:
                    at_least(act, ol_ok, b - 1)
                    at_least(act, rinv_ok, b - 1)
                act.wait_ge(mx, 4 * b + gr + 1)
                act.activation(prob[bs][:, gr, :], s_bank[gr % 2][:, 0:M], ACT.Exp, bias=negmax[bs][:, gr:gr + 1],
                               accum_out=rowsum[bs][:, gr:gr + 1]).then_inc(p_ex, 1)

            act.wait_ge(d_const, CONST)
            act.wait_ge(xT_mm, 1)
            act.activation(xnT[0][:, :, :], x_bank[:, 0:2 * P].rearrange("p (k t) -> p k t", k=2),
                           ACT.Identity).then_inc(xT_ev, 1)
            k_copy(0, 0, 0)
            k_copy(0, 0, 1)

            def q_copy(g, s):
                act.wait_ge(q_mm, g + 1)
                at_least(act, qbd_ok, GB * (g - 1))
                for half in range(2):
                    ins = act.activation(qT[s][:, half, :], x_bank[:, half * P:half * P + P], ACT.Identity,
                                         bias=bq[:, half:half + 1])
                ins.then_inc(q_ev, 1)

            q_copy(0, 0)

            def slot(g, s, first, last):
                for u in range(GB):
                    b = g * GB + u
                    nxt = not (last and u == GB - 1)
                    bs, bs1 = u % 2, (u + 1) % 2
                    if nxt:
                        k_copy(b + 1, bs1, 0)
                    exp(b, bs, 0)
                    exp(b, bs, 1)
                    if nxt:
                        k_copy(b + 1, bs1, 1)
                    exp(b, bs, 2)
                    exp(b, bs, 3)
                    act.wait_ge(pT_mm, 2 * b + 1)
                    at_least(act, o_mm, b)
                    act.activation(probT[:, 0, :], pT_bank[0][:, :], ACT.Identity).then_inc(pT0_ev, 1)
                    if u == 0 and not last:
                        act.wait_ge(xT_mm, g + 2)
                        act.activation(xnT[1 - s][:, :, :], x_bank[:, 0:2 * P].rearrange("p (k t) -> p k t", k=2),
                                       ACT.Identity).then_inc(xT_ev, 1)
                    if u == 1 and not first:
                        o_copy(g - 1, 1 - s)
                    if u == 2 and not last:
                        q_copy(g + 1, 1 - s)

            def o_copy(g, s):
                act.wait_ge(oT_mm, g + 1)
                act.activation(oT[s][:, :, :, :].rearrange("p j u l -> p u j l"),
                               x_bank[0:64, :].rearrange("p (u j l) -> p u j l", u=GB, j=4),
                               ACT.Identity).then_inc(oT_ev, 1)

            slots(act, slot)
            o_copy(NG - 1, (NG - 1) % 2)

            act.wait_ge(d_ff, FFW)
            act.wait_ge(be_ok, 3)

            def square_sum(c, i, src, need, Q, free, done):
                alone(act, (need, Q * 2 + i + 1 if c == "A" else Q + 1), (free, Q))
                act.activation(junk[c][i][:, :], src, ACT.Square,
                               accum_out=small["ss" + c][:, i:i + 1]).then_inc(done, 1)

            def scaled(dst, i, src, col, need, Q, free, done):
                alone(act, (need, Q + 1), (free, Q))
                act.activation(dst[:, i, :], src, ACT.Identity, scale=col[:, i:i + 1]).then_inc(done, 1)

            def gamma_copy(dst, g, mm, Q, done):
                act.wait_ge(mm, Q + 1)
                for k in range(2):
                    ins = act.activation(dst[:, k, :, :], t_bank[:, 2 * k * P:2 * (k + 1) * P].rearrange(
                        "p (i b) -> p i b", i=2), ACT.Identity, scale=gam1[g][:, k:k + 1])
                ins.then_inc(done, 1)

            def silu(q, f):
                act.wait_ge(gu_mm, NF * q + f + 1)
                at_least(act, prod_ok, NF * q + f - 1)
                act.activation(sg[f % 2][0:FW[f], :], gu_bank[f % 3][0:FW[f], 0:2 * P], ACT.Silu).then_inc(silu_ok, 1)

            def drive_copy(t, i):
                act.wait_ge(gc_mm, t + 1)
                at_least(act, pot_ok, t - 1)
                for w in range(2):
                    ins = act.activation(gc[i][:, 3 * w:3 * w + 3, :],
                                         gc_bank[w][:, 0:3 * P].rearrange("p (m b) -> p m b", m=3), ACT.Identity)
                ins.then_inc(gc_ev, 1)

            def route_copy(Q):
                act.wait_ge(xmT_mm, Q + 1)
                at_least(act, rt_mm, Q)
                act.activation(xmT[:, :, :, :], t_bank[:, :].rearrange("p (k i b) -> p k i b", k=2, i=2),
                               ACT.Identity).then_inc(xmT_ev, 1)

            def turn(q, par, parts):
                f, o, n, m, r = (c in parts for c in "fonmr")
                if n:
                    at_least(act, gc_mm, q * 2 + 4)
                    gamma_copy(xrT, 0, xrT_mm, q + 2, xrT_ev)
                if f:
                    silu(q, 0)
                if o:
                    for i in range(2):
                        square_sum("B", i, xa[:, i, :], xa_ok, q + 1, smB_ok, ssB_ok)
                if n:
                    drive_copy(q * 2 + 4, 0)
                if f:
                    silu(q, 1)
                if o:
                    for i in range(2):
                        scaled(fn, i, xa[:, i, :], small["scB"], scB_ok, q + 1, fnT_mm, fn_ok)
                if r:
                    route_copy(q - 1)
                if f:
                    silu(q, 2)
                if n:
                    drive_copy(q * 2 + 5, 1)
                if m:
                    for i in range(2):
                        square_sum("A", i, xm[:, q * 2 + 6 + i, :], xl_ok, q + 3, smA_ok, ssA_ok)
                if f:
                    silu(q, 3)
                if o:
                    at_least(act, gu_mm, NF * q)
                    gamma_copy(fnT[1 - par], 1, fnT_mm, q + 1, fnT_ev)
                if m:
                    for i in range(2):
                        scaled(xr, i, xm[:, q * 2 + 6 + i, :], small["scA"], scA_ok, q + 3, xrT_mm, xr_ok)
                if f:
                    silu(q, 4)
                    silu(q, 5)

            turns(act, turn)

            act.wait_ge(lsh_ok, 1)
            act.activation(lex[:, :], lsh[:, :], ACT.Exp).then_inc(lex_ok, 1)

            def astep(sl, i, first, last):
                for half in range(2):
                    act.wait_ge(ag_mm, 2 * sl + half + 1)
                    at_least(act, hid_ok, 2 * sl + half - 1)
                    act.activation(sa[half][:, :], a_bank[half][:, :], ACT.Silu).then_inc(sa_ok, 1)
                act.wait_ge(hT_mm, 2 * sl + 1)
                act.wait_ge(y_mm, sl + 1)
                act.activation(hidT[0][:, :, :], hT_bank[0][:, :].rearrange("p (f b) -> p f b", f=4),
                               ACT.Identity).then_inc(hT0_ev, 1)
                if not last:
                    xs_copy(sl + 1, 1 - i)

            def xs_copy(sl, i):
                act.wait_ge(xsT_mm, sl + 1)
                at_least(act, ag_mm, 2 * (sl - 1))
                act.activation(xsT[i][:, :, :], xs_bank[:, 0:2 * P].rearrange("p (k b) -> p k b", k=2),
                               ACT.Identity).then_inc(xsT_ev, 1)

            xs_copy(0, 0)
            tiles_of_experts(act, astep)

        @block.vector
        def _(dve):
            def norm_stats(g, s):
                dve.wait_ge(d_xin[s], loads(g, s))
                at_least(dve, mv_ok, g - 1)
                dve.bn_stats(stats[s][:, :], x_in[s][:, :]).then_inc(st_ok, 1)
                alone(dve, (st_ok, g + 1))
                dve.bn_aggr(mv[s][:, :], stats[s][:, :]).then_inc(mv_ok, 1)

            def loads(g, s):
                return (g - s) * 8 + 16

            def norm_apply(g, s):
                dve.wait_ge(rstd_ok, g + 1)
                at_least(dve, xT_mm, g - 1)
                dve.tensor_scalar(xn[s][:, :], x_in[s][:, :], mv[s][:, 0:1], rstd[s][:, 0:1],
                                  ALU.subtract, ALU.mult).then_inc(xn_ok, 1)

            def v_copy(b, bs):
                dve.wait_ge(kv_mm, 3 * b + 3)
                dve.tensor_tensor(v[bs][:, :, :], kv_bank[(3 * bs) % 2][:, :].rearrange("p (t n) -> p t n", t=2),
                                  spread(bv[:, :], 1, 2), ALU.add).then_inc(v_ev, 1)

            def take_out(b, bs):
                dve.wait_ge(p_ex, 4 * b + 4)
                at_least(dve, on_ok, b - 1)
                dve.reciprocal(rinv[bs][:, :], rowsum[bs][:, :]).then_inc(rinv_ok, 1)
                dve.wait_ge(o_mm, b + 1)
                dve.wait_ge(ol_ok, b + 1)
                for j in range(4):
                    q = slice(32 * j, 32 * j + 32)
                    ins = dve.tensor_tensor(
                        oraw[bs][q, :, :], o_bank[q, 0:D].rearrange("p (g n) -> p g n", g=4)[:, :, 16 * j:16 * j + 16],
                        olast[bs][q, :, :], ALU.add)
                ins.then_inc(o_ev, 1)

            def out_sum(g, s):
                dve.wait_ge(out_mm, g + 1)
                dve.wait_ge(d_xres[s], loads(g, s))
                at_least(dve, x1o_ok, g)
                dve.tensor_tensor(xsum[s][:, :], x_bank[:, 0:D], x_res[s][:, :], ALU.add).then_inc(xsum_ok, 1)

            dve.wait_ge(d_const, CONST)
            dve.wait_ge(vl_mm, 1)
            dve.tensor_tensor(vlast[:, :], x_bank[:, 0:D], bvl[:, :], ALU.add).then_inc(vl_ev, 1)
            for g in range(2):
                norm_stats(g, g)
                norm_apply(g, g)
            v_copy(0, 0)

            def slot(g, s, first, last):
                final = last or (isinstance(g, int) and g + 2 >= NG)
                for u in range(GB):
                    b = g * GB + u
                    nxt = not (last and u == GB - 1)
                    bs, bs1 = u % 2, (u + 1) % 2
                    if not (first and u == 0):
                        take_out(b - 1, bs1)
                    for gr in range(4):
                        dve.wait_ge(s_mm, 4 * b + gr + 1)
                        if gr == 0:
                            at_least(dve, p_ex, 4 * (b - 1))
                        dve.tensor_reduce(negmax[bs][:, gr:gr + 1], s_bank[gr % 2][:, 0:M], AXX, ALU.max,
                                          negate=True).then_inc(mx, 1)
                    if nxt:
                        v_copy(b + 1, bs1)
                    dve.wait_ge(pT_mm, 2 * b + 2)
                    at_least(dve, o_mm, b)
                    dve.tensor_copy(probT[:, 1, :], pT_bank[1][:, :]).then_inc(pT1_ev, 1)
                    if u == 1 and not final:
                        norm_stats(g + 2, s)
                    if u == 2 and not final:
                        norm_apply(g + 2, s)
                    if u == 3 and not first:
                        out_sum(g - 1, 1 - s)

            slot(0, 0, True, False)
            with dve.Fori(0, NG // 2 - 2) as k:
                slot(k * 2 + 1, 1, False, False)
                slot(k * 2 + 2, 0, False, False)
            slot(NG - 3, 1, False, False)
            slot(NG - 2, 0, False, False)
            slot(NG - 1, 1, False, True)
            take_out(B - 1, (B - 1) % 2)
            out_sum(NG - 1, (NG - 1) % 2)

            dve.wait_ge(x1o_ok, NG)
            dve.memset(mem[:, :, :], 0.0).then_inc(c2, 1)
            dve.wait_ge(be_ok, 1)
            dve.reciprocal(beta[:, :], beta[:, :]).then_inc(c2, 1)
            dve.wait_ge(be_ok, 4)
            dve.wait_ge(d_x, 16)
            dve.wait_ge(c2, 2)

            def stats_of(c, i, src, Q, st_ok_, mv_ok_, rs_ok_, used):
                alone(dve, (mv_ok_, Q * 2))
                dve.bn_stats(st[c][i][:, :], src).then_inc(st_ok_, 1)
                alone(dve, (st_ok_, Q * 2 + i + 1), (rs_ok_, Q), (used, Q * 2))
                dve.bn_aggr(mv2[c][:, i, :], st[c][i][:, :]).then_inc(mv_ok_, 1)

            def potential(t, i):
                dve.wait_ge(gc_ev, t + 1)
                at_least(dve, mem_ok, t)
                for m in range(6):
                    ins = dve.scalar_tensor_tensor(pot[:, m, :], mem[:, m, :], beta[:, m:m + 1], gc[i][:, m, :],
                                                   ALU.mult, ALU.add)
                ins.then_inc(pot_ok, 1)
                dve.wait_ge(pot_ok, t + 1)
                dve.tensor_scalar(rnd[:, :, :], pot[:, :, :], ROUND, ROUND, ALU.add, ALU.subtract).then_inc(rnd_ok, 1)

            def spikes(t, i):
                dve.wait_ge(rnd_ok, t + 1)
                at_least(dve, zc_ok, t - 1)
                dve.tensor_scalar(spk[i][:, :, :], rnd[:, :, :], -1.0, 1.0, ALU.max, ALU.min).then_inc(spk_ok, 1)

            def membrane(t, i):
                dve.wait_ge(spk_ok, t + 1)
                for m in range(6):
                    ins = dve.scalar_tensor_tensor(mem[:, m, :], spk[i][:, m, :], nthr[:, m:m + 1], pot[:, m, :],
                                                   ALU.mult, ALU.add)
                ins.then_inc(mem_ok, 1)

            def prod(q, f):
                dve.wait_ge(silu_ok, NF * q + f + 1)
                dve.tensor_tensor(fT[0:FW[f], f, :, :].rearrange("p i b -> p (i b)"), gu_bank[f % 3][0:FW[f], 2 * P:4 * P],
                                  sg[f % 2][0:FW[f], :], ALU.mult).then_inc(prod_ok, 1)

            def unit_sum(Q):
                dve.wait_ge(gru_mm, Q + 1)
                dve.wait_ge(xl_ok, Q * 2 + 2)
                at_least(dve, add_ok, Q)
                at_least(dve, fn_ok, Q * 2)
                dve.tensor_tensor(xa[:, :, :], r_bank[:, :].rearrange("p (i d) -> p i d", i=2),
                                  xm[:, bass.ds(Q * 2, 2), :], ALU.add).then_inc(xa_ok, 1)

            def logits_out(Q):
                dve.wait_ge(rt_mm, Q + 1)
                dve.tensor_tensor(logit[:, bass.ds(Q * 2, 2), :], r_bank[:, 0:2 * NE].rearrange("p (i e) -> p i e", i=2),
                                  spread(rb[:, :], 1, 2), ALU.add).then_inc(rt_ok, 1)

            def turn(q, par, parts):
                f, o, n, m, r = (c in parts for c in "fonmr")
                last = q * 2 - 2
                if r:
                    dve.wait_ge(fd_mm, q)
                    dve.wait_ge(add_ok, q)
                    dve.tensor_tensor(xall[:, bass.ds(last, 2), :], fd_bank[:, :].rearrange("p (i d) -> p i d", i=2),
                                      xall[:, bass.ds(last, 2), :], ALU.add).then_inc(x2_ok, 1)
                    alone(dve, (x2_ok, q))
                    for i in range(2):
                        stats_of("B", i, xall[:, last + i, :], q - 1, stB_ok, mvB_ok, rsB_ok, xm_ok)
                if f:
                    prod(q, 0)
                if m:
                    for i in range(2):
                        stats_of("A", i, xall[:, q * 2 + 6 + i, :], q + 3, stA_ok, mvA_ok, rsA_ok, xl_ok)
                if o:
                    unit_sum(q + 1)
                if r:
                    for i in range(2):
                        dve.wait_ge(rsB_ok, q)
                        at_least(dve, xmT_mm, q - 1)
                        at_least(dve, xm_kept, q - 1)
                        dve.tensor_scalar(xmt[:, i, :], xall[:, last + i, :], mv2["B"][:, i, 0:1],
                                          small["rsB"][:, i:i + 1], ALU.subtract, ALU.mult).then_inc(xm_ok, 1)
                if n:
                    potential(q * 2 + 4, 0)
                if f:
                    prod(q, 1)
                if n:
                    spikes(q * 2 + 4, 0)
                if m:
                    for i in range(2):
                        dve.wait_ge(rsA_ok, q + 4)
                        dve.tensor_scalar(xm[:, q * 2 + 6 + i, :], xall[:, q * 2 + 6 + i, :], mv2["A"][:, i, 0:1],
                                          small["rsA"][:, i:i + 1], ALU.subtract, ALU.mult).then_inc(xl_ok, 1)
                if n:
                    membrane(q * 2 + 4, 0)
                if f:
                    prod(q, 2)
                if n:
                    potential(q * 2 + 5, 1)
                if f:
                    prod(q, 3)
                if n:
                    spikes(q * 2 + 5, 1)
                    membrane(q * 2 + 5, 1)
                if r:
                    logits_out(q - 1)
                if f:
                    prod(q, 4)
                    prod(q, 5)

            turns(dve, turn)

            done = [0]

            def te_bank(b_):
                return b_[:, 0:NT * NE].rearrange("p (t e) -> p t e", e=NE)

            def one_col(n):
                return ones[:, 0:1].to_broadcast([P, n])

            def then(ins):
                done[0] += 1
                ins.then_inc(dv_chain, 1)
                dve.wait_ge(dv_chain, done[0])

            te = lambda a: a[:, :].rearrange("p (t e) -> p t e", e=NE)
            et = lambda a: a[:, :].rearrange("p (e t) -> p e t", e=NE)
            dve.wait_ge(d_mc, MOEC)
            dve.wait_ge(route_ok, 1)
            dve.wait_ge(rt_ok, NQ)
            then(dve.tensor_reduce(lmax[:, :], logit[:, :, :], AXX, ALU.max))
            dve.tensor_tensor(te(lsh), logit[:, :, :], spread(lmax[:, :], 2, NE), ALU.subtract).then_inc(lsh_ok, 1)
            dve.wait_ge(lsh_ok, 1)
            then(dve.tensor_scalar(rank[:, :], lsh[:, :], 0.0, None, ALU.is_ge))
            then(dve.tensor_tensor(te(cum), te(rank), spread(descend[:, :], 1, NT), ALU.mult))
            then(dve.tensor_reduce(best[:, :], te(cum), AXX, ALU.max))
            dve.tensor_tensor(te(oneh), te(cum), spread(best[:, :], 2, NE), ALU.is_equal).then_inc(oneh_ok, 1)
            dve.wait_ge(lex_ok, 1)
            then(dve.tensor_reduce(lsum[:, :], te(lex), AXX, ALU.add))
            then(dve.reciprocal(maxp[:, :], lsum[:, :]))
            dve.wait_ge(rank_mm, 1)
            then(dve.tensor_copy(et(tot), te_bank(bank[5]).rearrange("p t e -> p e t")))
            then(dve.tensor_tensor_scan(cum[:, :], one_col(NT * NE), tot[:, :], 0.0, ALU.mult, ALU.add))
            then(dve.tensor_tensor(exc[:, :], cum[:, :], tot[:, :], ALU.subtract))
            then(dve.tensor_reduce(cnt[:, :], et(tot), AXX, ALU.add))
            then(dve.tensor_scalar(tlf[:, :], cnt[:, :], 1.0 / P, (P - 1) / P - 0.5 + 0.5 / P, ALU.mult, ALU.add))
            then(dve.tensor_scalar(tiles[:, :], tlf[:, :], ROUND, ROUND, ALU.add, ALU.subtract))
            then(dve.tensor_tensor_scan(ctile[:, :], one_col(NE), tiles[:, :], 0.0, ALU.mult, ALU.add))
            then(dve.tensor_tensor(base_e[:, :], ctile[:, :], tiles[:, :], ALU.subtract))
            then(dve.scalar_tensor_tensor(shift[:, :], base_e[:, :], float(P), et(exc)[:, :, 0], ALU.mult, ALU.subtract))
            then(dve.tensor_tensor(et(exc), et(exc), spread(shift[:, :], 2, NT), ALU.add))
            then(dve.tensor_tensor(te(rank), te_bank(bank[4]), et(exc).rearrange("p e t -> p t e"), ALU.add))
            then(dve.tensor_tensor(rank[:, :], rank[:, :], oneh[:, :], ALU.mult))
            then(dve.tensor_reduce(posf[:, :], te(rank), AXX, ALU.add))
            dve.tensor_copy(pos[:, :], posf[:, :]).then_inc(pos_ok, 1)
            then(dve.tensor_tensor(cmp7[:, :, :], spread(slotno[:, :], 2, NE - 1), spread(ctile[:, 0:NE - 1], 1, NS), ALU.is_ge))
            then(dve.tensor_tensor(alt7[:, :, :], cmp7[:, :, :], spread(altern[:, 0:NE - 1], 1, NS), ALU.mult))
            then(dve.tensor_reduce(expf[:, :], cmp7[:, :, :], AXX, ALU.add))
            then(dve.tensor_reduce(parf[:, :], alt7[:, :, :], AXX, ALU.add))
            dve.tensor_copy(expi[:, :], expf[:, :]).then_inc(tab_ok, 1)
            dve.tensor_copy(pari[:, :], parf[:, :]).then_inc(tab_ok, 1)
            dve.tensor_copy(endi[:, :], ctile[:, :]).then_inc(tab_ok, 1)

            def vstep(sl, i, first, last):
                vhid(sl, 0)
                if not first:
                    vback(sl - 1, 1 - i)
                vhid(sl, 1)

            def vhid(sl, half):
                dve.wait_ge(sa_ok, 2 * sl + half + 1)
                at_least(dve, hT_mm, 2 * sl + half - 1)
                dve.tensor_tensor(hid[half][:, :], g_bank[half][:, :], sa[half][:, :], ALU.mult).then_inc(hid_ok, 1)

            def vback(sl, i):
                dve.wait_ge(hT_mm, 2 * sl + 2)
                dve.wait_ge(y_mm, sl + 1)
                dve.tensor_copy(hidT[1][:, :, :], hT_bank[1][:, :].rearrange("p (f b) -> p f b", f=4)).then_inc(hT1_ev, 1)
                dve.wait_ge(y_mm, sl + 2)
                at_least(dve, d_ys[i], (sl - i) * 8)
                dve.tensor_copy(ys[i][:, :], y_bank[:, 0:D]).then_inc(y_ok, 1)

            tiles_of_experts(dve, vstep)
            vback(NS - 1, (NS - 1) % 2)
            for t in range(NT):
                dve.wait_ge(d_yg[t % 4], 16 * (t // 4 + 1))
                dve.scalar_tensor_tensor(xall[:, t, :], yg[t % 4][:, :], maxp[:, t:t + 1], xall[:, t, :],
                                         ALU.mult, ALU.add).then_inc(fin_ok, 1)

        @block.gpsimd
        def _(pool):
            pool.memset(halfneg[:, :], -0.5).then_inc(c_ok, 1)
            pool.memset(x1o[0][:, :], 0.0).then_inc(z_ok, 1)
            pool.wait_ge(c_ok, 1)
            pool.wait_ge(d_const, CONST)
            pool.wait_ge(d_zero, 16)

            def norm_scale(g, s):
                alone(pool, (mv_ok, g + 1), (xn_ok, g - 1))
                pool.tensor_scalar(vare[s][:, :], mv[s][:, 1:2], EPS, None, ALU.add).then_inc(var_ok, 1)
                pool.wait_ge(var_ok, g + 1)
                pool.tensor_tensor(rstd[s][:, :], vare[s][:, :], halfneg[:, :], ALU.pow).then_inc(rstd_ok, 1)

            def block_queries(g, s):
                pool.wait_ge(q_ev, g + 1)
                at_least(pool, s_mm, 4 * GB * (g - 1))
                for u in range(GB):
                    q = qT[s][:, :, u * L:u * L + L]
                    for half in range(2):
                        ins = pool.tensor_tensor(
                            qbd[s][:, half, u, :].rearrange("p (j l) -> p j l", j=4),
                            spread(qT[s][:, half, u * L:u * L + L], 1, 4), spread(headmask[:, :], 2, L), ALU.mult)
                    ins.then_inc(qbd_ok, 1)

            def last_key(b, g, s, u, bs):
                pool.wait_ge(p_ex, 4 * b + 4)
                if u == 0:
                    pool.wait_ge(d_vb[s], ((g - s) * 8 + 16) * 4)
                at_least(pool, o_ev, b - 1)
                pool.tensor_tensor(olast[bs][:, :, :], vb[s][:, u, :].rearrange("p (g d) -> p g d", g=4),
                                   prob[bs][:, :, KEYS:M].to_broadcast([P, 4, DH]), ALU.mult).then_inc(ol_ok, 1)

            def normalise(b, g, s, u, bs):
                pool.wait_ge(o_ev, b + 1)
                if u == 0:
                    at_least(pool, oT_mm, g - 1)
                pool.tensor_tensor(on[s][:, u, :].rearrange("p (g d) -> p g d", g=4), oraw[bs][:, :, :],
                                   spread(rinv[bs][:, :], 2, DH), ALU.mult).then_inc(on_ok, 1)

            def add_bias(g, s):
                pool.wait_ge(xsum_ok, g + 1)
                at_least(pool, d_x1[s], (g - s) * 8)
                pool.tensor_tensor(x1o[s][:, :], xsum[s][:, :], bo[:, :], ALU.add).then_inc(x1o_ok, 1)

            norm_scale(0, 0)
            norm_scale(1, 1)
            block_queries(0, 0)

            def slot(g, s, first, last):
                final = last or (isinstance(g, int) and g + 2 >= NG)
                for u in range(GB):
                    b = g * GB + u
                    bs, bs1 = u % 2, (u + 1) % 2
                    if not (first and u == 0):
                        if u == 0:
                            normalise(b - 1, g - 1, 1 - s, GB - 1, bs1)
                        else:
                            normalise(b - 1, g, s, u - 1, bs1)
                    last_key(b, g, s, u, bs)
                    if u == 1 and not final:
                        norm_scale(g + 2, s)
                    if u == 3 and not last:
                        block_queries(g + 1, 1 - s)
                    if u == 3 and not first:
                        add_bias(g - 1, 1 - s)

            slot(0, 0, True, False)
            with pool.Fori(0, NG // 2 - 2) as k:
                slot(k * 2 + 1, 1, False, False)
                slot(k * 2 + 2, 0, False, False)
            slot(NG - 3, 1, False, False)
            slot(NG - 2, 0, False, False)
            slot(NG - 1, 1, False, True)
            normalise(B - 1, NG - 1, 1, GB - 1, 1)
            add_bias(NG - 1, 1)

            pool.memset(hT[1][:, :, :], 0.0).then_inc(c2, 16)
            pool.memset(ebase[:, :], float(np.e)).then_inc(c2, 16)
            pool.wait_ge(d_ff, FFW)
            pool.wait_ge(c2, 32)
            pool.tensor_scalar(braw[:, :], braw[:, :], -1.0, None, ALU.mult).then_inc(zw_ok, 1)
            pool.wait_ge(zw_ok, 1)
            pool.tensor_tensor(beta[:, :], ebase[:, :], braw[:, :], ALU.pow).then_inc(zw_ok, 1)
            pool.wait_ge(zw_ok, 2)
            pool.tensor_scalar(beta[:, :], beta[:, :], 1.0, None, ALU.add).then_inc(be_ok, 1)
            for i in range(2):
                pool.tensor_scalar(gam1[i][:, :], gam[i][:, :], 1.0, None, ALU.add).then_inc(be_ok, 1)
            pool.tensor_scalar(nthr[:, :], thr[:, :], -1.0, None, ALU.mult).then_inc(be_ok, 1)

            def std_inverse(c, Q, mv_ok_, ve_ok, rs_ok, used):
                alone(pool, (mv_ok_, Q * 2 + 2), (used, Q * 2))
                pool.tensor_scalar(small["ve" + c][:, :], mv2[c][:, :, 1], EPS, None, ALU.add).then_inc(ve_ok, 1)
                pool.wait_ge(ve_ok, Q + 1)
                pool.tensor_tensor(small["rs" + c][:, :], small["ve" + c][:, :], halfneg[:, :].to_broadcast([P, 2]),
                                   ALU.pow).then_inc(rs_ok, 1)

            def rms_scale(c, Q, ss_ok, sm_ok, sp_ok, sc_ok, used):
                alone(pool, (ss_ok, Q * 2 + 2))
                pool.tensor_scalar(small["sm" + c][:, :], small["ss" + c][:, :], RMS_MIN ** 2, None,
                                   ALU.max).then_inc(sm_ok, 1)
                pool.wait_ge(sm_ok, Q + 1)
                pool.tensor_tensor(small["sp" + c][:, :], small["sm" + c][:, :], halfneg[:, :].to_broadcast([P, 2]),
                                   ALU.pow).then_inc(sp_ok, 1)
                alone(pool, (sp_ok, Q + 1), (used, Q * 2))
                pool.tensor_scalar(small["sc" + c][:, :], small["sp" + c][:, :], float(D) ** 0.5, None,
                                   ALU.mult).then_inc(sc_ok, 1)

            def state(Q, i):
                t = Q * 2 + i
                alone(pool, (spk_ok, t + 1), (h_ok, t))
                pool.tensor_scalar(zed[:, :, :], spk[i][:, 0:3, :], 0.5, 0.5, ALU.mult, ALU.add)
                pool.tensor_scalar(wed[:, :, :], spk[i][:, 0:3, :], -0.5, 0.5, ALU.mult, ALU.add).then_inc(zw_ok, 1)
                pool.wait_ge(zw_ok, t + 3)
                pool.tensor_tensor(zc[:, :, :], zed[:, :, :], spk[i][:, 3:6, :], ALU.mult)
                pool.tensor_tensor(wh[:, :, :], wed[:, :, :], hT[1 - i][:, :, :], ALU.mult).then_inc(zc_ok, 1)
                pool.wait_ge(zc_ok, t + 1)
                at_least(pool, gru_mm, Q)
                pool.tensor_tensor(hT[i][:, :, :], wh[:, :, :], zc[:, :, :], ALU.add).then_inc(h_ok, 1)

            def turn(q, par, parts):
                f, o, n, m, r = (c in parts for c in "fonmr")
                if r:
                    std_inverse("B", q - 1, mvB_ok, veB_ok, rsB_ok, xm_ok)
                if m:
                    std_inverse("A", q + 3, mvA_ok, veA_ok, rsA_ok, xl_ok)
                if o:
                    rms_scale("B", q + 1, ssB_ok, smB_ok, spB_ok, scB_ok, fn_ok)
                    pool.wait_ge(xa_ok, q + 2)
                    pool.tensor_tensor(xall[:, bass.ds(q * 2 + 2, 2), :], xall[:, bass.ds(q * 2 + 2, 2), :], xa[:, :, :],
                                       ALU.add).then_inc(add_ok, 1)
                if r:
                    pool.wait_ge(xm_ok, q * 2)
                    pool.tensor_copy(xm[:, bass.ds(q * 2 - 2, 2), :], xmt[:, :, :]).then_inc(xm_kept, 1)
                if n:
                    state(q + 2, 0)
                if m:
                    rms_scale("A", q + 3, ssA_ok, smA_ok, spA_ok, scA_ok, xr_ok)
                if n:
                    state(q + 2, 1)

            turns(pool, turn)

            pool.memset(ones[:, :], 1.0).then_inc(route_ok, 1)
            for t in range(NT):
                if t == 0:
                    pool.wait_ge(pos_ok, 1)
                pool.indirect_dma_start(xs_scr, bass.IndirectOffsetOnAxis(pos[:, t:t + 1].bitcast(U32), 0),
                                        xm[:, t, :], None).then_inc(d_sort, 16)
            pool.wait_ge(d_sort, 16 * NT)

            def count(sl, i):
                return (sl - i) * 8

            def load_xs(sl, i):
                pool.dma_start(xs[i][:, :], xs_scr[bass.ds(sl * P, P), :]).then_inc(d_xs[i], 16)

            load_xs(0, 0)
            load_xs(1, 1)

            def pstep(sl, i, first, last):
                if isinstance(sl, int) and sl + 2 >= NS:
                    pass
                else:
                    pool.wait_ge(xsT_mm, sl + 1)
                    load_xs(sl + 2, i)
                pool.wait_ge(y_ok, sl + 1)
                pool.dma_start(ys_scr[bass.ds(sl * P, P), :], ys[i][:, :]).then_inc(d_ys[i], 16)

            tiles_of_experts(pool, pstep)
            pool.wait_ge(d_ys[0], 16 * ((NS + 1) // 2))
            pool.wait_ge(d_ys[1], 16 * (NS // 2))
            for t in range(NT):
                at_least(pool, fin_ok, t - 3)
                pool.indirect_dma_start(yg[t % 4][:, :], None, ys_scr,
                                        bass.IndirectOffsetOnAxis(pos[:, t:t + 1].bitcast(U32), 0)).then_inc(d_yg[t % 4], 16)


def lay_out(i):
    f = lambda a: np.ascontiguousarray(a)
    wkv = i["L0_xattn_Wkv"].reshape(NH, 2, DH, C)
    bkv = i["L0_xattn_bkv"].reshape(NH, 2, DH)
    ctxT = i["ctx_768"].transpose(2, 0, 1).reshape(2, CK, B, M)
    wv = wkv[:, 1].transpose(2, 0, 1)
    bv = bkv[:, 1]

    def rows(w):
        return f(w.reshape(2, w.shape[0] // 2, w.shape[1]).transpose(1, 0, 2))

    def by_head(a):
        return a.reshape(*a.shape[:-2], 4, 4, DH).swapaxes(-3, -2)

    T = {
        "x": f(i["x"].reshape(B * L, D)),
        "cx": f(ctxT.transpose(1, 2, 0, 3)),
        "cxl": f(ctxT[:, :, :, KEYS].transpose(1, 0, 2)),
        "wk": rows(wkv[:, 0].transpose(2, 0, 1).reshape(C, D)),
        "wv": rows(wv.reshape(C, D)),
        "wvl": rows(by_head(wv).reshape(C, D)),
        "wq": rows(i["L0_xattn_Wq"].T),
        "wo": f(i["L0_xattn_Wo"].T.reshape(4, 4, DH, D).transpose(0, 2, 1, 3).reshape(64, 4, D)),
        "bk": f(bkv[:, 0].reshape(2, P).T),
        "bq": f(i["L0_xattn_bq"].reshape(2, P).T),
        "bv": f(bv.reshape(D)),
        "bvl": f(by_head(bv).reshape(D)),
        "bo": f(i["L0_xattn_bo"]),
        "ident": np.eye(P, dtype=np.float32),
        "headmask": (DH ** -0.5 * (np.arange(P)[:, None] // DH % 4 == np.arange(4)[None, :])).astype(np.float32),
    }

    def block_diagonal(w):
        h, o, n = w.shape
        m = np.zeros((h, n, h, o), w.dtype)
        m[np.arange(h), :, np.arange(h), :] = w.transpose(0, 2, 1)
        return m.reshape(h * n, h * o)

    def drive(w):
        m = block_diagonal(w).reshape(2, P, 3, P)
        return f(np.stack([m[0, :, 0], m[0, :, 1], m[1, :, 1], m[1, :, 2]], 1))

    def columns(a):
        return f(a.reshape(-1, P).T)

    fd = np.zeros((NF * P, D), np.float32)
    fd[:FI] = i["L0_attn_ffd_W"].T
    T |= {
        "gw": drive(i["L0_attn_gate_W"]),
        "cw": drive(i["L0_attn_cand_W"]),
        "ow": f(block_diagonal(i["L0_attn_out_W"]).reshape(3, P, D).transpose(1, 0, 2)),
        "braw": f(np.concatenate([columns(i["L0_attn_gate_beta_raw"]), columns(i["L0_attn_cand_beta_raw"])], 1)),
        "thr": f(np.concatenate([columns(i["L0_attn_gate_theta"]), columns(i["L0_attn_cand_theta"])], 1)),
        "gamA": columns(i["L0_attn_in_gamma"]),
        "gamB": columns(i["L0_attn_ff_gamma"]),
        "fg": rows(i["L0_attn_ffg_W"].T),
        "fu": rows(i["L0_attn_ffu_W"].T),
        "fd": f(fd.reshape(NF, P, D).transpose(1, 0, 2)),
        "rw": rows(i["L0_ffn_router_w"]),
        "rb": f(i["L0_ffn_router_b"]),
        "we": f(np.concatenate([
            i["L0_ffn_w1"].reshape(NE, 2, P, 2 * FF).transpose(0, 2, 1, 3).reshape(NE, P, 4 * FF),
            i["L0_ffn_w2"].reshape(NE, FT, P, D).transpose(0, 2, 1, 3).reshape(NE, P, FT * D)], 2)),
        "lt": np.triu(np.ones((P, P), np.float32), 1),
        "descend": np.arange(NE, 0, -1).astype(np.float32),
        "slotno": np.arange(NS).astype(np.float32),
        "altern": np.where(np.arange(NE) % 2, -1.0, 1.0).astype(np.float32),
    }
    return T


def kernel(**inputs):
    import concourse.bacc as bacc
    from concourse.bass_utils import run_bass_kernel_spmd

    arrays = lay_out({name: np.asarray(a) for name, a in inputs.items()})
    nc = bacc.Bacc("TRN2", target_bir_lowering=False, num_devices=1)
    T = {name: nc.dram_tensor(name, a.shape, mybir.dt.from_np(a.dtype), kind="ExternalInput").ap()
         for name, a in arrays.items()}
    out = nc.dram_tensor("out", (B * L, D), F32, kind="ExternalOutput").ap()
    build(nc, T, out)
    results = run_bass_kernel_spmd(nc, [arrays], core_ids=[0])
    return results.results[0]["out"].reshape(B, L, D)
```

```python
from contextlib import ExitStack

import numpy as np

import concourse.bass as bass
from concourse import mybir

F32 = mybir.dt.float32
F32R = mybir.dt.float32r
I32 = mybir.dt.int32
U32 = mybir.dt.uint32
ALU = mybir.AluOpType
ACT = mybir.ActivationFunctionType
AXX = mybir.AxisListType.X

P = 128
B, L, D = 128, 32, 256
M, C = 257, 192
CK = C // 2
MP = M + 1
KEYS = M - 1
NH, DH = 16, 16
GB = P // L
NG = B // GB
SPLIT = ((0, 0), (0, 1), (1, 0))
EPS = 1e-5
NE = 8
FI = D * 4 * 2 // 3
FF = 1024
FT = FF // P
WE = 2 * 2 * FF + FT * D
WP = 6
NS = B * L // P + NE - 1
NF = (FI + P - 1) // P
HB, HI = 32, 48
RMS_MIN = 1e-12
ROUND = 1.5 * 2 ** 23


def at_least(eng, sem, value):
    if isinstance(value, int) and value <= 0:
        return
    eng.wait_ge(sem, value)


def spread(ap, axis, n):
    v = ap.unsqueeze(axis)
    shape = list(v.shape)
    shape[axis] = n
    return v.to_broadcast(shape)


class Plan:

    def __init__(self, nc, base, end):
        self.nc, self.at, self.end = nc, base, end

    def tensor(self, name, shape, dtype=F32):
        size = int(np.prod(shape[1:])) * 4
        self.at = (self.at + 31) // 32 * 32
        t = self.nc.alloc_sbuf_tensor_at(name, list(shape), dtype, offset=self.at)
        self.at += size
        assert self.at <= self.end, (name, self.at, self.end)
        return t


def build(nc, T, out):
    ctx = ExitStack()
    with ctx:
        def sem(name):
            return ctx.enter_context(nc.semaphore(name))

        x1_scr = nc.dram_tensor("x1_scr", (B * L, D), F32, kind="Internal").ap()
        vlast_scr = nc.dram_tensor("vlast_scr", (B, D), F32, kind="Internal").ap()

        base, end = nc.sbuf_base, nc.sbuf_usable_end
        keep = Plan(nc, base, end)
        ident = keep.tensor("ident", [P, P])
        halfneg = keep.tensor("halfneg", [P, 1])
        zero = keep.tensor("zero", [P, 1])

        att = Plan(nc, keep.at, end)
        wk = att.tensor("wk", [CK, 2, D])
        wv = att.tensor("wv", [CK, 2, D])
        wvl = att.tensor("wvl", [CK, 2, D])
        wq = att.tensor("wq", [P, 2, D])
        wo = att.tensor("wo", [64, 4, D])
        bk = att.tensor("bk", [P, 2])
        bq = att.tensor("bq", [P, 2])
        bv = att.tensor("bv", [P, D])
        bvl = att.tensor("bvl", [P, D])
        bo = att.tensor("bo", [P, D])
        headmask = att.tensor("headmask", [P, 4])
        cxl = att.tensor("cxl", [CK, 2, B])
        vlast = att.tensor("vlast", [P, D])
        cx = [att.tensor(f"cx{i}", [CK, GB, 2, M]) for i in range(2)]
        vb = [att.tensor(f"vb{i}", [P, GB, 64]) for i in range(2)]
        x_in = [att.tensor(f"x_in{i}", [P, D]) for i in range(2)]
        x_res = [att.tensor(f"x_res{i}", [P, D]) for i in range(2)]
        xsum = [att.tensor(f"xsum{i}", [P, D]) for i in range(2)]
        x1o = [att.tensor(f"x1o{i}", [P, D]) for i in range(2)]
        xn = [att.tensor(f"xn{i}", [P, D]) for i in range(2)]
        xnT = [att.tensor(f"xnT{i}", [P, 2, P]) for i in range(2)]

        def parts(name, shape):
            return [att.tensor(f"{name}_{c}", shape, F32R) for c in ("hi", "lo")]

        wk_s, wv_s = parts("wk_s", [CK, 2, D]), parts("wv_s", [CK, 2, D])
        cx_s = [parts(f"cx_s{i}", [CK, 2, MP]) for i in range(2)]
        qT = [parts(f"qT{i}", [P, 2, P]) for i in range(2)]
        qbd = [parts(f"qbd{i}", [P, 2, P]) for i in range(2)]
        kT = [parts(f"kT{i}", [P, 2, MP]) for i in range(2)]
        v = [att.tensor(f"v{i}", [P, 2, D]) for i in range(2)]
        prob = [att.tensor(f"prob{i}", [P, 4, M]) for i in range(2)]
        probT = att.tensor("probT", [P, 2, 4 * P])
        negmax = [att.tensor(f"negmax{i}", [P, 4]) for i in range(2)]
        rowsum = [att.tensor(f"rowsum{i}", [P, 4]) for i in range(2)]
        rinv = [att.tensor(f"rinv{i}", [P, 4]) for i in range(2)]
        olast = [att.tensor(f"olast{i}", [P, 4, DH]) for i in range(2)]
        oraw = [att.tensor(f"oraw{i}", [P, 4, DH]) for i in range(2)]
        on = [att.tensor(f"on{i}", [P, GB, 64]) for i in range(2)]
        oT = [att.tensor(f"oT{i}", [64, 4, GB, L]) for i in range(2)]
        stats = [att.tensor(f"stats{i}", [P, 6]) for i in range(2)]
        mv = [att.tensor(f"mv{i}", [P, 2]) for i in range(2)]
        vare = [att.tensor(f"vare{i}", [P, 1]) for i in range(2)]
        rstd = [att.tensor(f"rstd{i}", [P, 1]) for i in range(2)]

        bank = [ctx.enter_context(nc.psum_tensor(f"bank{i}", [P, 512], F32)) for i in range(8)]
        kv_bank = bank[0:2]
        s_bank = bank[2:4]
        pT_bank = bank[4:6]
        o_bank = bank[6]
        x_bank = bank[7]

        d_const = sem("d_const")
        d_cx = [sem(f"d_cx{i}") for i in range(2)]
        d_vb = [sem(f"d_vb{i}") for i in range(2)]
        d_xin = [sem(f"d_xin{i}") for i in range(2)]
        d_xres = [sem(f"d_xres{i}") for i in range(2)]
        d_x1 = [sem(f"d_x1{i}") for i in range(2)]
        d_vlast = sem("d_vlast")
        vl_mm, kv_mm, s_mm, pT_mm, o_mm = (sem(n) for n in ("vl_mm", "kv_mm", "s_mm", "pT_mm", "o_mm"))
        xT_mm, q_mm, oT_mm, out_mm = (sem(n) for n in ("xT_mm", "q_mm", "oT_mm", "out_mm"))
        k_ev, p_ex, pT0_ev = (sem(n) for n in ("k_ev", "p_ex", "pT0_ev"))
        xT_ev, q_ev, oT_ev = (sem(n) for n in ("xT_ev", "q_ev", "oT_ev"))
        vl_ev, mx, v_ev, pT1_ev, o_ev, rinv_ok, xsum_ok = (
            sem(n) for n in ("vl_ev", "mx", "v_ev", "pT1_ev", "o_ev", "rinv_ok", "xsum_ok"))
        st_ok, mv_ok, xn_ok = (sem(n) for n in ("st_ok", "mv_ok", "xn_ok"))
        pad_ok, wh_ok, wl_ok, ch_ok, cl_ok, kl_ok, ql_ok = (
            sem(n) for n in ("pad_ok", "wh_ok", "wl_ok", "ch_ok", "cl_ok", "kl_ok", "ql_ok"))
        c_ok, qbd_ok, ol_ok, on_ok, x1o_ok, var_ok, rstd_ok = (
            sem(n) for n in ("c_ok", "qbd_ok", "ol_ok", "on_ok", "x1o_ok", "var_ok", "rstd_ok"))

        consts = [(ident, "ident"), (wk, "wk"), (wv, "wv"), (wvl, "wvl"), (wq, "wq"), (wo, "wo"),
                  (bk, "bk"), (bq, "bq"), (headmask, "headmask"), (cxl, "cxl")]
        rows = [(bv, "bv"), (bvl, "bvl"), (bo, "bo")]
        CONST = 16 * (len(consts) + len(rows))

        passed = {}

        def alone(eng, *waits):
            for s_, v in waits:
                at_least(eng, s_, v)
            if eng not in passed:
                passed[eng] = sem(f"passed{len(passed)}")
            eng.sem_inc(passed[eng], 1)

        def slots(eng, slot):
            slot(0, 0, True, False)
            with eng.Fori(0, NG // 2 - 1) as k:
                slot(k * 2 + 1, 1, False, False)
                slot(k * 2 + 2, 0, False, False)
            slot(NG - 1, (NG - 1) % 2, False, True)


        NT = L
        ff = Plan(nc, keep.at, end)
        xall = ff.tensor("xall", [P, NT, D])
        xm_at = ff.at
        xm = ff.tensor("xm", [P, NT, D])
        logit = ff.tensor("logit", [P, NT, NE])
        raw = ff.tensor("raw", [P, WE])
        par_size = 2 * WE * 4
        moe_at = ff.at + par_size
        wsplit = Plan(nc, ff.at, end).tensor("wsplit", [P, 2, 2, WE], F32R)
        ff.at = moe_at
        gw = [ff.tensor(f"gw{i}", [P, 4, P]) for i in range(2)]
        ow = ff.tensor("ow", [P, 3, D])
        braw = ff.tensor("braw", [P, 6])
        thr = ff.tensor("thr", [P, 6])
        beta = ff.tensor("beta", [P, 6])
        nthr = ff.tensor("nthr", [P, 6])
        ebase = ff.tensor("ebase", [P, 6])
        gam = [ff.tensor(f"gam{i}", [P, 2]) for i in range(2)]
        gam1 = [ff.tensor(f"gam1{i}", [P, 2]) for i in range(2)]
        fg = ff.tensor("fg", [P, 2, FI])
        fu = ff.tensor("fu", [P, 2, FI])
        fd = ff.tensor("fd", [P, NF, D])
        rw = ff.tensor("rw", [P, 2, NE])
        rb = ff.tensor("rb", [P, NE])
        xr = ff.tensor("xr", [P, 2, D])
        xrT = ff.tensor("xrT", [P, 2, 2, P])
        gc = [ff.tensor(f"gc{i}", [P, 6, P]) for i in range(2)]
        mem = ff.tensor("mem", [P, 6, P])
        spk = [ff.tensor(f"spk{i}", [P, 6, P]) for i in range(2)]
        zed = ff.tensor("zed", [P, 3, P])
        wed = ff.tensor("wed", [P, 3, P])
        hT = [ff.tensor(f"hT{i}", [P, 3, P]) for i in range(2)]
        xa = ff.tensor("xa", [P, 2, D])
        fn = ff.tensor("fn", [P, 2, D])
        fnT = [ff.tensor(f"fnT{i}", [P, 2, 2, P]) for i in range(2)]
        sg = [ff.tensor(f"sg{i}", [P, 2 * P]) for i in range(2)]
        fT = ff.tensor("fT", [P, NF, 2, P])
        xmt = ff.tensor("xmt", [P, 2, D])
        xmT = ff.tensor("xmT", [P, 2, 2, P])
        st = {c: [ff.tensor(f"st{c}{i}", [P, 6]) for i in range(2)] for c in "AB"}
        mv2 = {c: ff.tensor(f"mv2{c}", [P, 2, 2]) for c in "AB"}
        small = {n: ff.tensor(n, [P, 2]) for n in
                 ("veA", "rsA", "veB", "rsB", "ssA", "smA", "spA", "scA", "ssB", "smB", "spB", "scB")}

        moe = Plan(nc, moe_at + par_size, end)
        lt = moe.tensor("lt", [P, P])
        ones = moe.tensor("ones", [P, P])
        descend = moe.tensor("descend", [P, NE])
        slotno = moe.tensor("slotno", [P, NS])
        altern = moe.tensor("altern", [P, NE])
        lmax, lsum, maxp, best, posf = (moe.tensor(n, [P, NT]) for n in ("lmax", "lsum", "maxp", "best", "posf"))
        lsh, lex, oneh, rank, tot, cum, exc = (moe.tensor(n, [P, NT * NE]) for n in (
            "lsh", "lex", "oneh", "rank", "tot", "cum", "exc"))
        cnt, tlf, tiles, ctile, base_e, shift = (moe.tensor(n, [P, NE]) for n in (
            "cnt", "tlf", "tiles", "ctile", "base_e", "shift"))
        pos = moe.tensor("pos", [P, NT], I32)
        cmp7, alt7 = (moe.tensor(n, [P, NS, NE - 1]) for n in ("cmp7", "alt7"))
        expf, parf = (moe.tensor(n, [P, NS]) for n in ("expf", "parf"))
        expi, pari = (moe.tensor(n, [P, NS], I32) for n in ("expi", "pari"))
        endi = moe.tensor("endi", [P, NE], I32)
        assert moe.at <= end
        moe = Plan(nc, xm_at, xm_at + NT * D * 4)
        xs = [moe.tensor(f"xs{i}", [P, D]) for i in range(2)]
        xsT = [[moe.tensor(f"xsT{i}{c}", [P, 2, P], F32R) for c in ("hi", "lo")] for i in range(2)]
        sa = [moe.tensor(f"sa{i}", [P, 512]) for i in range(2)]
        hid = [moe.tensor(f"hid{i}", [P, 512]) for i in range(2)]
        hidT = [[moe.tensor(f"hidT{i}{c}", [P, 4, P], F32R) for c in ("hi", "lo")] for i in range(2)]
        ys = [moe.tensor(f"ys{i}", [P, D]) for i in range(2)]
        yg = [moe.tensor(f"yg{i}", [P, D]) for i in range(4)]
        xs_scr = nc.dram_tensor("xs_scr", (NS * P, D), F32, kind="Internal").ap()
        ys_scr = nc.dram_tensor("ys_scr", (NS * P, D), F32, kind="Internal").ap()
        a_bank, g_bank = bank[0:2], bank[2:4]
        hT_bank = bank[4:6]
        xs_bank, y_bank = bank[6], bank[7]

        d_zero, d_mc, d_w = sem("d_zero"), sem("d_mc"), sem("d_w")
        z_ok, w_ready, d_sort = sem("z_ok"), sem("w_ready"), sem("d_sort")
        w0_ok, d_we = sem("w0_ok"), [sem(f"d_we{i}") for i in range(WP)]
        whi_ok, wlo_ok, xsTl_ok, hTl_ok = (sem(n) for n in ("whi_ok", "wlo_ok", "xsTl_ok", "hTl_ok"))
        PIECES = [slice(c * WE // WP, (c + 1) * WE // WP) for c in range(WP)]
        WC = WE // (NT // 2 - 4)
        d_xs, d_ys = [sem(f"d_xs{i}") for i in range(2)], [sem(f"d_ys{i}") for i in range(2)]
        d_yg = [sem(f"d_yg{i}") for i in range(4)]
        route_ok, lsh_ok, lex_ok, oneh_ok, rank_mm, pos_ok, tab_ok = (sem(n) for n in (
            "route_ok", "lsh_ok", "lex_ok", "oneh_ok", "rank_mm", "pos_ok", "tab_ok"))
        xsT_mm, xsT_ev, ag_mm, sa_ok, hid_ok, hT_mm, hT_ev, y_mm, y_ok, fin_ok = (sem(n) for n in (
            "xsT_mm", "xsT_ev", "ag_mm", "sa_ok", "hid_ok", "hT_mm", "hT_ev", "y_mm", "y_ok", "fin_ok"))
        d_out = sem("d_out")
        moec = [(lt, "lt")]
        moer = [(descend, "descend"), (slotno, "slotno"), (altern, "altern")]
        MOEC = 16 * (len(moec) + len(moer))

        def tiles_of_experts(eng, step):
            step(0, 0, True, False)
            with eng.Fori(0, (NS - 3) // 2) as k:
                step(k * 2 + 1, 1, False, False)
                step(k * 2 + 2, 0, False, False)
            step(NS - 2, (NS - 2) % 2, False, False)
            step(NS - 1, (NS - 1) % 2, False, True)

        gc_bank = bank[0:2]
        t_bank = bank[2]
        r_bank = bank[3]
        gu_bank = bank[4:7]
        fd_bank = bank[7]

        d_ff, d_x = sem("d_ff"), sem("d_x")
        c2, be_ok = sem("c2"), sem("be_ok")
        stA_ok, mvA_ok, veA_ok, rsA_ok, xl_ok, ssA_ok, smA_ok, spA_ok, scA_ok, xr_ok = (sem(n) for n in (
            "stA_ok", "mvA_ok", "veA_ok", "rsA_ok", "xl_ok", "ssA_ok", "smA_ok", "spA_ok", "scA_ok", "xr_ok"))
        xrT_mm, xrT_ev, gc_mm, gc_ev, pot_ok, rnd_ok, spk_ok, mem_ok = (sem(n) for n in (
            "xrT_mm", "xrT_ev", "gc_mm", "gc_ev", "pot_ok", "rnd_ok", "spk_ok", "mem_ok"))
        zw_ok, zc_ok, h_ok, gru_mm, xa_ok, add_ok = (sem(n) for n in (
            "zw_ok", "zc_ok", "h_ok", "gru_mm", "xa_ok", "add_ok"))
        ssB_ok, smB_ok, spB_ok, scB_ok, fn_ok, fnT_mm, fnT_ev = (sem(n) for n in (
            "ssB_ok", "smB_ok", "spB_ok", "scB_ok", "fn_ok", "fnT_mm", "fnT_ev"))
        gu_mm, silu_ok, prod_ok, fd_mm, x2_ok = (sem(n) for n in ("gu_mm", "silu_ok", "prod_ok", "fd_mm", "x2_ok"))
        stB_ok, mvB_ok, veB_ok, rsB_ok, xm_ok, xmT_mm, xmT_ev, rt_mm, rt_ok = (sem(n) for n in (
            "stB_ok", "mvB_ok", "veB_ok", "rsB_ok", "xm_ok", "xmT_mm", "xmT_ev", "rt_mm", "rt_ok"))
        dv_chain = sem("dv_chain")
        xm_kept = sem("xm_kept")

        ffw = [(gw[0], "gw"), (gw[1], "cw"), (ow, "ow"), (braw, "braw"), (thr, "thr"), (gam[0], "gamA"),
               (gam[1], "gamB"), (fg, "fg"), (fu, "fu"), (fd, "fd"), (rw, "rw")]
        FFW = 16 * (len(ffw) + 1)
        FW = [min(P, FI - P * f) for f in range(NF)]

        NQ = NT // 2

        def turns(eng, turn):
            turn(-3, 1, "m")
            turn(-2, 0, "nm")
            turn(-1, 1, "onm")
            turn(0, 0, "fonm")
            with eng.Fori(0, (NQ - 4) // 2) as k:
                turn(k * 2 + 1, 1, "fonmr")
                turn(k * 2 + 2, 0, "fonmr")
            turn(NQ - 3, 1, "fonr")
            turn(NQ - 2, 0, "for")
            turn(NQ - 1, 1, "fr")
            turn(NQ, 0, "r")

        block = ctx.enter_context(nc.Block())

        @block.sync
        def _(sp):
            def ln_row(g):
                return T["x"][bass.ds(g * P, P), :]

            def load_cx(g, s):
                sp.dma_start(cx[s][:, :, :, :], T["cx"][:, bass.ds(g * GB, GB), :, :]).then_inc(d_cx[s], 16)

            def load_vb(g, s):
                for j in range(4):
                    src = vlast_scr[bass.ds(g * GB, GB), 64 * j:64 * j + 64].partition_broadcast(L)
                    sp.dma_start(vb[s][32 * j:32 * j + 32, :, :], src).then_inc(d_vb[s], 16)

            for t, name in consts:
                full = tuple(slice(None) for _ in t.shape)
                sp.dma_start(t[full], T[name]).then_inc(d_const, 16)
            sp.wait_ge(z_ok, 1)
            sp.dma_start(xs_scr.rearrange("(s p) d -> p s d", p=P), spread(x1o[0][:, :], 1, NS)).then_inc(d_zero, 16)
            for t, name in rows:
                sp.dma_start(t[:, :], T[name].partition_broadcast(P)).then_inc(d_const, 16)
            for g in range(2):
                sp.dma_start(x_in[g][:, :], ln_row(g)).then_inc(d_xin[g], 16)
            load_cx(0, 0)
            load_cx(1, 1)
            sp.wait_ge(vl_ev, 1)
            sp.dma_start(vlast_scr, vlast[:, :]).then_inc(d_vlast, 16)
            sp.wait_ge(d_vlast, 16)
            load_vb(0, 0)

            def slot(g, s, first, last):
                if not last:
                    at_least(sp, ol_ok, GB * g)
                    load_vb(g + 1, 1 - s)
                if isinstance(g, int) and g + 2 >= NG:
                    pass
                elif not last:
                    sp.wait_ge(xn_ok, g + 1)
                    sp.dma_start(x_in[s][:, :], ln_row(g + 2)).then_inc(d_xin[s], 16)
                at_least(sp, xsum_ok, g - 1)
                sp.dma_start(x_res[s][:, :], ln_row(g)).then_inc(d_xres[s], 16)
                if not (isinstance(g, int) and g + 2 >= NG):
                    sp.wait_ge(cl_ok, GB * g + GB)
                    load_cx(g + 2, s)
                if not first:
                    store_x1(g - 1, 1 - s)

            def store_x1(g, s):
                sp.wait_ge(x1o_ok, g + 1)
                sp.dma_start(x1_scr[bass.ds(g * P, P), :], x1o[s][:, :]).then_inc(d_x1[s], 16)

            slot(0, 0, True, False)
            with sp.Fori(0, NG // 2 - 2) as k:
                slot(k * 2 + 1, 1, False, False)
                slot(k * 2 + 2, 0, False, False)
            slot(NG - 3, 1, False, False)
            slot(NG - 2, 0, False, False)
            slot(NG - 1, 1, False, True)
            store_x1(NG - 1, 1)
            sp.wait_ge(d_x1[0], 16 * NG // 2)
            sp.wait_ge(d_x1[1], 16 * NG // 2)

            sp.wait_ge(out_mm, NG)
            sp.wait_ge(x1o_ok, NG)
            for t, name in ffw:
                full = tuple(slice(None) for _ in t.shape)
                sp.dma_start(t[full], T[name]).then_inc(d_ff, 16)
            sp.dma_start(rb[:, :], T["rb"].partition_broadcast(P)).then_inc(d_ff, 16)
            sp.dma_start(xall[:, :, :], x1_scr.rearrange("(b t) d -> b t d", b=B)).then_inc(d_x, 16)
            sp.dma_start(raw[:, :], T["we"][0, :, :]).then_inc(d_w, 16)
            sp.wait_ge(xm_kept, NQ)
            sp.wait_ge(rt_ok, NQ)
            for t, name in moec:
                sp.dma_start(t[:, :], T[name]).then_inc(d_mc, 16)
            for t, name in moer:
                sp.dma_start(t[:, :], T[name].partition_broadcast(P)).then_inc(d_mc, 16)

            def load_xs(sl, i):
                sp.dma_start(xs[i][:, :], xs_scr[bass.ds(sl * P, P), :]).then_inc(d_xs[i], 16)

            sp.wait_ge(d_sort, 16 * NT)
            load_xs(0, 0)
            load_xs(1, 1)

            def sstep(sl, i, first, last):
                if not (isinstance(sl, int) and sl + 2 >= NS):
                    sp.wait_ge(xsT_mm, sl + 1)
                    load_xs(sl + 2, i)
                sp.wait_ge(y_ok, sl + 1)
                sp.dma_start(ys_scr[bass.ds(sl * P, P), :], ys[i][:, :]).then_inc(d_ys[i], 16)

            tiles_of_experts(sp, sstep)
            for c in range(4):
                sp.wait_ge(fin_ok, 8 * (c + 1))
                sp.dma_start(out.rearrange("(b t) d -> b t d", b=B)[:, 8 * c:8 * c + 8, :],
                             xall[:, 8 * c:8 * c + 8, :]).then_inc(d_out, 16)
            sp.wait_ge(d_out, 64)
            sp.wait_ge(d_zero, 16)

        @block.tensor
        def _(pe):
            def k_half(b, bs, half):
                if half == 0:
                    pe.wait_ge(cl_ok, b + 1)
                    at_least(pe, kl_ok, 2 * b)
                else:
                    at_least(pe, v_ev, b)
                dst = kv_bank[(b_par(bs) + half) % 2]
                for n, (x, w) in enumerate(SPLIT):
                    for k in range(2):
                        last = pe.matmul(dst[:, 0:MP], wk_s[w][:, k, half * P:half * P + P], cx_s[bs][x][:, k, :],
                                         start=(n + k == 0), stop=(n + k == 3))
                last.then_inc(kv_mm, 1)

            def b_par(bs):
                return (3 * bs) % 2

            def v_unit(b, bs):
                at_least(pe, kl_ok, 2 * b + 1)
                dst = kv_bank[b_par(bs)]
                for t in range(2):
                    for n, (x, w) in enumerate(SPLIT):
                        for k in range(2):
                            last = pe.matmul(dst[:, t * D:t * D + D], cx_s[bs][x][:, k, t * P:t * P + P],
                                             wv_s[w][:, k, :], start=(n + k == 0), stop=(n + k == 3))
                last.then_inc(kv_mm, 1)

            def scores(b, bs, gr):
                if gr == 0:
                    pe.wait_ge(qbd_ok, b + 1)
                if gr % 2 == 0:
                    pe.wait_ge(kl_ok, 2 * b + gr // 2 + 1)
                at_least(pe, p_ex, 4 * b + gr - 1)
                r = slice(64 * (gr % 2), 64 * (gr % 2) + 64)
                for n, (x, w) in enumerate(SPLIT):
                    ins = pe.matmul(s_bank[gr % 2][:, 0:MP], qbd[bs][x][r, gr // 2, :], kT[bs][w][r, gr // 2, :],
                                    start=(n == 0), stop=(n == 2))
                ins.then_inc(s_mm, 1)

            def prob_transpose(b, bs):
                pe.wait_ge(p_ex, 4 * b + 4)
                for t in range(2):
                    at_least(pe, (pT0_ev, pT1_ev)[t], b)
                    for gr in range(4):
                        last = pe.transpose(pT_bank[t][:, gr * P:gr * P + P],
                                            prob[bs][:, gr, t * P:t * P + P], ident[:, :])
                    last.then_inc(pT_mm, 1)

            def attend(b, bs):
                pe.wait_ge(pT0_ev, b + 1)
                pe.wait_ge(pT1_ev, b + 1)
                pe.wait_ge(v_ev, b + 1)
                at_least(pe, o_ev, b)
                for gr in range(4):
                    for t in range(2):
                        last = pe.matmul(o_bank[:, gr * 64:gr * 64 + 64], probT[:, t, gr * P:gr * P + P],
                                         v[bs][:, t, gr * 64:gr * 64 + 64], start=(t == 0), stop=(t == 1))
                last.then_inc(o_mm, 1)

            def x_transpose(g, s):
                pe.wait_ge(xn_ok, g + 1)
                at_least(pe, xsum_ok, g - 2)
                for k in range(2):
                    last = pe.transpose(x_bank[:, k * P:k * P + P], xn[s][:, k * P:k * P + P], ident[:, :])
                last.then_inc(xT_mm, 1)

            def o_transpose(g, s):
                for u in range(GB):
                    last = pe.transpose(x_bank[0:64, u * P:u * P + P], on[s][:, u, :], ident[:, :])
                last.then_inc(oT_mm, 1)

            def q_project(g, s):
                pe.wait_ge(xT_ev, g + 1)
                for half in range(2):
                    for k in range(2):
                        last = pe.matmul(x_bank[:, half * P:half * P + P], wq[:, k, half * P:half * P + P],
                                         xnT[s][:, k, :], start=(k == 0), stop=(k == 1))
                last.then_inc(q_mm, 1)

            def o_project(g, s):
                pe.wait_ge(oT_ev, g + 1)
                for j in range(4):
                    last = pe.matmul(x_bank[:, 0:D], oT[s][:, j, :, :], wo[:, j, :], start=(j == 0), stop=(j == 3))
                last.then_inc(out_mm, 1)

            pe.wait_ge(d_const, CONST)
            for k in range(2):
                last = pe.matmul(x_bank[:, 0:D], cxl[:, k, :], wvl[:, k, :], start=(k == 0), stop=(k == 1))
            last.then_inc(vl_mm, 1)
            pe.wait_ge(vl_ev, 1)
            x_transpose(0, 0)
            pe.wait_ge(pad_ok, 4)
            pe.wait_ge(wl_ok, 2)
            k_half(0, 0, 0)
            k_half(0, 0, 1)
            v_unit(0, 0)
            q_project(0, 0)

            def slot(g, s, first, last):
                for u in range(GB):
                    b = g * GB + u
                    nxt = not (last and u == GB - 1)
                    bs, bs1 = u % 2, (u + 1) % 2
                    if nxt:
                        k_half(b + 1, bs1, 0)
                    scores(b, bs, 0)
                    scores(b, bs, 1)
                    if not (first and u == 0):
                        attend(b - 1, bs1)
                    scores(b, bs, 2)
                    scores(b, bs, 3)
                    if nxt:
                        k_half(b + 1, bs1, 1)
                        v_unit(b + 1, bs1)
                    prob_transpose(b, bs)
                    if u == 0 and not last:
                        x_transpose(g + 1, 1 - s)
                    if u == 1 and not first:
                        alone(pe, (xT_ev, 0 if last else g + 2), (on_ok, GB * g))
                        o_transpose(g - 1, 1 - s)
                    if u == 2 and not last:
                        if not first:
                            pe.wait_ge(oT_ev, g)
                        q_project(g + 1, 1 - s)
                    if u == 3 and not first:
                        if not last:
                            pe.wait_ge(ql_ok, g + 2)
                        o_project(g - 1, 1 - s)

            slots(pe, slot)
            attend(B - 1, (B - 1) % 2)
            pe.wait_ge(xsum_ok, NG - 1)
            pe.wait_ge(on_ok, B)
            o_transpose(NG - 1, (NG - 1) % 2)
            o_project(NG - 1, (NG - 1) % 2)

            pe.wait_ge(d_ff, FFW)

            def transposes(src, done):
                for k in range(2):
                    for i in range(2):
                        c = (2 * k + i) * P
                        ins = pe.transpose(t_bank[:, c:c + P], src[:, i, k * P:k * P + P], ident[:, :])
                ins.then_inc(done, 1)

            def drives(t, i):
                at_least(pe, gc_ev, t)
                for w in range(2):
                    for c, (m, k) in enumerate(((0, 0), (1, 0), (1, 1), (2, 1))):
                        ins = pe.matmul(gc_bank[w][:, m * P:m * P + P], gw[w][:, c, :], xrT[:, k, i, :],
                                        start=(c in (0, 1, 3)), stop=(c in (0, 2, 3)))
                ins.then_inc(gc_mm, 1)

            def unit_out(Q):
                pe.wait_ge(h_ok, Q * 2 + 2)
                for i in range(2):
                    for m, a, b in ((1, 0, 2), (0, 0, 1), (2, 1, 2)):
                        ins = pe.matmul(r_bank[:, i * D + a * P:i * D + b * P], hT[i][:, m, :], ow[:, m, a * P:b * P],
                                        start=(m == 1), stop=(m == 2))
                ins.then_inc(gru_mm, 1)

            def route(Q):
                pe.wait_ge(xmT_ev, Q + 1)
                for i in range(2):
                    for k in range(2):
                        ins = pe.matmul(r_bank[:, i * NE:i * NE + NE], xmT[:, k, i, :], rw[:, k, :],
                                        start=(k == 0), stop=(k == 1))
                ins.then_inc(rt_mm, 1)

            def gate_up(q, par, f):
                if f == 0:
                    pe.wait_ge(fnT_ev, q + 1)
                at_least(pe, prod_ok, NF * q + f - 2)
                for h, w in enumerate((fg, fu)):
                    for k in range(2):
                        ins = pe.matmul(gu_bank[f % 3][0:FW[f], h * 2 * P:(h + 1) * 2 * P],
                                        w[:, k, f * P:f * P + FW[f]], fnT[par][:, k, :, :],
                                        start=(k == 0), stop=(k == 1))
                ins.then_inc(gu_mm, 1)

            def down(q):
                pe.wait_ge(prod_ok, NF * q + NF - 1)
                at_least(pe, x2_ok, q)
                for i in range(2):
                    for f in range(NF):
                        if i == 0 and f == NF - 1:
                            pe.wait_ge(prod_ok, NF * q + NF)
                        ins = pe.matmul(fd_bank[:, i * D:i * D + D], fT[0:FW[f], f, i, :], fd[0:FW[f], f, :],
                                        start=(f == 0), stop=(f == NF - 1))
                ins.then_inc(fd_mm, 1)

            def turn(q, par, parts):
                f, o, n, r = (c in parts for c in "fonr")
                if n:
                    pe.wait_ge(xr_ok, q * 2 + 6)
                    at_least(pe, xrT_ev, q + 2)
                    at_least(pe, fnT_ev, q + 1)
                    transposes(xr, xrT_mm)
                if f:
                    gate_up(q, par, 0)
                if o:
                    at_least(pe, rt_ok, q - 1)
                    at_least(pe, xa_ok, q + 1)
                    unit_out(q + 1)
                if n:
                    pe.wait_ge(xrT_ev, q + 3)
                    drives(q * 2 + 4, 0)
                if f:
                    gate_up(q, par, 1)
                if r:
                    pe.wait_ge(xm_ok, q * 2)
                    if n:
                        pe.wait_ge(xrT_ev, q + 3)
                    else:
                        pe.wait_ge(fnT_ev, min(q + 1, NQ))
                        pe.wait_ge(xmT_ev, q - 1)
                    transposes(xmt, xmT_mm)
                if f:
                    gate_up(q, par, 2)
                if n:
                    drives(q * 2 + 5, 1)
                if r:
                    if o:
                        pe.wait_ge(xa_ok, q + 2)
                    else:
                        pe.wait_ge(rt_ok, q - 1)
                    route(q - 1)
                if f:
                    gate_up(q, par, 3)
                if o:
                    pe.wait_ge(fn_ok, q * 2 + 4)
                    if r:
                        pe.wait_ge(xmT_ev, q)
                    else:
                        pe.wait_ge(xrT_ev, q + 3)
                    transposes(fn, fnT_mm)
                if f:
                    gate_up(q, par, 4)
                    gate_up(q, par, 5)
                    down(q)

            turns(pe, turn)

            pe.wait_ge(d_mc, MOEC)
            pe.wait_ge(route_ok, 1)
            pe.wait_ge(oneh_ok, 1)
            pe.matmul(bank[4][:, 0:NT * NE], lt[:, :], oneh[:, :], start=True, stop=True)
            pe.matmul(bank[5][:, 0:NT * NE], ones[:, :], oneh[:, :], start=True, stop=True).then_inc(rank_mm, 1)
            pe.wait_ge(tab_ok, 3)

            def xs_transpose(sl, i):
                pe.wait_ge(d_xs[i], (sl - i) * 8 + 16)
                at_least(pe, xsTl_ok, sl)
                for k in range(2):
                    ins = pe.transpose(xs_bank[:, k * P:k * P + P], xs[i][:, k * P:k * P + P], ident[:, :])
                ins.then_inc(xsT_mm, 1)

            def hidden(sl, i, half, par):
                at_least(pe, hid_ok, 2 * sl + half - 1)
                for b_, o in ((a_bank, 0), (g_bank, FF)):
                    for n, (x, w) in enumerate(SPLIT):
                        for k in range(2):
                            c = k * 2 * FF + o + half * 512
                            ins = pe.matmul(b_[half][:, :], xsT[i][x][:, k, :],
                                            wsplit[:, bass.ds(par, 1), w, c:c + 512],
                                            start=(n + k == 0), stop=(n + k == 3))
                ins.then_inc(ag_mm, 1)

            def hid_transpose(sl, half):
                pe.wait_ge(hid_ok, 2 * sl + half + 1)
                at_least(pe, hTl_ok, 2 * sl + half - 1)
                for f in range(4):
                    ins = pe.transpose(hT_bank[half][:, f * P:f * P + P], hid[half][:, f * P:f * P + P], ident[:, :])
                ins.then_inc(hT_mm, 1)

            def expert_down(sl, par):
                at_least(pe, y_ok, sl)
                pe.wait_ge(hTl_ok, 2 * sl + 2)
                for n, (x, w) in enumerate(SPLIT):
                    for f in range(FT):
                        c = 4 * FF + f * D
                        ins = pe.matmul(y_bank[:, 0:D], hidT[f // 4][x][:, f % 4, :],
                                        wsplit[:, bass.ds(par, 1), w, c:c + D],
                                        start=(n == 0 and f == 0), stop=(n == 2 and f == FT - 1))
                ins.then_inc(y_mm, 1)

            def parity(sl):
                return pe.value_load(pari[0:1, bass.ds(sl, 1)], min_val=0, max_val=1)

            pe.sem_inc(y_mm, 1)
            xs_transpose(0, 0)

            def estep(sl, i, first, last):
                e = pe.value_load(expi[0:1, bass.ds(sl, 1)], min_val=0, max_val=NE - 1)
                par = parity(sl)
                pe.wait_ge(w_ready, e + 1)
                pe.wait_ge(xsTl_ok, sl + 1)
                hidden(sl, i, 0, par)
                if not first:
                    hid_transpose(sl - 1, 1)
                hidden(sl, i, 1, par)
                if not last:
                    xs_transpose(sl + 1, 1 - i)
                if not first:
                    expert_down(sl - 1, parity(sl - 1))
                hid_transpose(sl, 0)

            tiles_of_experts(pe, estep)
            hid_transpose(NS - 1, 1)
            expert_down(NS - 1, parity(NS - 1))

        @block.scalar
        def _(act):
            def k_copy(b, bs, half):
                act.wait_ge(kv_mm, 3 * b + half + 1)
                src = kv_bank[((3 * bs) % 2 + half) % 2]
                act.activation(kT[bs][0][:, half, :], src[:, 0:MP], ACT.Identity,
                               bias=bk[:, half:half + 1]).then_inc(k_ev, 1)

            def exp(b, bs, gr):
                if gr == 0:
                    at_least(act, ol_ok, b - 1)
                    at_least(act, rinv_ok, b - 1)
                act.wait_ge(mx, 4 * b + gr + 1)
                act.activation(prob[bs][:, gr, :], s_bank[gr % 2][:, 0:M], ACT.Exp, bias=negmax[bs][:, gr:gr + 1],
                               accum_out=rowsum[bs][:, gr:gr + 1]).then_inc(p_ex, 1)

            def ctx_high(b, G, s, u, bs):
                if u == 0:
                    act.wait_ge(d_cx[s], (G - s) * 8 + 16)
                at_least(act, kv_mm, 3 * (b - 1))
                act.activation(cx_s[bs][0][:, :, 0:M], cx[s][:, u, :, :], ACT.Identity).then_inc(ch_ok, 1)

            act.wait_ge(d_const, CONST)
            for w, w_s in ((wk, wk_s), (wv, wv_s)):
                act.activation(w_s[0][:, :, :], w[:, :, :], ACT.Identity).then_inc(wh_ok, 1)
            ctx_high(0, 0, 0, 0, 0)
            ctx_high(1, 0, 0, 1, 1)
            act.wait_ge(xT_mm, 1)
            act.activation(xnT[0][:, :, :], x_bank[:, 0:2 * P].rearrange("p (k t) -> p k t", k=2),
                           ACT.Identity).then_inc(xT_ev, 1)
            k_copy(0, 0, 0)
            k_copy(0, 0, 1)

            def q_copy(g, s):
                act.wait_ge(q_mm, g + 1)
                at_least(act, qbd_ok, GB * (g - 1))
                for half in range(2):
                    ins = act.activation(qT[s][0][:, half, :], x_bank[:, half * P:half * P + P], ACT.Identity,
                                         bias=bq[:, half:half + 1])
                ins.then_inc(q_ev, 1)

            q_copy(0, 0)

            def slot(g, s, first, last):
                for u in range(GB):
                    b = g * GB + u
                    nxt = not (last and u == GB - 1)
                    bs, bs1 = u % 2, (u + 1) % 2
                    if nxt:
                        k_copy(b + 1, bs1, 0)
                    exp(b, bs, 0)
                    exp(b, bs, 1)
                    if not (last and u >= 2):
                        ctx_high(b + 2, g + u // 2, s if u < 2 else 1 - s, (u + 2) % GB, bs)
                    exp(b, bs, 2)
                    exp(b, bs, 3)
                    if nxt:
                        k_copy(b + 1, bs1, 1)
                    act.wait_ge(pT_mm, 2 * b + 1)
                    at_least(act, o_mm, b)
                    act.activation(probT[:, 0, :], pT_bank[0][:, :], ACT.Identity).then_inc(pT0_ev, 1)
                    if u == 0 and not last:
                        act.wait_ge(xT_mm, g + 2)
                        act.activation(xnT[1 - s][:, :, :], x_bank[:, 0:2 * P].rearrange("p (k t) -> p k t", k=2),
                                       ACT.Identity).then_inc(xT_ev, 1)
                    if u == 1 and not first:
                        o_copy(g - 1, 1 - s)
                    if u == 2 and not last:
                        q_copy(g + 1, 1 - s)

            def o_copy(g, s):
                act.wait_ge(oT_mm, g + 1)
                act.activation(oT[s][:, :, :, :].rearrange("p j u l -> p u j l"),
                               x_bank[0:64, :].rearrange("p (u j l) -> p u j l", u=GB, j=4),
                               ACT.Identity).then_inc(oT_ev, 1)

            slots(act, slot)
            o_copy(NG - 1, (NG - 1) % 2)

            act.wait_ge(d_ff, FFW)
            act.wait_ge(be_ok, 3)

            def square_sum(c, i, dst, src, need, Q, free, taken, done):
                alone(act, (need, Q * 2 + i + 1 if c == "A" else Q + 1), (free, Q), (taken, Q))
                act.activation(dst[:, i, :], src, ACT.Square,
                               accum_out=small["ss" + c][:, i:i + 1]).then_inc(done, 1)

            def scaled(dst, i, src, col, need, Q, done):
                alone(act, (need, Q + 1))
                act.activation(dst[:, i, :], src, ACT.Identity, scale=col[:, i:i + 1]).then_inc(done, 1)

            def gamma_copy(dst, g, mm, Q, done):
                act.wait_ge(mm, Q + 1)
                for k in range(2):
                    ins = act.activation(dst[:, k, :, :], t_bank[:, 2 * k * P:2 * (k + 1) * P].rearrange(
                        "p (i b) -> p i b", i=2), ACT.Identity, scale=gam1[g][:, k:k + 1])
                ins.then_inc(done, 1)

            def silu(q, f):
                act.wait_ge(gu_mm, NF * q + f + 1)
                at_least(act, prod_ok, NF * q + f - 1)
                act.activation(sg[f % 2][0:FW[f], :], gu_bank[f % 3][0:FW[f], 0:2 * P], ACT.Silu).then_inc(silu_ok, 1)

            def drive_copy(t, i):
                act.wait_ge(gc_mm, t + 1)
                at_least(act, pot_ok, t - 1)
                for w in range(2):
                    ins = act.activation(gc[i][:, 3 * w:3 * w + 3, :],
                                         gc_bank[w][:, 0:3 * P].rearrange("p (m b) -> p m b", m=3), ACT.Identity)
                ins.then_inc(gc_ev, 1)

            def route_copy(Q):
                act.wait_ge(xmT_mm, Q + 1)
                at_least(act, rt_mm, Q)
                act.activation(xmT[:, :, :, :], t_bank[:, :].rearrange("p (k i b) -> p k i b", k=2, i=2),
                               ACT.Identity).then_inc(xmT_ev, 1)

            def turn(q, par, parts):
                f, o, n, m, r = (c in parts for c in "fonmr")
                if n:
                    at_least(act, gc_mm, q * 2 + 4)
                    gamma_copy(xrT, 0, xrT_mm, q + 2, xrT_ev)
                if f:
                    silu(q, 0)
                if o:
                    for i in range(2):
                        square_sum("B", i, fn, xa[:, i, :], xa_ok, q + 1, smB_ok, fnT_mm, ssB_ok)
                if n:
                    drive_copy(q * 2 + 4, 0)
                if f:
                    silu(q, 1)
                if o:
                    for i in range(2):
                        scaled(fn, i, xa[:, i, :], small["scB"], scB_ok, q + 1, fn_ok)
                if r:
                    route_copy(q - 1)
                if f:
                    silu(q, 2)
                if n:
                    drive_copy(q * 2 + 5, 1)
                if m:
                    for i in range(2):
                        square_sum("A", i, xr, xm[:, q * 2 + 6 + i, :], xl_ok, q + 3, smA_ok, xrT_mm, ssA_ok)
                if f:
                    silu(q, 3)
                if o:
                    at_least(act, gu_mm, NF * q)
                    gamma_copy(fnT[1 - par], 1, fnT_mm, q + 1, fnT_ev)
                if m:
                    for i in range(2):
                        scaled(xr, i, xm[:, q * 2 + 6 + i, :], small["scA"], scA_ok, q + 3, xr_ok)
                if f:
                    silu(q, 4)
                    silu(q, 5)
                if parts == "fonmr":
                    act.activation(wsplit[:, 0, 0, bass.ds((q - 1) * WC, WC)], raw[:, bass.ds((q - 1) * WC, WC)],
                                   ACT.Identity).then_inc(w0_ok, 1)

            act.wait_ge(d_w, 16)
            turns(act, turn)

            act.wait_ge(lsh_ok, 1)
            act.activation(lex[:, :], lsh[:, :], ACT.Exp).then_inc(lex_ok, 1)

            def astep(sl, i, first, last):
                silu_half(sl, 0)
                if not first:
                    hT_high(sl - 1, 1)
                silu_half(sl, 1)
                if not last:
                    xs_high(sl + 1, 1 - i)
                hT_high(sl, 0)

            def silu_half(sl, half):
                act.wait_ge(ag_mm, 2 * sl + half + 1)
                at_least(act, hid_ok, 2 * sl + half - 1)
                act.activation(sa[half][:, :], a_bank[half][:, :], ACT.Silu).then_inc(sa_ok, 1)

            def hT_high(sl, half):
                act.wait_ge(hT_mm, 2 * sl + half + 1)
                act.wait_ge(y_mm, sl + 1)
                act.activation(hidT[half][0][:, :, :], hT_bank[half][:, :].rearrange("p (f b) -> p f b", f=4),
                               ACT.Identity).then_inc(hT_ev, 1)

            def xs_high(sl, i):
                act.wait_ge(xsT_mm, sl + 1)
                at_least(act, ag_mm, 2 * (sl - 1))
                act.activation(xsT[i][0][:, :, :], xs_bank[:, 0:2 * P].rearrange("p (k b) -> p k b", k=2),
                               ACT.Identity).then_inc(xsT_ev, 1)

            xs_high(0, 0)
            tiles_of_experts(act, astep)
            hT_high(NS - 1, 1)

        @block.vector
        def _(dve):
            def norm_stats(g, s):
                dve.wait_ge(d_xin[s], loads(g, s))
                at_least(dve, mv_ok, g - 1)
                dve.bn_stats(stats[s][:, :], x_in[s][:, :]).then_inc(st_ok, 1)
                alone(dve, (st_ok, g + 1))
                dve.bn_aggr(mv[s][:, :], stats[s][:, :]).then_inc(mv_ok, 1)

            def loads(g, s):
                return (g - s) * 8 + 16

            def norm_apply(g, s):
                dve.wait_ge(rstd_ok, g + 1)
                at_least(dve, xT_mm, g - 1)
                dve.tensor_scalar(xn[s][:, :], x_in[s][:, :], mv[s][:, 0:1], rstd[s][:, 0:1],
                                  ALU.subtract, ALU.mult).then_inc(xn_ok, 1)

            def v_copy(b, bs):
                dve.wait_ge(kv_mm, 3 * b + 3)
                dve.tensor_tensor(v[bs][:, :, :], kv_bank[(3 * bs) % 2][:, :].rearrange("p (t n) -> p t n", t=2),
                                  spread(bv[:, :], 1, 2), ALU.add).then_inc(v_ev, 1)

            def k_low(b, bs, half):
                dve.wait_ge(k_ev, 2 * b + half + 1)
                dve.scalar_tensor_tensor(kT[bs][1][:, half, :], kv_bank[((3 * bs) % 2 + half) % 2][:, 0:MP],
                                         bk[:, half:half + 1], kT[bs][0][:, half, :].bitcast(F32),
                                         ALU.add, ALU.subtract).then_inc(kl_ok, 1)

            def q_low(g, s):
                dve.wait_ge(q_ev, g + 1)
                for half in range(2):
                    ins = dve.scalar_tensor_tensor(qT[s][1][:, half, :], x_bank[:, half * P:half * P + P],
                                                   bq[:, half:half + 1], qT[s][0][:, half, :].bitcast(F32),
                                                   ALU.add, ALU.subtract)
                ins.then_inc(ql_ok, 1)

            def take_out(b, bs):
                dve.wait_ge(p_ex, 4 * b + 4)
                at_least(dve, on_ok, b - 1)
                dve.reciprocal(rinv[bs][:, :], rowsum[bs][:, :]).then_inc(rinv_ok, 1)
                dve.wait_ge(o_mm, b + 1)
                dve.wait_ge(ol_ok, b + 1)
                for j in range(4):
                    q = slice(32 * j, 32 * j + 32)
                    ins = dve.tensor_tensor(
                        oraw[bs][q, :, :], o_bank[q, 0:D].rearrange("p (g n) -> p g n", g=4)[:, :, 16 * j:16 * j + 16],
                        olast[bs][q, :, :], ALU.add)
                ins.then_inc(o_ev, 1)

            def out_sum(g, s):
                dve.wait_ge(out_mm, g + 1)
                dve.wait_ge(d_xres[s], loads(g, s))
                at_least(dve, x1o_ok, g)
                dve.tensor_tensor(xsum[s][:, :], x_bank[:, 0:D], x_res[s][:, :], ALU.add).then_inc(xsum_ok, 1)

            dve.wait_ge(d_const, CONST)
            for n, (w, w_s) in enumerate(((wk, wk_s), (wv, wv_s))):
                dve.wait_ge(wh_ok, n + 1)
                dve.tensor_tensor(w_s[1][:, :, :], w[:, :, :], w_s[0][:, :, :].bitcast(F32),
                                  ALU.subtract).then_inc(wl_ok, 1)
            dve.wait_ge(vl_mm, 1)
            dve.tensor_tensor(vlast[:, :], x_bank[:, 0:D], bvl[:, :], ALU.add).then_inc(vl_ev, 1)
            for g in range(2):
                norm_stats(g, g)
                norm_apply(g, g)
            k_low(0, 0, 0)
            k_low(0, 0, 1)
            v_copy(0, 0)
            q_low(0, 0)

            def slot(g, s, first, last):
                final = last or (isinstance(g, int) and g + 2 >= NG)
                for u in range(GB):
                    b = g * GB + u
                    nxt = not (last and u == GB - 1)
                    bs, bs1 = u % 2, (u + 1) % 2
                    if nxt:
                        k_low(b + 1, bs1, 0)
                    for gr in range(4):
                        dve.wait_ge(s_mm, 4 * b + gr + 1)
                        if gr == 0:
                            at_least(dve, p_ex, 4 * (b - 1))
                        dve.tensor_reduce(negmax[bs][:, gr:gr + 1], s_bank[gr % 2][:, 0:M], AXX, ALU.max,
                                          negate=True).then_inc(mx, 1)
                    if not (first and u == 0):
                        take_out(b - 1, bs1)
                    if nxt:
                        k_low(b + 1, bs1, 1)
                        v_copy(b + 1, bs1)
                    dve.wait_ge(pT_mm, 2 * b + 2)
                    at_least(dve, o_mm, b)
                    dve.tensor_copy(probT[:, 1, :], pT_bank[1][:, :]).then_inc(pT1_ev, 1)
                    if u == 1 and not final:
                        norm_stats(g + 2, s)
                    if u == 2 and not last:
                        q_low(g + 1, 1 - s)
                    if u == 2 and not final:
                        norm_apply(g + 2, s)
                    if u == 3 and not first:
                        out_sum(g - 1, 1 - s)

            slot(0, 0, True, False)
            with dve.Fori(0, NG // 2 - 2) as k:
                slot(k * 2 + 1, 1, False, False)
                slot(k * 2 + 2, 0, False, False)
            slot(NG - 3, 1, False, False)
            slot(NG - 2, 0, False, False)
            slot(NG - 1, 1, False, True)
            take_out(B - 1, (B - 1) % 2)
            out_sum(NG - 1, (NG - 1) % 2)

            dve.wait_ge(x1o_ok, NG)
            dve.memset(mem[:, :, :], 0.0).then_inc(c2, 1)
            dve.wait_ge(be_ok, 1)
            dve.reciprocal(beta[:, :], beta[:, :]).then_inc(c2, 1)
            dve.wait_ge(be_ok, 4)
            dve.wait_ge(d_x, 16)
            dve.wait_ge(c2, 2)

            def stats_of(c, i, src, Q, st_ok_, mv_ok_, rs_ok_, used):
                alone(dve, (mv_ok_, Q * 2))
                dve.bn_stats(st[c][i][:, :], src).then_inc(st_ok_, 1)
                alone(dve, (st_ok_, Q * 2 + i + 1), (rs_ok_, Q), (used, Q * 2))
                dve.bn_aggr(mv2[c][:, i, :], st[c][i][:, :]).then_inc(mv_ok_, 1)

            def potential(t, i):
                dve.wait_ge(gc_ev, t + 1)
                at_least(dve, mem_ok, t)
                for m in range(6):
                    ins = dve.scalar_tensor_tensor(mem[:, m, :], mem[:, m, :], beta[:, m:m + 1], gc[i][:, m, :],
                                                   ALU.mult, ALU.add)
                ins.then_inc(pot_ok, 1)
                dve.wait_ge(pot_ok, t + 1)
                at_least(dve, zc_ok, t - 1)
                dve.tensor_scalar(spk[i][:, :, :], mem[:, :, :], ROUND, ROUND, ALU.add, ALU.subtract).then_inc(rnd_ok, 1)

            def spikes(t, i):
                dve.wait_ge(rnd_ok, t + 1)
                dve.tensor_scalar(spk[i][:, :, :], spk[i][:, :, :], -1.0, 1.0, ALU.max, ALU.min).then_inc(spk_ok, 1)

            def membrane(t, i):
                dve.wait_ge(spk_ok, t + 1)
                for m in range(6):
                    ins = dve.scalar_tensor_tensor(mem[:, m, :], spk[i][:, m, :], nthr[:, m:m + 1], mem[:, m, :],
                                                   ALU.mult, ALU.add)
                ins.then_inc(mem_ok, 1)

            def prod(q, f):
                dve.wait_ge(silu_ok, NF * q + f + 1)
                dve.tensor_tensor(fT[0:FW[f], f, :, :].rearrange("p i b -> p (i b)"), gu_bank[f % 3][0:FW[f], 2 * P:4 * P],
                                  sg[f % 2][0:FW[f], :], ALU.mult).then_inc(prod_ok, 1)

            def unit_sum(Q):
                dve.wait_ge(gru_mm, Q + 1)
                dve.wait_ge(xl_ok, Q * 2 + 2)
                at_least(dve, add_ok, Q)
                at_least(dve, fn_ok, Q * 2)
                dve.tensor_tensor(xa[:, :, :], r_bank[:, :].rearrange("p (i d) -> p i d", i=2),
                                  xm[:, bass.ds(Q * 2, 2), :], ALU.add).then_inc(xa_ok, 1)

            def logits_out(Q):
                dve.wait_ge(rt_mm, Q + 1)
                dve.tensor_tensor(logit[:, bass.ds(Q * 2, 2), :], r_bank[:, 0:2 * NE].rearrange("p (i e) -> p i e", i=2),
                                  spread(rb[:, :], 1, 2), ALU.add).then_inc(rt_ok, 1)

            def turn(q, par, parts):
                f, o, n, m, r = (c in parts for c in "fonmr")
                last = q * 2 - 2
                if r:
                    dve.wait_ge(fd_mm, q)
                    dve.wait_ge(add_ok, q)
                    dve.tensor_tensor(xall[:, bass.ds(last, 2), :], fd_bank[:, :].rearrange("p (i d) -> p i d", i=2),
                                      xall[:, bass.ds(last, 2), :], ALU.add).then_inc(x2_ok, 1)
                    alone(dve, (x2_ok, q))
                    for i in range(2):
                        stats_of("B", i, xall[:, last + i, :], q - 1, stB_ok, mvB_ok, rsB_ok, xm_ok)
                if f:
                    prod(q, 0)
                if m:
                    for i in range(2):
                        stats_of("A", i, xall[:, q * 2 + 6 + i, :], q + 3, stA_ok, mvA_ok, rsA_ok, xl_ok)
                if o:
                    unit_sum(q + 1)
                if r:
                    for i in range(2):
                        dve.wait_ge(rsB_ok, q)
                        at_least(dve, xmT_mm, q - 1)
                        at_least(dve, xm_kept, q - 1)
                        dve.tensor_scalar(xmt[:, i, :], xall[:, last + i, :], mv2["B"][:, i, 0:1],
                                          small["rsB"][:, i:i + 1], ALU.subtract, ALU.mult).then_inc(xm_ok, 1)
                if n:
                    potential(q * 2 + 4, 0)
                if f:
                    prod(q, 1)
                if n:
                    spikes(q * 2 + 4, 0)
                if m:
                    for i in range(2):
                        dve.wait_ge(rsA_ok, q + 4)
                        dve.tensor_scalar(xm[:, q * 2 + 6 + i, :], xall[:, q * 2 + 6 + i, :], mv2["A"][:, i, 0:1],
                                          small["rsA"][:, i:i + 1], ALU.subtract, ALU.mult).then_inc(xl_ok, 1)
                if n:
                    membrane(q * 2 + 4, 0)
                if f:
                    prod(q, 2)
                if n:
                    potential(q * 2 + 5, 1)
                if f:
                    prod(q, 3)
                if n:
                    spikes(q * 2 + 5, 1)
                    membrane(q * 2 + 5, 1)
                if r:
                    logits_out(q - 1)
                if f:
                    prod(q, 4)
                    prod(q, 5)

            turns(dve, turn)

            done = [0]

            def te_bank(b_):
                return b_[:, 0:NT * NE].rearrange("p (t e) -> p t e", e=NE)

            def one_col(n):
                return ones[:, 0:1].to_broadcast([P, n])

            def then(ins):
                done[0] += 1
                ins.then_inc(dv_chain, 1)
                dve.wait_ge(dv_chain, done[0])

            te = lambda a: a[:, :].rearrange("p (t e) -> p t e", e=NE)
            et = lambda a: a[:, :].rearrange("p (e t) -> p e t", e=NE)
            dve.wait_ge(d_mc, MOEC)
            dve.wait_ge(route_ok, 1)
            dve.wait_ge(rt_ok, NQ)
            then(dve.tensor_reduce(lmax[:, :], logit[:, :, :], AXX, ALU.max))
            dve.tensor_tensor(te(lsh), logit[:, :, :], spread(lmax[:, :], 2, NE), ALU.subtract).then_inc(lsh_ok, 1)
            dve.wait_ge(lsh_ok, 1)
            then(dve.tensor_scalar(rank[:, :], lsh[:, :], 0.0, None, ALU.is_ge))
            then(dve.tensor_tensor(te(cum), te(rank), spread(descend[:, :], 1, NT), ALU.mult))
            then(dve.tensor_reduce(best[:, :], te(cum), AXX, ALU.max))
            dve.tensor_tensor(te(oneh), te(cum), spread(best[:, :], 2, NE), ALU.is_equal).then_inc(oneh_ok, 1)
            dve.wait_ge(lex_ok, 1)
            then(dve.tensor_reduce(lsum[:, :], te(lex), AXX, ALU.add))
            then(dve.reciprocal(maxp[:, :], lsum[:, :]))
            dve.wait_ge(rank_mm, 1)
            then(dve.tensor_copy(et(tot), te_bank(bank[5]).rearrange("p t e -> p e t")))
            then(dve.tensor_tensor_scan(cum[:, :], one_col(NT * NE), tot[:, :], 0.0, ALU.mult, ALU.add))
            then(dve.tensor_tensor(exc[:, :], cum[:, :], tot[:, :], ALU.subtract))
            then(dve.tensor_reduce(cnt[:, :], et(tot), AXX, ALU.add))
            then(dve.tensor_scalar(tlf[:, :], cnt[:, :], 1.0 / P, (P - 1) / P - 0.5 + 0.5 / P, ALU.mult, ALU.add))
            then(dve.tensor_scalar(tiles[:, :], tlf[:, :], ROUND, ROUND, ALU.add, ALU.subtract))
            then(dve.tensor_tensor_scan(ctile[:, :], one_col(NE), tiles[:, :], 0.0, ALU.mult, ALU.add))
            then(dve.tensor_tensor(base_e[:, :], ctile[:, :], tiles[:, :], ALU.subtract))
            then(dve.scalar_tensor_tensor(shift[:, :], base_e[:, :], float(P), et(exc)[:, :, 0], ALU.mult, ALU.subtract))
            then(dve.tensor_tensor(et(exc), et(exc), spread(shift[:, :], 2, NT), ALU.add))
            then(dve.tensor_tensor(te(rank), te_bank(bank[4]), et(exc).rearrange("p e t -> p t e"), ALU.add))
            then(dve.tensor_tensor(rank[:, :], rank[:, :], oneh[:, :], ALU.mult))
            then(dve.tensor_reduce(posf[:, :], te(rank), AXX, ALU.add))
            dve.tensor_copy(pos[:, :], posf[:, :]).then_inc(pos_ok, 1)
            then(dve.tensor_tensor(cmp7[:, :, :], spread(slotno[:, :], 2, NE - 1), spread(ctile[:, 0:NE - 1], 1, NS), ALU.is_ge))
            then(dve.tensor_tensor(alt7[:, :, :], cmp7[:, :, :], spread(altern[:, 0:NE - 1], 1, NS), ALU.mult))
            then(dve.tensor_reduce(expf[:, :], cmp7[:, :, :], AXX, ALU.add))
            then(dve.tensor_reduce(parf[:, :], alt7[:, :, :], AXX, ALU.add))
            dve.tensor_copy(expi[:, :], expf[:, :]).then_inc(tab_ok, 1)
            dve.tensor_copy(pari[:, :], parf[:, :]).then_inc(tab_ok, 1)
            dve.tensor_copy(endi[:, :], ctile[:, :]).then_inc(tab_ok, 1)

            def vstep(sl, i, first, last):
                vhid(sl, 0)
                if not first:
                    hT_low(sl - 1, 1)
                vhid(sl, 1)
                if not last:
                    xs_low(sl + 1, 1 - i)
                if not first:
                    y_copy(sl - 1, 1 - i)
                hT_low(sl, 0)

            def vhid(sl, half):
                dve.wait_ge(sa_ok, 2 * sl + half + 1)
                at_least(dve, hT_mm, 2 * sl + half - 1)
                dve.tensor_tensor(hid[half][:, :], g_bank[half][:, :], sa[half][:, :], ALU.mult).then_inc(hid_ok, 1)

            def hT_low(sl, half):
                dve.wait_ge(hT_ev, 2 * sl + half + 1)
                dve.tensor_tensor(hidT[half][1][:, :, :], hT_bank[half][:, :].rearrange("p (f b) -> p f b", f=4),
                                  hidT[half][0][:, :, :].bitcast(F32), ALU.subtract).then_inc(hTl_ok, 1)

            def xs_low(sl, i):
                dve.wait_ge(xsT_ev, sl + 1)
                dve.tensor_tensor(xsT[i][1][:, :, :], xs_bank[:, 0:2 * P].rearrange("p (k b) -> p k b", k=2),
                                  xsT[i][0][:, :, :].bitcast(F32), ALU.subtract).then_inc(xsTl_ok, 1)

            def y_copy(sl, i):
                dve.wait_ge(y_mm, sl + 2)
                at_least(dve, d_ys[i], (sl - i) * 8)
                dve.tensor_copy(ys[i][:, :], y_bank[:, 0:D]).then_inc(y_ok, 1)

            xs_low(0, 0)
            tiles_of_experts(dve, vstep)
            hT_low(NS - 1, 1)
            y_copy(NS - 1, (NS - 1) % 2)
            for t in range(NT):
                dve.wait_ge(d_yg[t % 4], 16 * (t // 4 + 1))
                dve.scalar_tensor_tensor(xall[:, t, :], yg[t % 4][:, :], maxp[:, t:t + 1], xall[:, t, :],
                                         ALU.mult, ALU.add).then_inc(fin_ok, 1)

        @block.gpsimd
        def _(pool):
            pool.memset(halfneg[:, :], -0.5).then_inc(c_ok, 1)
            pool.memset(x1o[0][:, :], 0.0).then_inc(z_ok, 1)
            pool.memset(zero[:, :], 0.0).then_inc(c_ok, 1)
            pool.wait_ge(c_ok, 2)
            pool.wait_ge(d_const, CONST)
            pool.wait_ge(d_zero, 16)

            def norm_scale(g, s):
                alone(pool, (mv_ok, g + 1), (xn_ok, g - 1))
                pool.tensor_scalar(vare[s][:, :], mv[s][:, 1:2], EPS, None, ALU.add).then_inc(var_ok, 1)
                pool.wait_ge(var_ok, g + 1)
                pool.tensor_tensor(rstd[s][:, :], vare[s][:, :], halfneg[:, :], ALU.pow).then_inc(rstd_ok, 1)

            def ctx_low(b, s, u, bs):
                pool.wait_ge(ch_ok, b + 1)
                pool.tensor_tensor(cx_s[bs][1][:, :, 0:M], cx[s][:, u, :, :], cx_s[bs][0][:, :, 0:M].bitcast(F32),
                                   ALU.subtract).then_inc(cl_ok, 1)

            def block_queries(b, g, s, u, bs):
                if u == 0:
                    pool.wait_ge(ql_ok, g + 1)
                at_least(pool, s_mm, 4 * (b - 1))
                for x in range(2):
                    for half in range(2):
                        ins = pool.tensor_tensor(
                            qbd[bs][x][:, half, :].rearrange("p (j l) -> p j l", j=4),
                            spread(qT[s][x][:, half, u * L:u * L + L].bitcast(F32), 1, 4),
                            spread(headmask[:, :], 2, L), ALU.mult)
                ins.then_inc(qbd_ok, 1)

            def last_key(b, g, s, u, bs):
                pool.wait_ge(p_ex, 4 * b + 4)
                if u == 0:
                    pool.wait_ge(d_vb[s], ((g - s) * 8 + 16) * 4)
                at_least(pool, o_ev, b - 1)
                pool.tensor_tensor(olast[bs][:, :, :], vb[s][:, u, :].rearrange("p (g d) -> p g d", g=4),
                                   prob[bs][:, :, KEYS:M].to_broadcast([P, 4, DH]), ALU.mult).then_inc(ol_ok, 1)

            def normalise(b, g, s, u, bs):
                pool.wait_ge(o_ev, b + 1)
                if u == 0:
                    at_least(pool, oT_mm, g - 1)
                pool.tensor_tensor(on[s][:, u, :].rearrange("p (g d) -> p g d", g=4), oraw[bs][:, :, :],
                                   spread(rinv[bs][:, :], 2, DH), ALU.mult).then_inc(on_ok, 1)

            def add_bias(g, s):
                pool.wait_ge(xsum_ok, g + 1)
                at_least(pool, d_x1[s], (g - s) * 8)
                pool.tensor_tensor(x1o[s][:, :], xsum[s][:, :], bo[:, :], ALU.add).then_inc(x1o_ok, 1)

            for i in range(2):
                for x in range(2):
                    pool.tensor_tensor(cx_s[i][x][:, :, M:MP], spread(zero[0:CK, :], 1, 2), spread(zero[0:CK, :], 1, 2),
                                       ALU.add).then_inc(pad_ok, 1)
            norm_scale(0, 0)
            norm_scale(1, 1)
            ctx_low(0, 0, 0, 0)
            ctx_low(1, 0, 1, 1)
            block_queries(0, 0, 0, 0, 0)

            def slot(g, s, first, last):
                final = last or (isinstance(g, int) and g + 2 >= NG)
                for u in range(GB):
                    b = g * GB + u
                    bs, bs1 = u % 2, (u + 1) % 2
                    if not (last and u >= 2):
                        ctx_low(b + 2, s if u < 2 else 1 - s, (u + 2) % GB, bs)
                    if not (first and u == 0):
                        if u == 0:
                            normalise(b - 1, g - 1, 1 - s, GB - 1, bs1)
                        else:
                            normalise(b - 1, g, s, u - 1, bs1)
                    if u < 3:
                        block_queries(b + 1, g, s, u + 1, bs1)
                    elif not last:
                        block_queries(b + 1, g + 1, 1 - s, 0, bs1)
                    last_key(b, g, s, u, bs)
                    if u == 1 and not final:
                        norm_scale(g + 2, s)
                    if u == 3 and not first:
                        add_bias(g - 1, 1 - s)

            slot(0, 0, True, False)
            with pool.Fori(0, NG // 2 - 2) as k:
                slot(k * 2 + 1, 1, False, False)
                slot(k * 2 + 2, 0, False, False)
            slot(NG - 3, 1, False, False)
            slot(NG - 2, 0, False, False)
            slot(NG - 1, 1, False, True)
            normalise(B - 1, NG - 1, 1, GB - 1, 1)
            add_bias(NG - 1, 1)

            pool.memset(hT[1][:, :, :], 0.0).then_inc(c2, 16)
            pool.memset(ebase[:, :], float(np.e)).then_inc(c2, 16)
            pool.wait_ge(d_ff, FFW)
            pool.wait_ge(c2, 32)
            pool.tensor_scalar(braw[:, :], braw[:, :], -1.0, None, ALU.mult).then_inc(zw_ok, 1)
            pool.wait_ge(zw_ok, 1)
            pool.tensor_tensor(beta[:, :], ebase[:, :], braw[:, :], ALU.pow).then_inc(zw_ok, 1)
            pool.wait_ge(zw_ok, 2)
            pool.tensor_scalar(beta[:, :], beta[:, :], 1.0, None, ALU.add).then_inc(be_ok, 1)
            for i in range(2):
                pool.tensor_scalar(gam1[i][:, :], gam[i][:, :], 1.0, None, ALU.add).then_inc(be_ok, 1)
            pool.tensor_scalar(nthr[:, :], thr[:, :], -1.0, None, ALU.mult).then_inc(be_ok, 1)

            def std_inverse(c, Q, mv_ok_, ve_ok, rs_ok, used):
                alone(pool, (mv_ok_, Q * 2 + 2), (used, Q * 2))
                pool.tensor_scalar(small["ve" + c][:, :], mv2[c][:, :, 1], EPS, None, ALU.add).then_inc(ve_ok, 1)
                pool.wait_ge(ve_ok, Q + 1)
                pool.tensor_tensor(small["rs" + c][:, :], small["ve" + c][:, :], halfneg[:, :].to_broadcast([P, 2]),
                                   ALU.pow).then_inc(rs_ok, 1)

            def rms_scale(c, Q, ss_ok, sm_ok, sp_ok, sc_ok, used):
                alone(pool, (ss_ok, Q * 2 + 2))
                pool.tensor_scalar(small["sm" + c][:, :], small["ss" + c][:, :], RMS_MIN ** 2, None,
                                   ALU.max).then_inc(sm_ok, 1)
                pool.wait_ge(sm_ok, Q + 1)
                pool.tensor_tensor(small["sp" + c][:, :], small["sm" + c][:, :], halfneg[:, :].to_broadcast([P, 2]),
                                   ALU.pow).then_inc(sp_ok, 1)
                alone(pool, (sp_ok, Q + 1), (used, Q * 2))
                pool.tensor_scalar(small["sc" + c][:, :], small["sp" + c][:, :], float(D) ** 0.5, None,
                                   ALU.mult).then_inc(sc_ok, 1)

            def state(Q, i):
                t = Q * 2 + i
                alone(pool, (spk_ok, t + 1), (h_ok, t))
                pool.tensor_scalar(zed[:, :, :], spk[i][:, 0:3, :], 0.5, 0.5, ALU.mult, ALU.add)
                pool.tensor_scalar(wed[:, :, :], spk[i][:, 0:3, :], -0.5, 0.5, ALU.mult, ALU.add).then_inc(zw_ok, 1)
                pool.wait_ge(zw_ok, t + 3)
                pool.tensor_tensor(zed[:, :, :], zed[:, :, :], spk[i][:, 3:6, :], ALU.mult)
                pool.tensor_tensor(wed[:, :, :], wed[:, :, :], hT[1 - i][:, :, :], ALU.mult).then_inc(zc_ok, 1)
                pool.wait_ge(zc_ok, t + 1)
                at_least(pool, gru_mm, Q)
                pool.tensor_tensor(hT[i][:, :, :], wed[:, :, :], zed[:, :, :], ALU.add).then_inc(h_ok, 1)

            def turn(q, par, parts):
                f, o, n, m, r = (c in parts for c in "fonmr")
                if r:
                    std_inverse("B", q - 1, mvB_ok, veB_ok, rsB_ok, xm_ok)
                if m:
                    std_inverse("A", q + 3, mvA_ok, veA_ok, rsA_ok, xl_ok)
                if o:
                    rms_scale("B", q + 1, ssB_ok, smB_ok, spB_ok, scB_ok, fn_ok)
                    pool.wait_ge(xa_ok, q + 2)
                    pool.tensor_tensor(xall[:, bass.ds(q * 2 + 2, 2), :], xall[:, bass.ds(q * 2 + 2, 2), :], xa[:, :, :],
                                       ALU.add).then_inc(add_ok, 1)
                if r:
                    pool.wait_ge(xm_ok, q * 2)
                    pool.tensor_copy(xm[:, bass.ds(q * 2 - 2, 2), :], xmt[:, :, :]).then_inc(xm_kept, 1)
                if n:
                    state(q + 2, 0)
                if m:
                    rms_scale("A", q + 3, ssA_ok, smA_ok, spA_ok, scA_ok, xr_ok)
                if n:
                    state(q + 2, 1)
                if parts == "fonmr":
                    piece = bass.ds((q - 1) * WC, WC)
                    pool.wait_ge(w0_ok, q)
                    pool.tensor_tensor(wsplit[:, 0, 1, piece], raw[:, piece], wsplit[:, 0, 0, piece].bitcast(F32),
                                       ALU.subtract).then_inc(wlo_ok, 1)

            turns(pool, turn)

            pool.memset(ones[:, :], 1.0).then_inc(route_ok, 1)

            def load_w(e, c):
                pool.dma_start(raw[:, PIECES[c]], T["we"][e, :, PIECES[c]]).then_inc(d_we[c], 16)

            W0 = NQ - 4
            pool.wait_ge(wlo_ok, W0)
            pool.sem_inc(w_ready, 1)
            for c in range(WP):
                load_w(1, c)
            for t in range(NT):
                if t == 0:
                    pool.wait_ge(pos_ok, 1)
                pool.indirect_dma_start(xs_scr, bass.IndirectOffsetOnAxis(pos[:, t:t + 1].bitcast(U32), 0),
                                        xm[:, t, :], None).then_inc(d_sort, 16)
            pool.wait_ge(tab_ok, 3)
            for e in range(1, NE):
                if e > 1:
                    last_slot = pool.value_load(endi[0:1, e - 2:e - 1], min_val=0, max_val=NS)
                    pool.wait_ge(y_mm, last_slot + 1)
                for c in range(WP):
                    n = (e - 1) * WP + c
                    pool.wait_ge(d_we[c], 16 * e)
                    high, low = (wsplit[:, e % 2, h, PIECES[c]] for h in range(2))
                    pool.tensor_tensor(high, raw[:, PIECES[c]], zero[:, :].to_broadcast([P, WE // WP]),
                                       ALU.add).then_inc(whi_ok, 1)
                    pool.wait_ge(whi_ok, n + 1)
                    pool.tensor_tensor(low, raw[:, PIECES[c]], high.bitcast(F32), ALU.subtract).then_inc(wlo_ok, 1)
                    pool.wait_ge(wlo_ok, W0 + n + 1)
                    if e + 1 < NE:
                        load_w(e + 1, c)
                pool.sem_inc(w_ready, 1)
            pool.wait_ge(d_ys[0], 16 * ((NS + 1) // 2))
            pool.wait_ge(d_ys[1], 16 * (NS // 2))
            for t in range(NT):
                at_least(pool, fin_ok, t - 3)
                pool.indirect_dma_start(yg[t % 4][:, :], None, ys_scr,
                                        bass.IndirectOffsetOnAxis(pos[:, t:t + 1].bitcast(U32), 0)).then_inc(d_yg[t % 4], 16)


def lay_out(i):
    f = lambda a: np.ascontiguousarray(a)
    wkv = i["L0_xattn_Wkv"].reshape(NH, 2, DH, C)
    bkv = i["L0_xattn_bkv"].reshape(NH, 2, DH)
    ctxT = i["ctx_768"].transpose(2, 0, 1).reshape(2, CK, B, M)
    wv = wkv[:, 1].transpose(2, 0, 1)
    bv = bkv[:, 1]

    def rows(w):
        return f(w.reshape(2, w.shape[0] // 2, w.shape[1]).transpose(1, 0, 2))

    def by_head(a):
        return a.reshape(*a.shape[:-2], 4, 4, DH).swapaxes(-3, -2)

    T = {
        "x": f(i["x"].reshape(B * L, D)),
        "cx": f(ctxT.transpose(1, 2, 0, 3)),
        "cxl": f(ctxT[:, :, :, KEYS].transpose(1, 0, 2)),
        "wk": rows(wkv[:, 0].transpose(2, 0, 1).reshape(C, D)),
        "wv": rows(wv.reshape(C, D)),
        "wvl": rows(by_head(wv).reshape(C, D)),
        "wq": rows(i["L0_xattn_Wq"].T),
        "wo": f(i["L0_xattn_Wo"].T.reshape(4, 4, DH, D).transpose(0, 2, 1, 3).reshape(64, 4, D)),
        "bk": f(bkv[:, 0].reshape(2, P).T),
        "bq": f(i["L0_xattn_bq"].reshape(2, P).T),
        "bv": f(bv.reshape(D)),
        "bvl": f(by_head(bv).reshape(D)),
        "bo": f(i["L0_xattn_bo"]),
        "ident": np.eye(P, dtype=np.float32),
        "headmask": (DH ** -0.5 * (np.arange(P)[:, None] // DH % 4 == np.arange(4)[None, :])).astype(np.float32),
    }

    def block_diagonal(w):
        h, o, n = w.shape
        m = np.zeros((h, n, h, o), w.dtype)
        m[np.arange(h), :, np.arange(h), :] = w.transpose(0, 2, 1)
        return m.reshape(h * n, h * o)

    def drive(w):
        m = block_diagonal(w).reshape(2, P, 3, P)
        return f(np.stack([m[0, :, 0], m[0, :, 1], m[1, :, 1], m[1, :, 2]], 1))

    def columns(a):
        return f(a.reshape(-1, P).T)

    fd = np.zeros((NF * P, D), np.float32)
    fd[:FI] = i["L0_attn_ffd_W"].T
    T |= {
        "gw": drive(i["L0_attn_gate_W"]),
        "cw": drive(i["L0_attn_cand_W"]),
        "ow": f(block_diagonal(i["L0_attn_out_W"]).reshape(3, P, D).transpose(1, 0, 2)),
        "braw": f(np.concatenate([columns(i["L0_attn_gate_beta_raw"]), columns(i["L0_attn_cand_beta_raw"])], 1)),
        "thr": f(np.concatenate([columns(i["L0_attn_gate_theta"]), columns(i["L0_attn_cand_theta"])], 1)),
        "gamA": columns(i["L0_attn_in_gamma"]),
        "gamB": columns(i["L0_attn_ff_gamma"]),
        "fg": rows(i["L0_attn_ffg_W"].T),
        "fu": rows(i["L0_attn_ffu_W"].T),
        "fd": f(fd.reshape(NF, P, D).transpose(1, 0, 2)),
        "rw": rows(i["L0_ffn_router_w"]),
        "rb": f(i["L0_ffn_router_b"]),
        "we": f(np.concatenate([
            i["L0_ffn_w1"].reshape(NE, 2, P, 2 * FF).transpose(0, 2, 1, 3).reshape(NE, P, 4 * FF),
            i["L0_ffn_w2"].reshape(NE, FT, P, D).transpose(0, 2, 1, 3).reshape(NE, P, FT * D)], 2)),
        "lt": np.triu(np.ones((P, P), np.float32), 1),
        "descend": np.arange(NE, 0, -1).astype(np.float32),
        "slotno": np.arange(NS).astype(np.float32),
        "altern": np.where(np.arange(NE) % 2, -1.0, 1.0).astype(np.float32),
    }
    return T


def kernel(**inputs):
    import concourse.bacc as bacc
    from concourse.bass_utils import run_bass_kernel_spmd

    arrays = lay_out({name: np.asarray(a) for name, a in inputs.items()})
    nc = bacc.Bacc("TRN2", target_bir_lowering=False, num_devices=1)
    T = {name: nc.dram_tensor(name, a.shape, mybir.dt.from_np(a.dtype), kind="ExternalInput").ap()
         for name, a in arrays.items()}
    out = nc.dram_tensor("out", (B * L, D), F32, kind="ExternalOutput").ap()
    build(nc, T, out)
    results = run_bass_kernel_spmd(nc, [arrays], core_ids=[0])
    return results.results[0]["out"].reshape(B, L, D)
```

```python
from contextlib import ExitStack

import numpy as np

import concourse.bass as bass
from concourse import mybir

F32 = mybir.dt.float32
F32R = mybir.dt.float32r
I32 = mybir.dt.int32
U32 = mybir.dt.uint32
ALU = mybir.AluOpType
ACT = mybir.ActivationFunctionType
AXX = mybir.AxisListType.X

P = 128
B, L, D = 128, 32, 256
M, C = 257, 192
CK = C // 2
MP = M + 1
KEYS = M - 1
NH, DH = 16, 16
GB = P // L
NG = B // GB
SPLIT = ((0, 0), (0, 1), (1, 0))
EPS = 1e-5
NE = 8
FI = D * 4 * 2 // 3
FF = 1024
FT = FF // P
WE = 2 * 2 * FF + FT * D
DX = D + 2
WP = 3
NS = B * L // P + NE - 1
NF = (FI + P - 1) // P
RMS_MIN = 1e-12
ROUND = 1.5 * 2 ** 23


def at_least(eng, sem, value):
    if isinstance(value, int) and value <= 0:
        return
    eng.wait_ge(sem, value)


def spread(ap, axis, n):
    v = ap.unsqueeze(axis)
    shape = list(v.shape)
    shape[axis] = n
    return v.to_broadcast(shape)


class Plan:

    def __init__(self, nc, base, end):
        self.nc, self.at, self.end = nc, base, end

    def tensor(self, name, shape, dtype=F32):
        size = int(np.prod(shape[1:])) * 4
        self.at = (self.at + 31) // 32 * 32
        t = self.nc.alloc_sbuf_tensor_at(name, list(shape), dtype, offset=self.at)
        self.at += size
        assert self.at <= self.end, (name, self.at, self.end)
        return t


def build(nc, T, out):
    ctx = ExitStack()
    with ctx:
        def sem(name):
            return ctx.enter_context(nc.semaphore(name))

        x1_scr = nc.dram_tensor("x1_scr", (B * L, D), F32, kind="Internal").ap()
        vlast_scr = nc.dram_tensor("vlast_scr", (B, D), F32, kind="Internal").ap()

        base, end = nc.sbuf_base, nc.sbuf_usable_end
        keep = Plan(nc, base, end)
        ident = keep.tensor("ident", [P, P])
        halfneg = keep.tensor("halfneg", [P, 1])
        zero = keep.tensor("zero", [P, 1])

        NT = L
        top = Plan(nc, end - 4 * (NT * D + NT * DX + NT * NE + 4 * FI + NF * D + 3 * NE + WE) - 96 - 9 * 32, end)
        top_at = top.at
        xall = top.tensor("xall", [P, NT, D])
        xm_at = top.at
        xm = top.tensor("xm", [P, NT, DX])
        logit = top.tensor("logit", [P, NT, NE])
        moe_at = top.at
        fg = top.tensor("fg", [P, 2, FI])
        fu = top.tensor("fu", [P, 2, FI])
        fd = top.tensor("fd", [P, NF, D])
        rw = top.tensor("rw", [P, 2, NE])
        rb = top.tensor("rb", [P, NE])
        braw = top.tensor("braw", [P, 6])
        thr = top.tensor("thr", [P, 6])
        beta = top.tensor("beta", [P, 6])
        nthr = top.tensor("nthr", [P, 6])
        ebase = top.tensor("ebase", [P, 6])
        gam = [top.tensor(f"gam{i}", [P, 2]) for i in range(2)]
        gam1 = [top.tensor(f"gam1{i}", [P, 2]) for i in range(2)]
        moe_end = top.at
        first = Plan(nc, top.at, end)
        raw = top.tensor("raw", [P, WE])
        wk = first.tensor("wk", [CK, 2, D])
        wv = first.tensor("wv", [CK, 2, D])
        wvl = first.tensor("wvl", [CK, 2, D])
        cxl = first.tensor("cxl", [CK, 2, B])
        bvl = first.tensor("bvl", [P, D])
        vlast = first.tensor("vlast", [P, D])

        att = Plan(nc, keep.at, top_at)
        wq = att.tensor("wq", [P, 2, D])
        wo = att.tensor("wo", [P, 2, D])
        bk = att.tensor("bk", [P, 2])
        bq = att.tensor("bq", [P, 2])
        bv = att.tensor("bv", [P, D])
        bo = att.tensor("bo", [P, D])
        headmask = att.tensor("headmask", [P, 4])
        cx = [att.tensor(f"cx{i}", [CK, GB, 2, M]) for i in range(2)]
        vb = [att.tensor(f"vb{i}", [P, GB, 64]) for i in range(2)]
        x_in = [att.tensor(f"x_in{i}", [P, D]) for i in range(2)]
        x_res = [att.tensor(f"x_res{i}", [P, D]) for i in range(2)]
        xsum = [att.tensor(f"xsum{i}", [P, D]) for i in range(2)]
        x1o = [att.tensor(f"x1o{i}", [P, D]) for i in range(2)]
        xn = [att.tensor(f"xn{i}", [P, D]) for i in range(2)]
        xnT = [att.tensor(f"xnT{i}", [P, 2, P]) for i in range(2)]

        def parts(name, shape):
            return [att.tensor(f"{name}_{c}", shape, F32R) for c in ("hi", "lo")]

        wk_s, wv_s = parts("wk_s", [CK, 2, D]), parts("wv_s", [CK, 2, D])
        cx_s = [parts(f"cx_s{i}", [CK, 2, MP]) for i in range(2)]
        qT = [parts(f"qT{i}", [P, 2, P]) for i in range(2)]
        qbd = [parts(f"qbd{i}", [P, 2, P]) for i in range(2)]
        kT = [parts(f"kT{i}", [P, 2, MP]) for i in range(2)]
        v = [att.tensor(f"v{i}", [P, 2, D]) for i in range(2)]
        prob = [att.tensor(f"prob{i}", [P, 4, M]) for i in range(2)]
        probT = att.tensor("probT", [P, 2, 4 * P])
        negmax = [att.tensor(f"negmax{i}", [P, 4]) for i in range(2)]
        rowsum = [att.tensor(f"rowsum{i}", [P, 4]) for i in range(2)]
        rinv = [att.tensor(f"rinv{i}", [P, 4]) for i in range(2)]
        olast = [att.tensor(f"olast{i}", [P, 4, DH]) for i in range(2)]
        oraw = [att.tensor(f"oraw{i}", [P, 4, DH]) for i in range(2)]
        on = [att.tensor(f"on{i}", [P, GB, 64]) for i in range(2)]
        oT = [att.tensor(f"oT{i}", [P, 2, GB, L]) for i in range(2)]
        stats = [att.tensor(f"stats{i}", [P, 6]) for i in range(2)]
        mv = [att.tensor(f"mv{i}", [P, 2]) for i in range(2)]
        vare = [att.tensor(f"vare{i}", [P, 1]) for i in range(2)]
        rstd = [att.tensor(f"rstd{i}", [P, 1]) for i in range(2)]

        bank = [ctx.enter_context(nc.psum_tensor(f"bank{i}", [P, 512], F32)) for i in range(8)]
        kv_bank = bank[0:2]
        s_bank = bank[2:4]
        pT_bank = bank[4:6]
        o_bank = bank[6]
        x_bank = bank[7]

        d_const = sem("d_const")
        d_cx = [sem(f"d_cx{i}") for i in range(2)]
        d_vb = [sem(f"d_vb{i}") for i in range(2)]
        d_xin = [sem(f"d_xin{i}") for i in range(2)]
        d_xres = [sem(f"d_xres{i}") for i in range(2)]
        d_x1 = [sem(f"d_x1{i}") for i in range(2)]
        d_vlast = sem("d_vlast")
        vl_mm, kv_mm, s_mm, pT_mm, o_mm = (sem(n) for n in ("vl_mm", "kv_mm", "s_mm", "pT_mm", "o_mm"))
        xT_mm, q_mm, oT_mm, out_mm = (sem(n) for n in ("xT_mm", "q_mm", "oT_mm", "out_mm"))
        k_ev, p_ex, pT0_ev = (sem(n) for n in ("k_ev", "p_ex", "pT0_ev"))
        xT_ev, q_ev, oT_ev = (sem(n) for n in ("xT_ev", "q_ev", "oT_ev"))
        vl_ev, mx, v_ev, pT1_ev, o_ev, rinv_ok, xsum_ok = (
            sem(n) for n in ("vl_ev", "mx", "v_ev", "pT1_ev", "o_ev", "rinv_ok", "xsum_ok"))
        st_ok, mv_ok, xn_ok = (sem(n) for n in ("st_ok", "mv_ok", "xn_ok"))
        pad_ok, wh_ok, wl_ok, ch_ok, cl_ok, kl_ok, ql_ok = (
            sem(n) for n in ("pad_ok", "wh_ok", "wl_ok", "ch_ok", "cl_ok", "kl_ok", "ql_ok"))
        c_ok, qbd_ok, ol_ok, on_ok, x1o_ok, var_ok, rstd_ok = (
            sem(n) for n in ("c_ok", "qbd_ok", "ol_ok", "on_ok", "x1o_ok", "var_ok", "rstd_ok"))

        consts = [(cxl, "cxl"), (wvl, "wvl"), (ident, "ident"), (wk, "wk"), (wv, "wv"), (wq, "wq"),
                  (bk, "bk"), (bq, "bq"), (headmask, "headmask"), (wo, "wo")]
        rows = [(bv, "bv"), (bvl, "bvl"), (bo, "bo")]
        CONST = 16 * (len(consts) + len(rows))

        passed = sem("passed")

        def alone(eng, *waits):
            for s_, v in waits:
                at_least(eng, s_, v)
            eng.sem_inc(passed, 1)

        def slots(eng, slot):
            slot(0, 0, True, False)
            with eng.Fori(0, NG // 2 - 1) as k:
                slot(k * 2 + 1, 1, False, False)
                slot(k * 2 + 2, 0, False, False)
            slot(NG - 1, (NG - 1) % 2, False, True)

        wsplit = Plan(nc, keep.at, end).tensor("wsplit", [P, 2, 2, WE], F32R)
        ff = Plan(nc, keep.at, keep.at + 2 * WE * 4)

        def ff_parts(name, shape):
            return [ff.tensor(f"{name}_{c}", shape, F32R) for c in ("hi", "lo")]

        fg_s, fu_s = ff_parts("fg_s", [P, 2, FI]), ff_parts("fu_s", [P, 2, FI])
        fnT = [ff_parts(f"fnT{i}", [P, 2, 2, P]) for i in range(2)]
        ff = Plan(nc, keep.at + 2 * WE * 4, top_at)
        gw = [ff.tensor(f"gw{i}", [P, 4, P]) for i in range(2)]
        ow = ff.tensor("ow", [P, 3, D])
        xr = ff.tensor("xr", [P, 2, D])
        xrT = ff.tensor("xrT", [P, 2, 2, P])
        gc = [ff.tensor(f"gc{i}", [P, 6, P]) for i in range(2)]
        mem = ff.tensor("mem", [P, 6, P])
        spk = [ff.tensor(f"spk{i}", [P, 6, P]) for i in range(2)]
        zed = ff.tensor("zed", [P, 3, P])
        wed = ff.tensor("wed", [P, 3, P])
        hT = [ff.tensor(f"hT{i}", [P, 3, P]) for i in range(2)]
        xa = ff.tensor("xa", [P, 2, D])
        fn = ff.tensor("fn", [P, 2, D])
        sg = [ff.tensor(f"sg{i}", [P, 2 * P]) for i in range(2)]
        fT = ff.tensor("fT", [P, NF, 2, P])
        xmt = ff.tensor("xmt", [P, 2, D])
        xmT = ff.tensor("xmT", [P, 2, 2, P])
        st = {c: [ff.tensor(f"st{c}{i}", [P, 6]) for i in range(2)] for c in "AB"}
        mv2 = {c: ff.tensor(f"mv2{c}", [P, 2, 2]) for c in "AB"}
        small = {n: ff.tensor(n, [P, 2]) for n in
                 ("veA", "rsA", "veB", "rsB", "ssA", "smA", "spA", "scA", "ssB", "smB", "spB", "scB")}

        moe = Plan(nc, moe_at, moe_end)
        lt = moe.tensor("lt", [P, P])
        ones = moe.tensor("ones", [P, P])
        token = moe.tensor("token", [P, NT])
        descend = moe.tensor("descend", [P, NE])
        slotno = moe.tensor("slotno", [P, NS])
        lmax, lsum, maxp, best, posf = (moe.tensor(n, [P, NT]) for n in ("lmax", "lsum", "maxp", "best", "posf"))
        lsh, lex, oneh, rank, tot, cum, exc = (moe.tensor(n, [P, NT * NE]) for n in (
            "lsh", "lex", "oneh", "rank", "tot", "cum", "exc"))
        cnt, tlf, tiles, ctile, base_e, shift = (moe.tensor(n, [P, NE]) for n in (
            "cnt", "tlf", "tiles", "ctile", "base_e", "shift"))
        pos = moe.tensor("pos", [P, NT], I32)
        cmp7 = moe.tensor("cmp7", [P, NS, NE - 1])
        expf = moe.tensor("expf", [P, NS])
        expi = moe.tensor("expi", [P, NS], I32)
        endi = moe.tensor("endi", [P, NE], I32)
        assert moe.at <= end
        moe = Plan(nc, xm_at, xm_at + NT * DX * 4)
        xs = [moe.tensor(f"xs{i}", [P, DX]) for i in range(2)]
        xsT = [[moe.tensor(f"xsT{i}{c}", [P, 2, P], F32R) for c in ("hi", "lo")] for i in range(2)]
        sa = [moe.tensor(f"sa{i}", [P, 512]) for i in range(2)]
        hid = [moe.tensor(f"hid{i}", [P, 512]) for i in range(2)]
        hidT = [[moe.tensor(f"hidT{i}{c}", [P, 4, P], F32R) for c in ("hi", "lo")] for i in range(2)]
        aux = [moe.tensor(f"aux{i}", [P, 2]) for i in range(2)]
        ys = [moe.tensor(f"ys{i}", [P, D + 1]) for i in range(2)]
        yr = [moe.tensor(f"yr{i}", [P, D + 1]) for i in range(4)]
        xs_scr = nc.dram_tensor("xs_scr", (NS * P, DX), F32, kind="Internal").ap()
        ys_scr = nc.dram_tensor("ys_scr", (NS * P, D + 1), F32, kind="Internal").ap()
        a_bank, g_bank = bank[0:2], bank[2:4]
        hT_bank = bank[4:6]
        xs_bank, y_bank = bank[6], bank[7]

        d_zero, d_mc, d_w = sem("d_zero"), sem("d_mc"), sem("d_w")
        z_ok, w_ready, d_sort = sem("z_ok"), sem("w_ready"), sem("d_sort")
        w0_ok, d_we = sem("w0_ok"), [sem(f"d_we{i}") for i in range(WP)]
        whi_ok, wlo_ok, xsTl_ok, hTl_ok = (sem(n) for n in ("whi_ok", "wlo_ok", "xsTl_ok", "hTl_ok"))
        PIECES = [slice(c * WE // WP, (c + 1) * WE // WP) for c in range(WP)]
        d_xs, d_ys = [sem(f"d_xs{i}") for i in range(2)], [sem(f"d_ys{i}") for i in range(2)]
        d_yr = [sem(f"d_yr{i}") for i in range(4)]
        route_ok, lsh_ok, lex_ok, oneh_ok, rank_mm, pos_ok, tab_ok = (sem(n) for n in (
            "route_ok", "lsh_ok", "lex_ok", "oneh_ok", "rank_mm", "pos_ok", "tab_ok"))
        xsT_mm, xsT_ev, ag_mm, sa_ok, hid_ok, hT_mm, hT_ev, y_mm, y_ok, aux_ok = (sem(n) for n in (
            "xsT_mm", "xsT_ev", "ag_mm", "sa_ok", "hid_ok", "hT_mm", "hT_ev", "y_mm", "y_ok", "aux_ok"))
        d_out, d_add = sem("d_out"), [sem(f"d_add{i}") for i in range(4)]
        moec = [(lt, "lt"), (token, "token")]
        moer = [(descend, "descend"), (slotno, "slotno")]
        MOEC = 16 * (len(moec) + len(moer))

        def tiles_of_experts(eng, step):
            step(0, 0, True, False)
            with eng.Fori(0, (NS - 3) // 2) as k:
                step(k * 2 + 1, 1, False, False)
                step(k * 2 + 2, 0, False, False)
            step(NS - 2, (NS - 2) % 2, False, False)
            step(NS - 1, (NS - 1) % 2, False, True)

        gc_bank = bank[0:2]
        t_bank = bank[2]
        r_bank = bank[3]
        gu_bank = bank[4:7]
        fd_bank = bank[7]

        d_ff, d_x, d_vec = sem("d_ff"), sem("d_x"), sem("d_vec")
        c2, be_ok, eb_ok, ez_ok, h0_ok = (sem(n) for n in ("c2", "be_ok", "eb_ok", "ez_ok", "h0_ok"))
        fh_ok, fl_ok, fnl_ok, w0l_ok = (sem(n) for n in ("fh_ok", "fl_ok", "fnl_ok", "w0l_ok"))
        stA_ok, mvA_ok, veA_ok, rsA_ok, xl_ok, ssA_ok, smA_ok, spA_ok, scA_ok, xr_ok = (sem(n) for n in (
            "stA_ok", "mvA_ok", "veA_ok", "rsA_ok", "xl_ok", "ssA_ok", "smA_ok", "spA_ok", "scA_ok", "xr_ok"))
        xrT_mm, xrT_ev, gc_mm, gc_ev, pot_ok, rnd_ok, spk_ok, mem_ok = (sem(n) for n in (
            "xrT_mm", "xrT_ev", "gc_mm", "gc_ev", "pot_ok", "rnd_ok", "spk_ok", "mem_ok"))
        zw_ok, zc_ok, h_ok, gru_mm, xa_ok, add_ok = (sem(n) for n in (
            "zw_ok", "zc_ok", "h_ok", "gru_mm", "xa_ok", "add_ok"))
        ssB_ok, smB_ok, spB_ok, scB_ok, fn_ok, fnT_mm, fnT_ev = (sem(n) for n in (
            "ssB_ok", "smB_ok", "spB_ok", "scB_ok", "fn_ok", "fnT_mm", "fnT_ev"))
        gu_mm, silu_ok, prod_ok, fd_mm, x2_ok = (sem(n) for n in ("gu_mm", "silu_ok", "prod_ok", "fd_mm", "x2_ok"))
        stB_ok, mvB_ok, veB_ok, rsB_ok, xm_ok, xmT_mm, xmT_ev, rt_mm, rt_ok = (sem(n) for n in (
            "stB_ok", "mvB_ok", "veB_ok", "rsB_ok", "xm_ok", "xmT_mm", "xmT_ev", "rt_mm", "rt_ok"))
        dv_chain = sem("dv_chain")
        xm_kept = sem("xm_kept")

        vectors = [(braw, "braw"), (thr, "thr"), (gam[0], "gamA"), (gam[1], "gamB")]
        early = [(fg, "fg"), (fu, "fu"), (fd, "fd"), (rw, "rw")]
        late = [(gw[0], "gw"), (gw[1], "cw"), (ow, "ow")]
        FFW = 16 * (len(early) + 1 + len(late))
        XROWS = NS * P // NG
        FW = [min(P, FI - P * f) for f in range(NF)]

        NQ = NT // 2

        def turns(eng, turn):
            turn(-3, 1, "m")
            turn(-2, 0, "nm")
            turn(-1, 1, "onm")
            turn(0, 0, "fonm")
            with eng.Fori(0, (NQ - 4) // 2) as k:
                turn(k * 2 + 1, 1, "fonmr")
                turn(k * 2 + 2, 0, "fonmr")
            turn(NQ - 3, 1, "fonr")
            turn(NQ - 2, 0, "for")
            turn(NQ - 1, 1, "fr")
            turn(NQ, 0, "r")

        block = ctx.enter_context(nc.Block())

        @block.sync
        def _(sp):
            def ln_row(g):
                return T["x"][bass.ds(g * P, P), :]

            def load_cx(g, s):
                sp.dma_start(cx[s][:, :, :, :], T["cx"][:, bass.ds(g * GB, GB), :, :]).then_inc(d_cx[s], 16)

            def load_vb(g, s):
                for j in range(4):
                    src = vlast_scr[bass.ds(g * GB, GB), 64 * j:64 * j + 64].partition_broadcast(L)
                    sp.dma_start(vb[s][32 * j:32 * j + 32, :, :], src).then_inc(d_vb[s], 16)

            def load(t, name, done):
                sp.dma_start(t[tuple(slice(None) for _ in t.shape)], T[name]).then_inc(done, 16)

            def zero_rows(g):
                sp.dma_start(xs_scr[bass.ds(g * XROWS, XROWS), :].rearrange("(p s) d -> p s d", s=2),
                             xm[0:XROWS // 2, 0:2, :]).then_inc(d_zero, 16)

            def load_raw(c):
                sp.dma_start(raw[:, PIECES[c]], T["we"][0, :, PIECES[c]]).then_inc(d_w, 16)

            sp.dma_start(x_in[0][:, :], ln_row(0)).then_inc(d_xin[0], 16)
            for t, name in consts[:5]:
                load(t, name, d_const)
            load_cx(0, 0)
            for t, name in consts[5:]:
                load(t, name, d_const)
            for t, name in vectors:
                load(t, name, d_vec)
            for t, name in rows:
                sp.dma_start(t[:, :], T[name].partition_broadcast(P)).then_inc(d_const, 16)
            sp.dma_start(x_in[1][:, :], ln_row(1)).then_inc(d_xin[1], 16)
            load_cx(1, 1)
            sp.wait_ge(vl_ev, 1)
            sp.dma_start(vlast_scr, vlast[:, :]).then_inc(d_vlast, 16)
            sp.wait_ge(d_vlast, 16)
            load_vb(0, 0)

            def slot(g, s, first, last):
                if not last:
                    at_least(sp, ol_ok, GB * g)
                    load_vb(g + 1, 1 - s)
                if isinstance(g, int) and g + 2 >= NG:
                    pass
                elif not last:
                    sp.wait_ge(xn_ok, g + 1)
                    sp.dma_start(x_in[s][:, :], ln_row(g + 2)).then_inc(d_xin[s], 16)
                at_least(sp, xsum_ok, g - 1)
                sp.dma_start(x_res[s][:, :], ln_row(g)).then_inc(d_xres[s], 16)
                if not (isinstance(g, int) and g + 2 >= NG):
                    sp.wait_ge(cl_ok, GB * g + GB)
                    load_cx(g + 2, s)
                if not first:
                    store_x1(g - 1, 1 - s)

            def store_x1(g, s):
                sp.wait_ge(x1o_ok, g + 1)
                sp.dma_start(x1_scr[bass.ds(g * P, P), :], x1o[s][:, :]).then_inc(d_x1[s], 16)
                zero_rows(g)

            def load_x1(g0, g1, stored):
                for i in range(2):
                    sp.wait_ge(d_x1[i], 16 * ((stored + 1 - i) // 2))
                rows = slice(g0 * GB, g1 * GB)
                sp.dma_start(xall[rows, :, :], x1_scr.rearrange("(b t) d -> b t d", b=B)[rows, :, :]).then_inc(d_x, 16)

            slot(0, 0, True, False)
            for t, name in early:
                load(t, name, d_ff)
            sp.dma_start(rb[:, :], T["rb"].partition_broadcast(P)).then_inc(d_ff, 16)
            sp.wait_ge(z_ok, 1)
            for k0, k1, g0, g1 in ((0, 5, 0, 8), (5, 10, 8, 18), (10, NG // 2 - 2, 18, 26)):
                with sp.Fori(k0, k1) as k:
                    slot(k * 2 + 1, 1, False, False)
                    slot(k * 2 + 2, 0, False, False)
                load_x1(g0, g1, 2 * k1)
            slot(NG - 3, 1, False, False)
            sp.wait_ge(wl_ok, 2)
            sp.wait_ge(d_vlast, 16)
            for c in range(WP):
                load_raw(c)
            slot(NG - 2, 0, False, False)
            slot(NG - 1, 1, False, True)
            store_x1(NG - 1, 1)
            load_x1(26, NG, NG)
            sp.wait_ge(d_x1[0], 16 * NG // 2)
            sp.wait_ge(d_x1[1], 16 * NG // 2)

            sp.wait_ge(out_mm, NG)
            sp.wait_ge(x1o_ok, NG)
            for t, name in late:
                load(t, name, d_ff)
            sp.wait_ge(fl_ok, 2)
            for t, name in moec:
                load(t, name, d_mc)
            for t, name in moer:
                sp.dma_start(t[:, :], T[name].partition_broadcast(P)).then_inc(d_mc, 16)
            with sp.Fori(0, NQ) as q:
                sp.wait_ge(x2_ok, q + 1)
                sp.dma_start(out.rearrange("(b t) d -> b t d", b=B)[:, bass.ds(q * 2, 2), :],
                             xall[:, bass.ds(q * 2, 2), :]).then_inc(d_out, 16)
            sp.wait_ge(w0l_ok, 1)
            for c in range(WP):
                sp.dma_start(raw[:, PIECES[c]], T["we"][1, :, PIECES[c]]).then_inc(d_w, 16)

            def load_xs(sl, i):
                sp.dma_start(xs[i][:, :], xs_scr[bass.ds(sl * P, P), :]).then_inc(d_xs[i], 16)

            sp.wait_ge(d_sort, 16 * NT)
            load_xs(0, 0)
            load_xs(1, 1)

            def sstep(sl, i, first, last):
                if not (isinstance(sl, int) and sl + 2 >= NS):
                    sp.wait_ge(xsT_mm, sl + 1)
                    sp.wait_ge(aux_ok, sl + 1)
                    load_xs(sl + 2, i)
                sp.wait_ge(y_ok, 2 * sl + 2)
                sp.dma_start(ys_scr[bass.ds(sl * P, P), :], ys[i][:, :]).then_inc(d_ys[i], 16)

            tiles_of_experts(sp, sstep)
            sp.wait_ge(d_out, 16 * NQ)

        @block.tensor
        def _(pe):
            def k_half(b, bs, half):
                if half == 0:
                    pe.wait_ge(cl_ok, b + 1)
                    at_least(pe, kl_ok, 2 * b)
                else:
                    at_least(pe, v_ev, b)
                dst = kv_bank[(b_par(bs) + half) % 2]
                for n, (x, w) in enumerate(SPLIT):
                    for k in range(2):
                        last = pe.matmul(dst[:, 0:MP], wk_s[w][:, k, half * P:half * P + P], cx_s[bs][x][:, k, :],
                                         start=(n + k == 0), stop=(n + k == 3))
                last.then_inc(kv_mm, 1)

            def b_par(bs):
                return (3 * bs) % 2

            def v_unit(b, bs):
                at_least(pe, kl_ok, 2 * b + 1)
                dst = kv_bank[b_par(bs)]
                for t in range(2):
                    for n, (x, w) in enumerate(SPLIT):
                        for k in range(2):
                            last = pe.matmul(dst[:, t * D:t * D + D], cx_s[bs][x][:, k, t * P:t * P + P],
                                             wv_s[w][:, k, :], start=(n + k == 0), stop=(n + k == 3))
                last.then_inc(kv_mm, 1)

            def scores(b, bs, gr):
                if gr == 0:
                    pe.wait_ge(qbd_ok, b + 1)
                if gr % 2 == 0:
                    pe.wait_ge(kl_ok, 2 * b + gr // 2 + 1)
                at_least(pe, p_ex, 4 * b + gr - 1)
                r = slice(64 * (gr % 2), 64 * (gr % 2) + 64)
                for n, (x, w) in enumerate(SPLIT):
                    ins = pe.matmul(s_bank[gr % 2][:, 0:MP], qbd[bs][x][r, gr // 2, :], kT[bs][w][r, gr // 2, :],
                                    start=(n == 0), stop=(n == 2))
                ins.then_inc(s_mm, 1)

            def prob_transpose(b, bs):
                pe.wait_ge(p_ex, 4 * b + 4)
                for t in range(2):
                    at_least(pe, (pT0_ev, pT1_ev)[t], b)
                    for gr in range(4):
                        last = pe.transpose(pT_bank[t][:, gr * P:gr * P + P],
                                            prob[bs][:, gr, t * P:t * P + P], ident[:, :])
                    last.then_inc(pT_mm, 1)

            def attend(b, bs):
                pe.wait_ge(pT0_ev, b + 1)
                pe.wait_ge(pT1_ev, b + 1)
                pe.wait_ge(v_ev, b + 1)
                at_least(pe, o_ev, b)
                for gr in range(4):
                    for t in range(2):
                        last = pe.matmul(o_bank[:, gr * 64:gr * 64 + 64], probT[:, t, gr * P:gr * P + P],
                                         v[bs][:, t, gr * 64:gr * 64 + 64], start=(t == 0), stop=(t == 1))
                last.then_inc(o_mm, 1)

            def x_transpose(g, s):
                pe.wait_ge(xn_ok, g + 1)
                at_least(pe, xsum_ok, g - 2)
                for k in range(2):
                    last = pe.transpose(x_bank[:, k * P:k * P + P], xn[s][:, k * P:k * P + P], ident[:, :])
                last.then_inc(xT_mm, 1)

            def o_transpose(g, s):
                for u in range(GB):
                    last = pe.transpose(x_bank[0:64, u * P:u * P + P], on[s][:, u, :], ident[:, :])
                last.then_inc(oT_mm, 1)

            def q_project(g, s):
                pe.wait_ge(xT_ev, g + 1)
                for half in range(2):
                    for k in range(2):
                        last = pe.matmul(x_bank[:, half * P:half * P + P], wq[:, k, half * P:half * P + P],
                                         xnT[s][:, k, :], start=(k == 0), stop=(k == 1))
                last.then_inc(q_mm, 1)

            def o_project(g, s):
                pe.wait_ge(oT_ev, g + 1)
                for j in range(2):
                    last = pe.matmul(x_bank[:, 0:D], oT[s][:, j, :, :], wo[:, j, :], start=(j == 0), stop=(j == 1))
                last.then_inc(out_mm, 1)

            pe.wait_ge(d_const, CONST)
            for k in range(2):
                last = pe.matmul(x_bank[:, 0:D], cxl[:, k, :], wvl[:, k, :], start=(k == 0), stop=(k == 1))
            last.then_inc(vl_mm, 1)
            pe.wait_ge(vl_ev, 1)
            x_transpose(0, 0)
            pe.wait_ge(pad_ok, 4)
            pe.wait_ge(wl_ok, 2)
            k_half(0, 0, 0)
            k_half(0, 0, 1)
            v_unit(0, 0)
            q_project(0, 0)

            def slot(g, s, first, last):
                for u in range(GB):
                    b = g * GB + u
                    nxt = not (last and u == GB - 1)
                    bs, bs1 = u % 2, (u + 1) % 2
                    if nxt:
                        k_half(b + 1, bs1, 0)
                    scores(b, bs, 0)
                    scores(b, bs, 1)
                    if not (first and u == 0):
                        attend(b - 1, bs1)
                    scores(b, bs, 2)
                    scores(b, bs, 3)
                    if nxt:
                        k_half(b + 1, bs1, 1)
                        v_unit(b + 1, bs1)
                    prob_transpose(b, bs)
                    if u == 0 and not last:
                        x_transpose(g + 1, 1 - s)
                    if u == 1 and not first:
                        alone(pe, (xT_ev, 0 if last else g + 2), (on_ok, GB * g))
                        o_transpose(g - 1, 1 - s)
                    if u == 2 and not last:
                        if not first:
                            pe.wait_ge(oT_ev, g)
                        q_project(g + 1, 1 - s)
                    if u == 3 and not first:
                        if not last:
                            pe.wait_ge(ql_ok, g + 2)
                        o_project(g - 1, 1 - s)

            slots(pe, slot)
            attend(B - 1, (B - 1) % 2)
            pe.wait_ge(xsum_ok, NG - 1)
            pe.wait_ge(on_ok, B)
            o_transpose(NG - 1, (NG - 1) % 2)
            o_project(NG - 1, (NG - 1) % 2)

            pe.wait_ge(d_ff, FFW)

            def transposes(src, done):
                for k in range(2):
                    for i in range(2):
                        c = (2 * k + i) * P
                        ins = pe.transpose(t_bank[:, c:c + P], src[:, i, k * P:k * P + P], ident[:, :])
                ins.then_inc(done, 1)

            def drives(t, i):
                at_least(pe, gc_ev, t)
                for w in range(2):
                    for c, (m, k) in enumerate(((0, 0), (1, 0), (1, 1), (2, 1))):
                        ins = pe.matmul(gc_bank[w][:, m * P:m * P + P], gw[w][:, c, :], xrT[:, k, i, :],
                                        start=(c in (0, 1, 3)), stop=(c in (0, 2, 3)))
                ins.then_inc(gc_mm, 1)

            def unit_out(Q):
                pe.wait_ge(h_ok, Q * 2 + 2)
                for i in range(2):
                    for m, a, b in ((1, 0, 2), (0, 0, 1), (2, 1, 2)):
                        ins = pe.matmul(r_bank[:, i * D + a * P:i * D + b * P], hT[i][:, m, :], ow[:, m, a * P:b * P],
                                        start=(m == 1), stop=(m == 2))
                ins.then_inc(gru_mm, 1)

            def route(Q):
                pe.wait_ge(xmT_ev, Q + 1)
                for i in range(2):
                    for k in range(2):
                        ins = pe.matmul(r_bank[:, i * NE:i * NE + NE], xmT[:, k, i, :], rw[:, k, :],
                                        start=(k == 0), stop=(k == 1))
                ins.then_inc(rt_mm, 1)

            def gate_up(q, par, f):
                if f == 0:
                    pe.wait_ge(fnl_ok, q + 1)
                at_least(pe, prod_ok, NF * q + f - 2)
                for h, w_s in enumerate((fg_s, fu_s)):
                    for n, (x, w) in enumerate(SPLIT):
                        for k in range(2):
                            ins = pe.matmul(gu_bank[f % 3][0:FW[f], h * 2 * P:(h + 1) * 2 * P],
                                            w_s[w][:, k, f * P:f * P + FW[f]], fnT[par][x][:, k, :, :],
                                            start=(n + k == 0), stop=(n + k == 3))
                ins.then_inc(gu_mm, 1)

            def down(q):
                pe.wait_ge(prod_ok, NF * q + NF - 1)
                at_least(pe, x2_ok, q)
                for i in range(2):
                    for f in range(NF):
                        if i == 0 and f == NF - 1:
                            pe.wait_ge(prod_ok, NF * q + NF)
                        ins = pe.matmul(fd_bank[:, i * D:i * D + D], fT[0:FW[f], f, i, :], fd[0:FW[f], f, :],
                                        start=(f == 0), stop=(f == NF - 1))
                ins.then_inc(fd_mm, 1)

            def turn(q, par, parts):
                f, o, n, r = (c in parts for c in "fonr")
                if n:
                    pe.wait_ge(xr_ok, q * 2 + 6)
                    at_least(pe, xrT_ev, q + 2)
                    at_least(pe, fnl_ok, q + 1)
                    transposes(xr, xrT_mm)
                if f:
                    if isinstance(q, int) and q == 0:
                        pe.wait_ge(fl_ok, 2)
                    gate_up(q, par, 0)
                if n:
                    pe.wait_ge(xrT_ev, q + 3)
                    drives(q * 2 + 4, 0)
                if o:
                    at_least(pe, rt_ok, q - 1)
                    at_least(pe, xa_ok, q + 1)
                    unit_out(q + 1)
                if f:
                    gate_up(q, par, 1)
                if r:
                    pe.wait_ge(xm_ok, q * 2)
                    if n:
                        pe.wait_ge(xrT_ev, q + 3)
                    else:
                        pe.wait_ge(fnl_ok, min(q + 1, NQ))
                        pe.wait_ge(xmT_ev, q - 1)
                    transposes(xmt, xmT_mm)
                if f:
                    gate_up(q, par, 2)
                if n:
                    drives(q * 2 + 5, 1)
                if r:
                    if o:
                        pe.wait_ge(xa_ok, q + 2)
                    else:
                        pe.wait_ge(rt_ok, q - 1)
                    route(q - 1)
                if f:
                    gate_up(q, par, 3)
                if o:
                    pe.wait_ge(fn_ok, q * 2 + 4)
                    if r:
                        pe.wait_ge(xmT_ev, q)
                    else:
                        pe.wait_ge(xrT_ev, q + 3)
                    transposes(fn, fnT_mm)
                if f:
                    gate_up(q, par, 4)
                    gate_up(q, par, 5)
                    down(q)

            turns(pe, turn)

            pe.wait_ge(d_mc, MOEC)
            pe.wait_ge(route_ok, 1)
            pe.wait_ge(oneh_ok, 1)
            pe.matmul(bank[4][:, 0:NT * NE], lt[:, :], oneh[:, :], start=True, stop=True)
            pe.matmul(bank[5][:, 0:NT * NE], ones[:, :], oneh[:, :], start=True, stop=True).then_inc(rank_mm, 1)
            pe.wait_ge(tab_ok, 2)

            def xs_transpose(sl, i):
                pe.wait_ge(d_xs[i], (sl - i) * 8 + 16)
                at_least(pe, xsTl_ok, sl)
                for k in range(2):
                    ins = pe.transpose(xs_bank[:, k * P:k * P + P], xs[i][:, k * P:k * P + P], ident[:, :])
                ins.then_inc(xsT_mm, 1)

            def hidden(sl, i, half, par):
                at_least(pe, hid_ok, 2 * sl + half - 1)
                for b_, o in ((a_bank, 0), (g_bank, FF)):
                    for n, (x, w) in enumerate(SPLIT):
                        for k in range(2):
                            c = k * 2 * FF + o + half * 512
                            ins = pe.matmul(b_[half][:, :], xsT[i][x][:, k, :],
                                            wsplit[:, bass.ds(par, 1), w, c:c + 512],
                                            start=(n + k == 0), stop=(n + k == 3))
                ins.then_inc(ag_mm, 1)

            def hid_transpose(sl, half):
                pe.wait_ge(hid_ok, 2 * sl + half + 1)
                at_least(pe, hTl_ok, 2 * sl + half - 1)
                for f in range(4):
                    ins = pe.transpose(hT_bank[half][:, f * P:f * P + P], hid[half][:, f * P:f * P + P], ident[:, :])
                ins.then_inc(hT_mm, 1)

            def expert_down(sl, par):
                at_least(pe, y_ok, 2 * sl)
                pe.wait_ge(hTl_ok, 2 * sl + 2)
                for n, (x, w) in enumerate(SPLIT):
                    for f in range(FT):
                        c = 4 * FF + f * D
                        ins = pe.matmul(y_bank[:, 0:D], hidT[f // 4][x][:, f % 4, :],
                                        wsplit[:, bass.ds(par, 1), w, c:c + D],
                                        start=(n == 0 and f == 0), stop=(n == 2 and f == FT - 1))
                ins.then_inc(y_mm, 1)

            def expert(sl):
                return pe.value_load(expi[0:1, bass.ds(sl, 1)], min_val=0, max_val=NE - 1)

            pe.sem_inc(y_mm, 1)
            xs_transpose(0, 0)

            def estep(sl, i, first, last):
                e = expert(sl)
                par = e % 2
                pe.wait_ge(w_ready, e + 1)
                pe.wait_ge(xsTl_ok, sl + 1)
                hidden(sl, i, 0, par)
                if not first:
                    hid_transpose(sl - 1, 1)
                hidden(sl, i, 1, par)
                if not last:
                    xs_transpose(sl + 1, 1 - i)
                if not first:
                    expert_down(sl - 1, expert(sl - 1) % 2)
                hid_transpose(sl, 0)

            tiles_of_experts(pe, estep)
            hid_transpose(NS - 1, 1)
            expert_down(NS - 1, expert(NS - 1) % 2)

        @block.scalar
        def _(act):
            def k_copy(b, bs, half):
                act.wait_ge(kv_mm, 3 * b + half + 1)
                src = kv_bank[((3 * bs) % 2 + half) % 2]
                act.activation(kT[bs][0][:, half, :], src[:, 0:MP], ACT.Identity,
                               bias=bk[:, half:half + 1]).then_inc(k_ev, 1)

            def exp(b, bs, gr):
                if gr == 0:
                    at_least(act, ol_ok, b - 1)
                    at_least(act, rinv_ok, b - 1)
                act.wait_ge(mx, 4 * b + gr + 1)
                act.activation(prob[bs][:, gr, :], s_bank[gr % 2][:, 0:M], ACT.Exp, bias=negmax[bs][:, gr:gr + 1],
                               accum_out=rowsum[bs][:, gr:gr + 1]).then_inc(p_ex, 1)

            def ctx_high(b, G, s, u, bs):
                if u == 0:
                    act.wait_ge(d_cx[s], (G - s) * 8 + 16)
                at_least(act, kv_mm, 3 * (b - 1))
                act.activation(cx_s[bs][0][:, :, 0:M], cx[s][:, u, :, :], ACT.Identity).then_inc(ch_ok, 1)

            act.wait_ge(d_const, CONST)
            for w, w_s in ((wk, wk_s), (wv, wv_s)):
                act.activation(w_s[0][:, :, :], w[:, :, :], ACT.Identity).then_inc(wh_ok, 1)
            ctx_high(0, 0, 0, 0, 0)
            ctx_high(1, 0, 0, 1, 1)
            act.wait_ge(xT_mm, 1)
            act.activation(xnT[0][:, :, :], x_bank[:, 0:2 * P].rearrange("p (k t) -> p k t", k=2),
                           ACT.Identity).then_inc(xT_ev, 1)
            k_copy(0, 0, 0)
            k_copy(0, 0, 1)

            def q_copy(g, s):
                act.wait_ge(q_mm, g + 1)
                at_least(act, qbd_ok, GB * (g - 1))
                for half in range(2):
                    ins = act.activation(qT[s][0][:, half, :], x_bank[:, half * P:half * P + P], ACT.Identity,
                                         bias=bq[:, half:half + 1])
                ins.then_inc(q_ev, 1)

            q_copy(0, 0)

            def slot(g, s, first, last):
                for u in range(GB):
                    b = g * GB + u
                    nxt = not (last and u == GB - 1)
                    bs, bs1 = u % 2, (u + 1) % 2
                    if nxt:
                        k_copy(b + 1, bs1, 0)
                    exp(b, bs, 0)
                    exp(b, bs, 1)
                    if not (last and u >= 2):
                        ctx_high(b + 2, g + u // 2, s if u < 2 else 1 - s, (u + 2) % GB, bs)
                    exp(b, bs, 2)
                    exp(b, bs, 3)
                    if nxt:
                        k_copy(b + 1, bs1, 1)
                    act.wait_ge(pT_mm, 2 * b + 1)
                    at_least(act, o_mm, b)
                    act.activation(probT[:, 0, :], pT_bank[0][:, :], ACT.Identity).then_inc(pT0_ev, 1)
                    if u == 0 and not last:
                        act.wait_ge(xT_mm, g + 2)
                        act.activation(xnT[1 - s][:, :, :], x_bank[:, 0:2 * P].rearrange("p (k t) -> p k t", k=2),
                                       ACT.Identity).then_inc(xT_ev, 1)
                    if u == 1 and not first:
                        o_copy(g - 1, 1 - s)
                    if u == 2 and not last:
                        q_copy(g + 1, 1 - s)

            def o_copy(g, s):
                act.wait_ge(oT_mm, g + 1)
                x = x_bank[0:64, :].rearrange("p (u h j l) -> p h u j l", u=GB, h=2, j=2)
                for h in range(2):
                    ins = act.activation(oT[s][64 * h:64 * h + 64, :, :, :].rearrange("p j u l -> p u j l"),
                                         x[:, h, :, :, :], ACT.Identity)
                ins.then_inc(oT_ev, 1)

            slots(act, slot)
            o_copy(NG - 1, (NG - 1) % 2)

            act.wait_ge(d_ff, FFW)
            act.wait_ge(be_ok, 3)

            def square_sum(c, i, dst, src, need, Q, free, taken, done):
                alone(act, (need, Q * 2 + i + 1 if c == "A" else Q + 1), (free, Q), (taken, Q))
                act.activation(dst[:, i, :], src, ACT.Square,
                               accum_out=small["ss" + c][:, i:i + 1]).then_inc(done, 1)

            def scaled(dst, i, src, col, need, Q, done):
                alone(act, (need, Q + 1))
                act.activation(dst[:, i, :], src, ACT.Identity, scale=col[:, i:i + 1]).then_inc(done, 1)

            def gamma_copy(dst, g, mm, Q, done):
                act.wait_ge(mm, Q + 1)
                for k in range(2):
                    ins = act.activation(dst[:, k, :, :], t_bank[:, 2 * k * P:2 * (k + 1) * P].rearrange(
                        "p (i b) -> p i b", i=2), ACT.Identity, scale=gam1[g][:, k:k + 1])
                ins.then_inc(done, 1)

            def silu(q, f):
                act.wait_ge(gu_mm, NF * q + f + 1)
                at_least(act, prod_ok, NF * q + f - 1)
                act.activation(sg[f % 2][0:FW[f], :], gu_bank[f % 3][0:FW[f], 0:2 * P], ACT.Silu).then_inc(silu_ok, 1)

            def drive_copy(t, i):
                act.wait_ge(gc_mm, t + 1)
                at_least(act, pot_ok, t - 1)
                for w in range(2):
                    ins = act.activation(gc[i][:, 3 * w:3 * w + 3, :],
                                         gc_bank[w][:, 0:3 * P].rearrange("p (m b) -> p m b", m=3), ACT.Identity)
                ins.then_inc(gc_ev, 1)

            def route_copy(Q):
                act.wait_ge(xmT_mm, Q + 1)
                at_least(act, rt_mm, Q)
                act.activation(xmT[:, :, :, :], t_bank[:, :].rearrange("p (k i b) -> p k i b", k=2, i=2),
                               ACT.Identity).then_inc(xmT_ev, 1)

            def turn(q, par, parts):
                f, o, n, m, r = (c in parts for c in "fonmr")
                if n:
                    at_least(act, gc_mm, q * 2 + 4)
                    gamma_copy(xrT, 0, xrT_mm, q + 2, xrT_ev)
                if f:
                    silu(q, 0)
                if n:
                    drive_copy(q * 2 + 4, 0)
                if f:
                    silu(q, 1)
                if o:
                    for i in range(2):
                        square_sum("B", i, fn, xa[:, i, :], xa_ok, q + 1, smB_ok, fnT_mm, ssB_ok)
                if r:
                    route_copy(q - 1)
                if f:
                    silu(q, 2)
                if o:
                    for i in range(2):
                        scaled(fn, i, xa[:, i, :], small["scB"], scB_ok, q + 1, fn_ok)
                if n:
                    drive_copy(q * 2 + 5, 1)
                if m:
                    for i in range(2):
                        square_sum("A", i, xr, xm[:, q * 2 + 6 + i, 0:D], xl_ok, q + 3, smA_ok, xrT_mm, ssA_ok)
                if f:
                    silu(q, 3)
                if o:
                    at_least(act, gu_mm, NF * q)
                    gamma_copy(fnT[1 - par][0], 1, fnT_mm, q + 1, fnT_ev)
                if f:
                    silu(q, 4)
                    silu(q, 5)
                if m:
                    for i in range(2):
                        scaled(xr, i, xm[:, q * 2 + 6 + i, 0:D], small["scA"], scA_ok, q + 3, xr_ok)
                if parts == "m":
                    for w, w_s in ((fg, fg_s), (fu, fu_s)):
                        act.activation(w_s[0][:, :, :], w[:, :, :], ACT.Identity).then_inc(fh_ok, 1)

            turns(act, turn)

            act.wait_ge(lsh_ok, 1)
            act.activation(lex[:, :], lsh[:, :], ACT.Exp).then_inc(lex_ok, 1)
            act.wait_ge(d_w, 16 * WP)
            act.wait_ge(fd_mm, NQ)
            act.activation(wsplit[:, 0, 0, :], raw[:, :], ACT.Identity).then_inc(w0_ok, 1)

            def astep(sl, i, first, last):
                silu_half(sl, 0)
                if not first:
                    hT_high(sl - 1, 1)
                silu_half(sl, 1)
                if not last:
                    xs_high(sl + 1, 1 - i)
                hT_high(sl, 0)

            def silu_half(sl, half):
                act.wait_ge(ag_mm, 2 * sl + half + 1)
                at_least(act, hid_ok, 2 * sl + half - 1)
                act.activation(sa[half][:, :], a_bank[half][:, :], ACT.Silu).then_inc(sa_ok, 1)

            def hT_high(sl, half):
                act.wait_ge(hT_mm, 2 * sl + half + 1)
                act.wait_ge(y_mm, sl + 1)
                act.activation(hidT[half][0][:, :, :], hT_bank[half][:, :].rearrange("p (f b) -> p f b", f=4),
                               ACT.Identity).then_inc(hT_ev, 1)

            def xs_high(sl, i):
                act.wait_ge(xsT_mm, sl + 1)
                at_least(act, ag_mm, 2 * (sl - 1))
                act.activation(xsT[i][0][:, :, :], xs_bank[:, 0:2 * P].rearrange("p (k b) -> p k b", k=2),
                               ACT.Identity).then_inc(xsT_ev, 1)

            xs_high(0, 0)
            tiles_of_experts(act, astep)
            hT_high(NS - 1, 1)

        @block.vector
        def _(dve):
            def norm_stats(g, s):
                dve.wait_ge(d_xin[s], loads(g, s))
                at_least(dve, mv_ok, g - 1)
                dve.bn_stats(stats[s][:, :], x_in[s][:, :]).then_inc(st_ok, 1)
                alone(dve, (st_ok, g + 1))
                dve.bn_aggr(mv[s][:, :], stats[s][:, :]).then_inc(mv_ok, 1)

            def loads(g, s):
                return (g - s) * 8 + 16

            def norm_apply(g, s):
                dve.wait_ge(rstd_ok, g + 1)
                at_least(dve, xT_mm, g - 1)
                dve.tensor_scalar(xn[s][:, :], x_in[s][:, :], mv[s][:, 0:1], rstd[s][:, 0:1],
                                  ALU.subtract, ALU.mult).then_inc(xn_ok, 1)

            def v_copy(b, bs):
                dve.wait_ge(kv_mm, 3 * b + 3)
                dve.tensor_tensor(v[bs][:, :, :], kv_bank[(3 * bs) % 2][:, :].rearrange("p (t n) -> p t n", t=2),
                                  spread(bv[:, :], 1, 2), ALU.add).then_inc(v_ev, 1)

            def k_low(b, bs, half):
                dve.wait_ge(k_ev, 2 * b + half + 1)
                dve.scalar_tensor_tensor(kT[bs][1][:, half, :], kv_bank[((3 * bs) % 2 + half) % 2][:, 0:MP],
                                         bk[:, half:half + 1], kT[bs][0][:, half, :].bitcast(F32),
                                         ALU.add, ALU.subtract).then_inc(kl_ok, 1)

            def q_low(g, s):
                dve.wait_ge(q_ev, g + 1)
                for half in range(2):
                    ins = dve.scalar_tensor_tensor(qT[s][1][:, half, :], x_bank[:, half * P:half * P + P],
                                                   bq[:, half:half + 1], qT[s][0][:, half, :].bitcast(F32),
                                                   ALU.add, ALU.subtract)
                ins.then_inc(ql_ok, 1)

            def take_out(b, bs):
                dve.wait_ge(p_ex, 4 * b + 4)
                at_least(dve, on_ok, b - 1)
                dve.reciprocal(rinv[bs][:, :], rowsum[bs][:, :]).then_inc(rinv_ok, 1)
                dve.wait_ge(o_mm, b + 1)
                dve.wait_ge(ol_ok, b + 1)
                for j in range(4):
                    q = slice(32 * j, 32 * j + 32)
                    ins = dve.tensor_tensor(
                        oraw[bs][q, :, :], o_bank[q, 0:D].rearrange("p (g n) -> p g n", g=4)[:, :, 16 * j:16 * j + 16],
                        olast[bs][q, :, :], ALU.add)
                ins.then_inc(o_ev, 1)

            def out_sum(g, s):
                dve.wait_ge(out_mm, g + 1)
                dve.wait_ge(d_xres[s], loads(g, s))
                at_least(dve, x1o_ok, g)
                dve.tensor_tensor(xsum[s][:, :], x_bank[:, 0:D], x_res[s][:, :], ALU.add).then_inc(xsum_ok, 1)

            norm_stats(0, 0)
            norm_apply(0, 0)
            dve.wait_ge(d_const, CONST)
            for n, (w, w_s) in enumerate(((wk, wk_s), (wv, wv_s))):
                dve.wait_ge(wh_ok, n + 1)
                dve.tensor_tensor(w_s[1][:, :, :], w[:, :, :], w_s[0][:, :, :].bitcast(F32),
                                  ALU.subtract).then_inc(wl_ok, 1)
            dve.wait_ge(vl_mm, 1)
            dve.tensor_tensor(vlast[:, :], x_bank[:, 0:D], bvl[:, :], ALU.add).then_inc(vl_ev, 1)
            norm_stats(1, 1)
            norm_apply(1, 1)
            k_low(0, 0, 0)
            k_low(0, 0, 1)
            v_copy(0, 0)
            q_low(0, 0)

            def slot(g, s, first, last):
                final = last or (isinstance(g, int) and g + 2 >= NG)
                for u in range(GB):
                    b = g * GB + u
                    nxt = not (last and u == GB - 1)
                    bs, bs1 = u % 2, (u + 1) % 2
                    if nxt:
                        k_low(b + 1, bs1, 0)
                    for gr in range(4):
                        dve.wait_ge(s_mm, 4 * b + gr + 1)
                        if gr == 0:
                            at_least(dve, p_ex, 4 * (b - 1))
                        dve.tensor_reduce(negmax[bs][:, gr:gr + 1], s_bank[gr % 2][:, 0:M], AXX, ALU.max,
                                          negate=True).then_inc(mx, 1)
                    if not (first and u == 0):
                        take_out(b - 1, bs1)
                    if nxt:
                        k_low(b + 1, bs1, 1)
                        v_copy(b + 1, bs1)
                    dve.wait_ge(pT_mm, 2 * b + 2)
                    at_least(dve, o_mm, b)
                    dve.tensor_copy(probT[:, 1, :], pT_bank[1][:, :]).then_inc(pT1_ev, 1)
                    if u == 1 and not final:
                        norm_stats(g + 2, s)
                    if u == 2 and not last:
                        q_low(g + 1, 1 - s)
                    if u == 2 and not final:
                        norm_apply(g + 2, s)
                    if u == 3 and not first:
                        out_sum(g - 1, 1 - s)

            slot(0, 0, True, False)
            with dve.Fori(0, NG // 2 - 2) as k:
                slot(k * 2 + 1, 1, False, False)
                slot(k * 2 + 2, 0, False, False)
            slot(NG - 3, 1, False, False)
            slot(NG - 2, 0, False, False)
            slot(NG - 1, 1, False, True)
            take_out(B - 1, (B - 1) % 2)
            out_sum(NG - 1, (NG - 1) % 2)

            dve.wait_ge(x1o_ok, NG)
            dve.wait_ge(d_x, 16 * 4)
            dve.wait_ge(d_zero, 16 * NG)
            dve.memset(mem[:, :, :], 0.0).then_inc(c2, 1)
            dve.wait_ge(be_ok, 1)
            dve.reciprocal(beta[:, :], beta[:, :]).then_inc(c2, 1)
            dve.wait_ge(be_ok, 4)
            dve.wait_ge(c2, 2)

            def stats_of(c, i, src, Q, st_ok_, mv_ok_, rs_ok_, used):
                alone(dve, (mv_ok_, Q * 2))
                dve.bn_stats(st[c][i][:, :], src).then_inc(st_ok_, 1)
                alone(dve, (st_ok_, Q * 2 + i + 1), (rs_ok_, Q), (used, Q * 2))
                dve.bn_aggr(mv2[c][:, i, :], st[c][i][:, :]).then_inc(mv_ok_, 1)

            def potential(t, i):
                dve.wait_ge(gc_ev, t + 1)
                at_least(dve, mem_ok, t)
                for m in range(6):
                    ins = dve.scalar_tensor_tensor(mem[:, m, :], mem[:, m, :], beta[:, m:m + 1], gc[i][:, m, :],
                                                   ALU.mult, ALU.add)
                ins.then_inc(pot_ok, 1)
                dve.wait_ge(pot_ok, t + 1)
                at_least(dve, zc_ok, t - 1)
                dve.tensor_scalar(spk[i][:, :, :], mem[:, :, :], ROUND, ROUND, ALU.add, ALU.subtract).then_inc(rnd_ok, 1)

            def spikes(t, i):
                dve.wait_ge(rnd_ok, t + 1)
                dve.tensor_scalar(spk[i][:, :, :], spk[i][:, :, :], -1.0, 1.0, ALU.max, ALU.min).then_inc(spk_ok, 1)

            def membrane(t, i):
                dve.wait_ge(spk_ok, t + 1)
                for m in range(6):
                    ins = dve.scalar_tensor_tensor(mem[:, m, :], spk[i][:, m, :], nthr[:, m:m + 1], mem[:, m, :],
                                                   ALU.mult, ALU.add)
                ins.then_inc(mem_ok, 1)

            def fn_low(Q, buf):
                dve.wait_ge(fnT_ev, Q + 1)
                for k in range(2):
                    ins = dve.scalar_tensor_tensor(
                        buf[1][:, k, :, :], t_bank[:, 2 * k * P:2 * (k + 1) * P].rearrange("p (i b) -> p i b", i=2),
                        gam1[1][:, k:k + 1], buf[0][:, k, :, :].bitcast(F32), ALU.mult, ALU.subtract)
                ins.then_inc(fnl_ok, 1)

            def prod(q, f):
                dve.wait_ge(silu_ok, NF * q + f + 1)
                dve.tensor_tensor(fT[0:FW[f], f, :, :].rearrange("p i b -> p (i b)"), gu_bank[f % 3][0:FW[f], 2 * P:4 * P],
                                  sg[f % 2][0:FW[f], :], ALU.mult).then_inc(prod_ok, 1)

            def unit_sum(Q):
                dve.wait_ge(gru_mm, Q + 1)
                dve.wait_ge(xl_ok, Q * 2 + 2)
                at_least(dve, add_ok, Q)
                at_least(dve, fn_ok, Q * 2)
                dve.tensor_tensor(xa[:, :, :], r_bank[:, :].rearrange("p (i d) -> p i d", i=2),
                                  xm[:, bass.ds(Q * 2, 2), 0:D], ALU.add).then_inc(xa_ok, 1)

            def logits_out(Q):
                dve.wait_ge(rt_mm, Q + 1)
                dve.tensor_tensor(logit[:, bass.ds(Q * 2, 2), :], r_bank[:, 0:2 * NE].rearrange("p (i e) -> p i e", i=2),
                                  spread(rb[:, :], 1, 2), ALU.add).then_inc(rt_ok, 1)

            def turn(q, par, parts):
                f, o, n, m, r = (c in parts for c in "fonmr")
                last = q * 2 - 2
                if m:
                    for i in range(2):
                        stats_of("A", i, xall[:, q * 2 + 6 + i, :], q + 3, stA_ok, mvA_ok, rsA_ok, xl_ok)
                if r:
                    dve.wait_ge(fd_mm, q)
                    dve.wait_ge(add_ok, q)
                    dve.tensor_tensor(xall[:, bass.ds(last, 2), :], fd_bank[:, :].rearrange("p (i d) -> p i d", i=2),
                                      xall[:, bass.ds(last, 2), :], ALU.add).then_inc(x2_ok, 1)
                    alone(dve, (x2_ok, q))
                    for i in range(2):
                        stats_of("B", i, xall[:, last + i, :], q - 1, stB_ok, mvB_ok, rsB_ok, xm_ok)
                if f:
                    prod(q, 0)
                if r:
                    for i in range(2):
                        dve.wait_ge(rsB_ok, q)
                        at_least(dve, xmT_mm, q - 1)
                        at_least(dve, xm_kept, q - 1)
                        dve.tensor_scalar(xmt[:, i, :], xall[:, last + i, :], mv2["B"][:, i, 0:1],
                                          small["rsB"][:, i:i + 1], ALU.subtract, ALU.mult).then_inc(xm_ok, 1)
                if n:
                    potential(q * 2 + 4, 0)
                if o:
                    unit_sum(q + 1)
                if f:
                    prod(q, 1)
                if n:
                    spikes(q * 2 + 4, 0)
                if m:
                    for i in range(2):
                        dve.wait_ge(rsA_ok, q + 4)
                        dve.tensor_scalar(xm[:, q * 2 + 6 + i, 0:D], xall[:, q * 2 + 6 + i, :], mv2["A"][:, i, 0:1],
                                          small["rsA"][:, i:i + 1], ALU.subtract, ALU.mult).then_inc(xl_ok, 1)
                if n:
                    membrane(q * 2 + 4, 0)
                if f:
                    prod(q, 2)
                if n:
                    potential(q * 2 + 5, 1)
                if f:
                    prod(q, 3)
                if n:
                    spikes(q * 2 + 5, 1)
                if f:
                    prod(q, 4)
                    prod(q, 5)
                if n:
                    membrane(q * 2 + 5, 1)
                if r:
                    logits_out(q - 1)
                if parts == "nm":
                    for n, (w, w_s) in enumerate(((fg, fg_s), (fu, fu_s))):
                        dve.wait_ge(fh_ok, n + 1)
                        dve.tensor_tensor(w_s[1][:, :, :], w[:, :, :], w_s[0][:, :, :].bitcast(F32),
                                          ALU.subtract).then_inc(fl_ok, 1)
                if o:
                    fn_low(q + 1, fnT[1 - par])

            turns(dve, turn)

            done = [0]

            def te_bank(b_):
                return b_[:, 0:NT * NE].rearrange("p (t e) -> p t e", e=NE)

            def one_col(n):
                return ones[:, 0:1].to_broadcast([P, n])

            def then(ins):
                done[0] += 1
                ins.then_inc(dv_chain, 1)
                dve.wait_ge(dv_chain, done[0])

            te = lambda a: a[:, :].rearrange("p (t e) -> p t e", e=NE)
            et = lambda a: a[:, :].rearrange("p (e t) -> p e t", e=NE)
            dve.wait_ge(d_mc, MOEC)
            dve.wait_ge(route_ok, 1)
            dve.wait_ge(rt_ok, NQ)
            dve.wait_ge(xm_kept, NQ)
            then(dve.tensor_reduce(lmax[:, :], logit[:, :, :], AXX, ALU.max))
            dve.tensor_tensor(te(lsh), logit[:, :, :], spread(lmax[:, :], 2, NE), ALU.subtract).then_inc(lsh_ok, 1)
            dve.wait_ge(lsh_ok, 1)
            then(dve.tensor_scalar(rank[:, :], lsh[:, :], 0.0, None, ALU.is_ge))
            then(dve.tensor_tensor(te(cum), te(rank), spread(descend[:, :], 1, NT), ALU.mult))
            then(dve.tensor_reduce(best[:, :], te(cum), AXX, ALU.max))
            dve.tensor_tensor(te(oneh), te(cum), spread(best[:, :], 2, NE), ALU.is_equal).then_inc(oneh_ok, 1)
            dve.wait_ge(lex_ok, 1)
            then(dve.tensor_reduce(lsum[:, :], te(lex), AXX, ALU.add))
            then(dve.reciprocal(maxp[:, :], lsum[:, :]))
            dve.wait_ge(rank_mm, 1)
            then(dve.tensor_copy(et(tot), te_bank(bank[5]).rearrange("p t e -> p e t")))
            then(dve.tensor_tensor_scan(cum[:, :], one_col(NT * NE), tot[:, :], 0.0, ALU.mult, ALU.add))
            then(dve.tensor_tensor(exc[:, :], cum[:, :], tot[:, :], ALU.subtract))
            then(dve.tensor_reduce(cnt[:, :], et(tot), AXX, ALU.add))
            then(dve.tensor_scalar(tlf[:, :], cnt[:, :], 1.0 / P, (P - 1) / P - 0.5 + 0.5 / P, ALU.mult, ALU.add))
            then(dve.tensor_scalar(tiles[:, :], tlf[:, :], ROUND, ROUND, ALU.add, ALU.subtract))
            then(dve.tensor_scalar(tiles[:, :], tiles[:, :], 1.0, None, ALU.max))
            then(dve.tensor_tensor_scan(ctile[:, :], one_col(NE), tiles[:, :], 0.0, ALU.mult, ALU.add))
            then(dve.tensor_tensor(base_e[:, :], ctile[:, :], tiles[:, :], ALU.subtract))
            then(dve.scalar_tensor_tensor(shift[:, :], base_e[:, :], float(P), et(exc)[:, :, 0], ALU.mult, ALU.subtract))
            then(dve.tensor_tensor(et(exc), et(exc), spread(shift[:, :], 2, NT), ALU.add))
            then(dve.tensor_tensor(te(rank), te_bank(bank[4]), et(exc).rearrange("p e t -> p t e"), ALU.add))
            then(dve.tensor_tensor(rank[:, :], rank[:, :], oneh[:, :], ALU.mult))
            then(dve.tensor_reduce(posf[:, :], te(rank), AXX, ALU.add))
            then(dve.tensor_copy(xm[:, :, D], maxp[:, :]))
            then(dve.tensor_copy(xm[:, :, D + 1], token[:, :]))
            dve.tensor_copy(pos[:, :], posf[:, :]).then_inc(pos_ok, 1)
            then(dve.tensor_tensor(cmp7[:, :, :], spread(slotno[:, :], 2, NE - 1), spread(ctile[:, 0:NE - 1], 1, NS), ALU.is_ge))
            then(dve.tensor_reduce(expf[:, :], cmp7[:, :, :], AXX, ALU.add))
            dve.tensor_copy(expi[:, :], expf[:, :]).then_inc(tab_ok, 1)
            dve.tensor_copy(endi[:, :], ctile[:, :]).then_inc(tab_ok, 1)
            dve.wait_ge(w0_ok, 1)
            dve.tensor_tensor(wsplit[:, 0, 1, :], raw[:, :], wsplit[:, 0, 0, :].bitcast(F32), ALU.subtract).then_inc(w0l_ok, 1)

            def vstep(sl, i, first, last):
                vhid(sl, 0)
                if not first:
                    hT_low(sl - 1, 1)
                vhid(sl, 1)
                if not last:
                    xs_low(sl + 1, 1 - i)
                if not first:
                    y_copy(sl - 1, 1 - i)
                if not last:
                    aux_copy(sl + 1, 1 - i)
                hT_low(sl, 0)

            def vhid(sl, half):
                dve.wait_ge(sa_ok, 2 * sl + half + 1)
                at_least(dve, hT_mm, 2 * sl + half - 1)
                dve.tensor_tensor(hid[half][:, :], g_bank[half][:, :], sa[half][:, :], ALU.mult).then_inc(hid_ok, 1)

            def hT_low(sl, half):
                dve.wait_ge(hT_ev, 2 * sl + half + 1)
                dve.tensor_tensor(hidT[half][1][:, :, :], hT_bank[half][:, :].rearrange("p (f b) -> p f b", f=4),
                                  hidT[half][0][:, :, :].bitcast(F32), ALU.subtract).then_inc(hTl_ok, 1)

            def xs_low(sl, i):
                dve.wait_ge(xsT_ev, sl + 1)
                dve.tensor_tensor(xsT[i][1][:, :, :], xs_bank[:, 0:2 * P].rearrange("p (k b) -> p k b", k=2),
                                  xsT[i][0][:, :, :].bitcast(F32), ALU.subtract).then_inc(xsTl_ok, 1)

            def y_copy(sl, i):
                dve.wait_ge(y_mm, sl + 2)
                dve.wait_ge(aux_ok, sl + 1)
                at_least(dve, d_ys[i], (sl - i) * 8)
                dve.tensor_scalar(ys[i][:, 0:D], y_bank[:, 0:D], aux[i][:, 0:1], None, ALU.mult).then_inc(y_ok, 1)
                dve.tensor_scalar(ys[i][:, D:D + 1].bitcast(I32), aux[i][:, 1:2], -1.0, float(B * L),
                                  ALU.mult, ALU.add).then_inc(y_ok, 1)

            def aux_copy(sl, i):
                at_least(dve, y_ok, 2 * (sl - 1))
                dve.wait_ge(xsT_mm, sl + 1)
                dve.tensor_copy(aux[i][:, :], xs[i][:, D:DX]).then_inc(aux_ok, 1)

            xs_low(0, 0)
            aux_copy(0, 0)
            tiles_of_experts(dve, vstep)
            hT_low(NS - 1, 1)
            y_copy(NS - 1, (NS - 1) % 2)

        @block.gpsimd
        def _(pool):
            pool.memset(halfneg[:, :], -0.5).then_inc(c_ok, 1)
            pool.memset(xm[:, 0:2, :], 0.0).then_inc(z_ok, 1)
            pool.memset(zero[:, :], 0.0).then_inc(c_ok, 1)
            pool.wait_ge(c_ok, 2)

            def norm_scale(g, s):
                alone(pool, (mv_ok, g + 1), (xn_ok, g - 1))
                pool.tensor_scalar(vare[s][:, :], mv[s][:, 1:2], EPS, None, ALU.add).then_inc(var_ok, 1)
                pool.wait_ge(var_ok, g + 1)
                pool.tensor_tensor(rstd[s][:, :], vare[s][:, :], halfneg[:, :], ALU.pow).then_inc(rstd_ok, 1)

            def ctx_low(b, s, u, bs):
                pool.wait_ge(ch_ok, b + 1)
                pool.tensor_tensor(cx_s[bs][1][:, :, 0:M], cx[s][:, u, :, :], cx_s[bs][0][:, :, 0:M].bitcast(F32),
                                   ALU.subtract).then_inc(cl_ok, 1)

            def block_queries(b, g, s, u, bs):
                if u == 0:
                    pool.wait_ge(ql_ok, g + 1)
                at_least(pool, s_mm, 4 * (b - 1))
                for x in range(2):
                    for half in range(2):
                        ins = pool.tensor_tensor(
                            qbd[bs][x][:, half, :].rearrange("p (j l) -> p j l", j=4),
                            spread(qT[s][x][:, half, u * L:u * L + L].bitcast(F32), 1, 4),
                            spread(headmask[:, :], 2, L), ALU.mult)
                ins.then_inc(qbd_ok, 1)

            def last_key(b, g, s, u, bs):
                pool.wait_ge(p_ex, 4 * b + 4)
                if u == 0:
                    pool.wait_ge(d_vb[s], ((g - s) * 8 + 16) * 4)
                at_least(pool, o_ev, b - 1)
                pool.tensor_tensor(olast[bs][:, :, :], vb[s][:, u, :].rearrange("p (g d) -> p g d", g=4),
                                   prob[bs][:, :, KEYS:M].to_broadcast([P, 4, DH]), ALU.mult).then_inc(ol_ok, 1)

            def normalise(b, g, s, u, bs):
                pool.wait_ge(o_ev, b + 1)
                if u == 0:
                    at_least(pool, oT_mm, g - 1)
                pool.tensor_tensor(on[s][:, u, :].rearrange("p (g d) -> p g d", g=4), oraw[bs][:, :, :],
                                   spread(rinv[bs][:, :], 2, DH), ALU.mult).then_inc(on_ok, 1)

            def add_bias(g, s):
                pool.wait_ge(xsum_ok, g + 1)
                at_least(pool, d_x1[s], (g - s) * 8)
                pool.tensor_tensor(x1o[s][:, :], xsum[s][:, :], bo[:, :], ALU.add).then_inc(x1o_ok, 1)

            norm_scale(0, 0)
            pool.wait_ge(d_const, CONST)
            for i in range(2):
                for x in range(2):
                    pool.tensor_tensor(cx_s[i][x][:, :, M:MP], spread(zero[0:CK, :], 1, 2), spread(zero[0:CK, :], 1, 2),
                                       ALU.add).then_inc(pad_ok, 1)
            norm_scale(1, 1)
            ctx_low(0, 0, 0, 0)
            ctx_low(1, 0, 1, 1)
            block_queries(0, 0, 0, 0, 0)

            pool.memset(ebase[:, :], float(np.e)).then_inc(eb_ok, 1)
            pool.wait_ge(d_vec, 16 * len(vectors))
            pool.wait_ge(eb_ok, 1)
            pool.tensor_scalar(braw[:, :], braw[:, :], -1.0, None, ALU.mult).then_inc(ez_ok, 1)
            pool.wait_ge(ez_ok, 1)
            pool.tensor_tensor(beta[:, :], ebase[:, :], braw[:, :], ALU.pow).then_inc(ez_ok, 1)
            pool.wait_ge(ez_ok, 2)
            pool.tensor_scalar(beta[:, :], beta[:, :], 1.0, None, ALU.add).then_inc(be_ok, 1)
            for i in range(2):
                pool.tensor_scalar(gam1[i][:, :], gam[i][:, :], 1.0, None, ALU.add).then_inc(be_ok, 1)
            pool.tensor_scalar(nthr[:, :], thr[:, :], -1.0, None, ALU.mult).then_inc(be_ok, 1)

            def slot(g, s, first, last):
                final = last or (isinstance(g, int) and g + 2 >= NG)
                for u in range(GB):
                    b = g * GB + u
                    bs, bs1 = u % 2, (u + 1) % 2
                    if not (last and u >= 2):
                        ctx_low(b + 2, s if u < 2 else 1 - s, (u + 2) % GB, bs)
                    if not (first and u == 0):
                        if u == 0:
                            normalise(b - 1, g - 1, 1 - s, GB - 1, bs1)
                        else:
                            normalise(b - 1, g, s, u - 1, bs1)
                    if u < 3:
                        block_queries(b + 1, g, s, u + 1, bs1)
                    elif not last:
                        block_queries(b + 1, g + 1, 1 - s, 0, bs1)
                    last_key(b, g, s, u, bs)
                    if u == 1 and not final:
                        norm_scale(g + 2, s)
                    if u == 3 and not first:
                        add_bias(g - 1, 1 - s)

            slot(0, 0, True, False)
            with pool.Fori(0, NG // 2 - 2) as k:
                slot(k * 2 + 1, 1, False, False)
                slot(k * 2 + 2, 0, False, False)
            slot(NG - 3, 1, False, False)
            slot(NG - 2, 0, False, False)
            slot(NG - 1, 1, False, True)
            normalise(B - 1, NG - 1, 1, GB - 1, 1)
            add_bias(NG - 1, 1)

            for i in range(2):
                pool.wait_ge(d_x1[i], 16 * NG // 2)
            pool.memset(hT[1][:, :, :], 0.0).then_inc(h0_ok, 1)
            pool.wait_ge(h0_ok, 1)

            def std_inverse(c, Q, mv_ok_, ve_ok, rs_ok, used):
                alone(pool, (mv_ok_, Q * 2 + 2), (used, Q * 2))
                pool.tensor_scalar(small["ve" + c][:, :], mv2[c][:, :, 1], EPS, None, ALU.add).then_inc(ve_ok, 1)
                pool.wait_ge(ve_ok, Q + 1)
                pool.tensor_tensor(small["rs" + c][:, :], small["ve" + c][:, :], halfneg[:, :].to_broadcast([P, 2]),
                                   ALU.pow).then_inc(rs_ok, 1)

            def rms_scale(c, Q, ss_ok, sm_ok, sp_ok, sc_ok, used):
                alone(pool, (ss_ok, Q * 2 + 2))
                pool.tensor_scalar(small["sm" + c][:, :], small["ss" + c][:, :], RMS_MIN ** 2, None,
                                   ALU.max).then_inc(sm_ok, 1)
                pool.wait_ge(sm_ok, Q + 1)
                pool.tensor_tensor(small["sp" + c][:, :], small["sm" + c][:, :], halfneg[:, :].to_broadcast([P, 2]),
                                   ALU.pow).then_inc(sp_ok, 1)
                alone(pool, (sp_ok, Q + 1), (used, Q * 2))
                pool.tensor_scalar(small["sc" + c][:, :], small["sp" + c][:, :], float(D) ** 0.5, None,
                                   ALU.mult).then_inc(sc_ok, 1)

            def state(Q, i):
                t = Q * 2 + i
                alone(pool, (spk_ok, t + 1), (h_ok, t))
                pool.tensor_scalar(zed[:, :, :], spk[i][:, 0:3, :], 0.5, 0.5, ALU.mult, ALU.add)
                pool.tensor_scalar(wed[:, :, :], spk[i][:, 0:3, :], -0.5, 0.5, ALU.mult, ALU.add).then_inc(zw_ok, 1)
                pool.wait_ge(zw_ok, t + 1)
                pool.tensor_tensor(zed[:, :, :], zed[:, :, :], spk[i][:, 3:6, :], ALU.mult)
                pool.tensor_tensor(wed[:, :, :], wed[:, :, :], hT[1 - i][:, :, :], ALU.mult).then_inc(zc_ok, 1)
                pool.wait_ge(zc_ok, t + 1)
                at_least(pool, gru_mm, Q)
                pool.tensor_tensor(hT[i][:, :, :], wed[:, :, :], zed[:, :, :], ALU.add).then_inc(h_ok, 1)

            def turn(q, par, parts):
                f, o, n, m, r = (c in parts for c in "fonmr")
                if r:
                    std_inverse("B", q - 1, mvB_ok, veB_ok, rsB_ok, xm_ok)
                if m:
                    std_inverse("A", q + 3, mvA_ok, veA_ok, rsA_ok, xl_ok)
                if o:
                    rms_scale("B", q + 1, ssB_ok, smB_ok, spB_ok, scB_ok, fn_ok)
                    pool.wait_ge(xa_ok, q + 2)
                    pool.tensor_tensor(xall[:, bass.ds(q * 2 + 2, 2), :], xall[:, bass.ds(q * 2 + 2, 2), :], xa[:, :, :],
                                       ALU.add).then_inc(add_ok, 1)
                if r:
                    pool.wait_ge(xm_ok, q * 2)
                    pool.tensor_copy(xm[:, bass.ds(q * 2 - 2, 2), 0:D], xmt[:, :, :]).then_inc(xm_kept, 1)
                if n:
                    state(q + 2, 0)
                if m:
                    rms_scale("A", q + 3, ssA_ok, smA_ok, spA_ok, scA_ok, xr_ok)
                if n:
                    state(q + 2, 1)
            turns(pool, turn)

            pool.memset(ones[:, :], 1.0).then_inc(route_ok, 1)

            def load_w(e, c):
                pool.dma_start(raw[:, PIECES[c]], T["we"][e, :, PIECES[c]]).then_inc(d_we[c], 16)

            for t in range(NT):
                if t == 0:
                    pool.wait_ge(pos_ok, 1)
                pool.indirect_dma_start(xs_scr, bass.IndirectOffsetOnAxis(pos[:, t:t + 1].bitcast(U32), 0),
                                        xm[:, t, :], None).then_inc(d_sort, 16)
            pool.wait_ge(w0l_ok, 1)
            pool.sem_inc(w_ready, 1)
            pool.wait_ge(d_w, 32 * WP)
            pool.wait_ge(tab_ok, 2)
            for e in range(1, NE):
                if e > 1:
                    last_slot = pool.value_load(endi[0:1, e - 2:e - 1], min_val=0, max_val=NS)
                    pool.wait_ge(y_mm, last_slot + 1)
                for c in range(WP):
                    n = (e - 1) * WP + c
                    if e > 1:
                        pool.wait_ge(d_we[c], 16 * (e - 1))
                    high, low = (wsplit[:, e % 2, h, PIECES[c]] for h in range(2))
                    pool.tensor_tensor(high, raw[:, PIECES[c]], zero[:, :].to_broadcast([P, WE // WP]),
                                       ALU.add).then_inc(whi_ok, 1)
                    pool.wait_ge(whi_ok, n + 1)
                    pool.tensor_tensor(low, raw[:, PIECES[c]], high.bitcast(F32), ALU.subtract).then_inc(wlo_ok, 1)
                    pool.wait_ge(wlo_ok, n + 1)
                    if e + 1 < NE:
                        load_w(e + 1, c)
                pool.sem_inc(w_ready, 1)
            pool.wait_ge(d_out, 16 * NQ)

            def load_ys(sl):
                pool.wait_ge(d_ys[sl % 2], 16 * (sl // 2 + 1))
                at_least(pool, d_add[sl % 4], 16 * (sl // 4))
                pool.dma_start(yr[sl % 4][:, :], ys_scr[sl * P:(sl + 1) * P, :]).then_inc(d_yr[sl % 4], 16)

            for sl in range(2):
                load_ys(sl)
            for sl in range(NS):
                if sl + 2 < NS:
                    load_ys(sl + 2)
                pool.wait_ge(d_yr[sl % 4], 16 * (sl // 4 + 1))
                pool.indirect_dma_start(out, bass.IndirectOffsetOnAxis(yr[sl % 4][:, D:D + 1].bitcast(U32), 0),
                                        yr[sl % 4][:, 0:D], None, bounds_check=B * L - 1, oob_is_err=False,
                                        compute_op=ALU.add).then_inc(d_add[sl % 4], 16)
            for i in range(4):
                pool.wait_ge(d_add[i], 16 * ((NS + 3 - i) // 4))


def lay_out(i):
    f = lambda a: np.ascontiguousarray(a)
    wkv = i["L0_xattn_Wkv"].reshape(NH, 2, DH, C)
    bkv = i["L0_xattn_bkv"].reshape(NH, 2, DH)
    ctxT = i["ctx_768"].transpose(2, 0, 1).reshape(2, CK, B, M)
    wv = wkv[:, 1].transpose(2, 0, 1)
    bv = bkv[:, 1]

    def rows(w):
        return f(w.reshape(2, w.shape[0] // 2, w.shape[1]).transpose(1, 0, 2))

    def by_head(a):
        return a.reshape(*a.shape[:-2], 4, 4, DH).swapaxes(-3, -2)

    T = {
        "x": f(i["x"].reshape(B * L, D)),
        "cx": f(ctxT.transpose(1, 2, 0, 3)),
        "cxl": f(ctxT[:, :, :, KEYS].transpose(1, 0, 2)),
        "wk": rows(wkv[:, 0].transpose(2, 0, 1).reshape(C, D)),
        "wv": rows(wv.reshape(C, D)),
        "wvl": rows(by_head(wv).reshape(C, D)),
        "wq": rows(i["L0_xattn_Wq"].T),
        "wo": f(i["L0_xattn_Wo"].T.reshape(4, 2, 2, DH, D).transpose(1, 0, 3, 2, 4).reshape(P, 2, D)),
        "bk": f(bkv[:, 0].reshape(2, P).T),
        "bq": f(i["L0_xattn_bq"].reshape(2, P).T),
        "bv": f(bv.reshape(D)),
        "bvl": f(by_head(bv).reshape(D)),
        "bo": f(i["L0_xattn_bo"]),
        "ident": np.eye(P, dtype=np.float32),
        "headmask": (DH ** -0.5 * (np.arange(P)[:, None] // DH % 4 == np.arange(4)[None, :])).astype(np.float32),
    }

    def block_diagonal(w):
        h, o, n = w.shape
        m = np.zeros((h, n, h, o), w.dtype)
        m[np.arange(h), :, np.arange(h), :] = w.transpose(0, 2, 1)
        return m.reshape(h * n, h * o)

    def drive(w):
        m = block_diagonal(w).reshape(2, P, 3, P)
        return f(np.stack([m[0, :, 0], m[0, :, 1], m[1, :, 1], m[1, :, 2]], 1))

    def columns(a):
        return f(a.reshape(-1, P).T)

    fd = np.zeros((NF * P, D), np.float32)
    fd[:FI] = i["L0_attn_ffd_W"].T
    T |= {
        "gw": drive(i["L0_attn_gate_W"]),
        "cw": drive(i["L0_attn_cand_W"]),
        "ow": f(block_diagonal(i["L0_attn_out_W"]).reshape(3, P, D).transpose(1, 0, 2)),
        "braw": f(np.concatenate([columns(i["L0_attn_gate_beta_raw"]), columns(i["L0_attn_cand_beta_raw"])], 1)),
        "thr": f(np.concatenate([columns(i["L0_attn_gate_theta"]), columns(i["L0_attn_cand_theta"])], 1)),
        "gamA": columns(i["L0_attn_in_gamma"]),
        "gamB": columns(i["L0_attn_ff_gamma"]),
        "fg": rows(i["L0_attn_ffg_W"].T),
        "fu": rows(i["L0_attn_ffu_W"].T),
        "fd": f(fd.reshape(NF, P, D).transpose(1, 0, 2)),
        "rw": rows(i["L0_ffn_router_w"]),
        "rb": f(i["L0_ffn_router_b"]),
        "we": f(np.concatenate([
            i["L0_ffn_w1"].reshape(NE, 2, P, 2 * FF).transpose(0, 2, 1, 3).reshape(NE, P, 4 * FF),
            i["L0_ffn_w2"].reshape(NE, FT, P, D).transpose(0, 2, 1, 3).reshape(NE, P, FT * D)], 2)),
        "lt": np.triu(np.ones((P, P), np.float32), 1),
        "token": (B * L - np.arange(B * L)).astype(np.float32).reshape(B, L),
        "descend": np.arange(NE, 0, -1).astype(np.float32),
        "slotno": np.arange(NS).astype(np.float32),
    }
    return T


def kernel(**inputs):
    import concourse.bacc as bacc
    from concourse.bass_utils import run_bass_kernel_spmd

    arrays = lay_out({name: np.asarray(a) for name, a in inputs.items()})
    nc = bacc.Bacc("TRN2", target_bir_lowering=False, num_devices=1)
    T = {name: nc.dram_tensor(name, a.shape, mybir.dt.from_np(a.dtype), kind="ExternalInput").ap()
         for name, a in arrays.items()}
    out = nc.dram_tensor("out", (B * L, D), F32, kind="ExternalOutput").ap()
    build(nc, T, out)
    results = run_bass_kernel_spmd(nc, [arrays], core_ids=[0])
    return results.results[0]["out"].reshape(B, L, D)
```
